# Optimizing a Trainium2 kernel written in Bass

```python
import numpy as np
import jax
import jax.numpy as jnp

def _softmax(x, axis=-1):
    return jax.nn.softmax(x, axis=axis)

def _gelu(x):
    return jax.nn.gelu(x, approximate=True)

def _silu(x):
    return jax.nn.silu(x)

def _sigmoid(x):
    return jax.nn.sigmoid(x)

def _layernorm(x, axis=-1, eps=1e-05):
    m = jnp.mean(x, axis=axis, keepdims=True)
    v = jnp.var(x, axis=axis, keepdims=True)
    return (x - m) / jnp.sqrt(v + eps)

def _scatter_add(tgt, idx, src, axis=0):
    return tgt.at[idx].add(src)

def _segment_sum(src, seg, n):
    return jax.ops.segment_sum(src, seg, n)
kernel_name = 'mk_early_fusion_d1_tok_img1024_r4_339a4b'

def setup_inputs(seed: int=0):
    np.random.seed(seed)
    _w = jnp.asarray

    def _rec_inputs():
        import jax
        import jax.numpy as jnp
        _rk = jax.random.key(seed)
        x = -0.00016672 + 0.999947 * jax.random.normal(jax.random.fold_in(_rk, 1), (64, 3, 96, 96), jnp.float32)
        txt = 0.00140885 + 1.4139 * jax.random.normal(jax.random.fold_in(_rk, 2), (64, 32, 256), jnp.float32)
        return (x, txt)
    x, txt = _rec_inputs()

    def _L0_tok_setup():
        import jax, jax.numpy as jnp
        import numpy as np
        B, C, H, W = (64, 3, 96, 96)
        P = 16
        NP = H // P * (W // P)
        PD = C * P * P
        ED = 256
        NCLS = 1

        def _layernorm(x, g, b, eps=1e-05):
            mu = jnp.mean(x, axis=-1, keepdims=True)
            var = jnp.mean(jnp.square(x - mu), axis=-1, keepdims=True)
            return (x - mu) * jax.lax.rsqrt(var + eps) * g + b
        key = jax.random.key(seed)
        ks = jax.random.split(key, 8)
        x = jax.random.normal(ks[0], (B, C, H, W), dtype=jnp.float32)
        ln1_g = jnp.ones((PD,), jnp.float32)
        ln1_b = jnp.zeros((PD,), jnp.float32)
        W_proj = jax.random.normal(ks[1], (PD, ED), jnp.float32) / np.sqrt(PD)
        b_proj = jnp.zeros((ED,), jnp.float32)
        ln2_g = jnp.ones((ED,), jnp.float32)
        ln2_b = jnp.zeros((ED,), jnp.float32)
        cls_token = jax.random.normal(ks[2], (1, NCLS, ED), jnp.float32)
        pos_emb = jax.random.normal(ks[3], (1, NP + NCLS, ED), jnp.float32)
        return {'x': x, 'ln1_g': ln1_g, 'ln1_b': ln1_b, 'W_proj': W_proj, 'b_proj': b_proj, 'ln2_g': ln2_g, 'ln2_b': ln2_b, 'cls_token': cls_token, 'pos_emb': pos_emb}
    _L0_tok_all = _L0_tok_setup()
    _L0_tok_in = {k: v for k, v in _L0_tok_all.items() if k in ('ln1_g', 'ln1_b', 'W_proj', 'b_proj', 'ln2_g', 'ln2_b', 'cls_token', 'pos_emb')}
    del _L0_tok_all

    def _L0_attn_setup():
        import jax, jax.numpy as jnp
        import numpy as np
        HIDDEN = 256
        N_HEAD = 16
        HEAD_DIM = HIDDEN // N_HEAD
        BATCH = 1
        SEQ = 1024
        THETA = 10000.0

        def _rope_cos_sin(seq_len, head_dim, dtype=jnp.float32):
            inv_freq = 1.0 / THETA ** (jnp.arange(0, head_dim, 2, dtype=dtype) / head_dim)
            t = jnp.arange(seq_len, dtype=dtype)
            freqs = jnp.outer(t, inv_freq)
            return (jnp.cos(freqs), jnp.sin(freqs))

        def _apply_rope(x, cos, sin):
            x2 = x.reshape(*x.shape[:-1], -1, 2)
            x_re, x_im = (x2[..., 0], x2[..., 1])
            c = cos[None, :, None, :]
            s = sin[None, :, None, :]
            out_re = x_re * c - x_im * s
            out_im = x_re * s + x_im * c
            out = jnp.stack([out_re, out_im], axis=-1)
            return out.reshape(x.shape)
        key = jax.random.key(seed)
        kx, kq, kk, kv = jax.random.split(key, 4)
        scale = 1.0 / np.sqrt(HIDDEN)
        return {'x': jax.random.normal(kx, (BATCH, SEQ, HIDDEN), dtype=jnp.float32), 'wq': jax.random.normal(kq, (HIDDEN, HIDDEN), dtype=jnp.float32) * scale, 'wk': jax.random.normal(kk, (HIDDEN, HIDDEN), dtype=jnp.float32) * scale, 'wv': jax.random.normal(kv, (HIDDEN, HIDDEN), dtype=jnp.float32) * scale}
    _L0_attn_all = _L0_attn_setup()
    _L0_attn_in = {k: v for k, v in _L0_attn_all.items() if k in ('wq', 'wk', 'wv')}
    del _L0_attn_all

    def _L0_ffn_setup():
        import jax, jax.numpy as jnp
        import numpy as np
        NUM_EXPERTS = 8
        TOP_K = 2
        MOE_DIM = 512

        def _moe_forward(x, moe_router, moe_w13, moe_w2):
            b, s, d = x.shape
            x_flat = x.reshape(b * s, d)
            router_logits = jnp.einsum('td,de->te', x_flat, moe_router)
            topk_logits, topk_idx = jax.lax.top_k(router_logits, TOP_K)
            topk_weights = jax.nn.softmax(topk_logits, axis=-1).astype(x.dtype)
            tokens = x_flat.shape[0]
            expert_ids = topk_idx.reshape(tokens * TOP_K)
            dispatch_weights = topk_weights.reshape(tokens * TOP_K)
            sort_idx = jnp.argsort(expert_ids, axis=0)
            token_ids = jnp.arange(tokens * TOP_K, dtype=jnp.int32) // TOP_K
            token_ids_sort = token_ids[sort_idx]
            x_sort = x_flat[token_ids_sort]
            w_sort = dispatch_weights[sort_idx].astype(x_flat.dtype)
            group_sizes = jnp.bincount(expert_ids, length=NUM_EXPERTS).astype(jnp.int32)
            w13_out = jax.lax.ragged_dot(x_sort, moe_w13, group_sizes)
            gate, up = jnp.split(w13_out, [MOE_DIM], axis=-1)
            hidden = jax.nn.silu(gate) * up
            out_dispatch = jax.lax.ragged_dot(hidden, moe_w2, group_sizes)
            out_flat = jnp.zeros_like(x_flat).at[token_ids_sort].add(out_dispatch * w_sort[:, None], mode='drop')
            return out_flat.reshape(b, s, d)
        key = jax.random.key(seed)
        k1, k2, k3, k4 = jax.random.split(key, 4)
        B, S, D = (4, 512, 256)
        x = jax.random.normal(k1, (B, S, D), dtype=jnp.float32)
        moe_router = jax.random.normal(k2, (D, NUM_EXPERTS), dtype=jnp.float32) * 0.02
        moe_w13 = jax.random.normal(k3, (NUM_EXPERTS, D, 2 * MOE_DIM), dtype=jnp.float32) * 0.02
        moe_w2 = jax.random.normal(k4, (NUM_EXPERTS, MOE_DIM, D), dtype=jnp.float32) * 0.02
        return {'x': x, 'moe_router': moe_router, 'moe_w13': moe_w13, 'moe_w2': moe_w2}
    _L0_ffn_all = _L0_ffn_setup()
    _L0_ffn_in = {k: v for k, v in _L0_ffn_all.items() if k in ('moe_router', 'moe_w13', 'moe_w2')}
    del _L0_ffn_all
    return {'x': x, 'txt': txt, 'L0_tok_ln1_g': _L0_tok_in['ln1_g'], 'L0_tok_ln1_b': _L0_tok_in['ln1_b'], 'L0_tok_W_proj': _L0_tok_in['W_proj'], 'L0_tok_b_proj': _L0_tok_in['b_proj'], 'L0_tok_ln2_g': _L0_tok_in['ln2_g'], 'L0_tok_ln2_b': _L0_tok_in['ln2_b'], 'L0_tok_cls_token': _L0_tok_in['cls_token'], 'L0_tok_pos_emb': _L0_tok_in['pos_emb'], 'L0_attn_wq': _L0_attn_in['wq'], 'L0_attn_wk': _L0_attn_in['wk'], 'L0_attn_wv': _L0_attn_in['wv'], 'L0_ffn_moe_router': _L0_ffn_in['moe_router'], 'L0_ffn_moe_w13': _L0_ffn_in['moe_w13'], 'L0_ffn_moe_w2': _L0_ffn_in['moe_w2']}

def reference(x, txt, L0_tok_ln1_g, L0_tok_ln1_b, L0_tok_W_proj, L0_tok_b_proj, L0_tok_ln2_g, L0_tok_ln2_b, L0_tok_cls_token, L0_tok_pos_emb, L0_attn_wq, L0_attn_wk, L0_attn_wv, L0_ffn_moe_router, L0_ffn_moe_w13, L0_ffn_moe_w2):
    import jax
    import jax.numpy as jnp

    def _L0_tok_ref(x, ln1_g, ln1_b, W_proj, b_proj, ln2_g, ln2_b, cls_token, pos_emb):
        import jax, jax.numpy as jnp
        import numpy as np
        B, C, H, W = (64, 3, 96, 96)
        P = 16
        NP = H // P * (W // P)
        PD = C * P * P
        ED = 256
        NCLS = 1

        def _layernorm(x, g, b, eps=1e-05):
            mu = jnp.mean(x, axis=-1, keepdims=True)
            var = jnp.mean(jnp.square(x - mu), axis=-1, keepdims=True)
            return (x - mu) * jax.lax.rsqrt(var + eps) * g + b
        b = x.shape[0]
        h, w = (H // P, W // P)
        patches = x.reshape(b, C, h, P, w, P)
        patches = patches.transpose(0, 2, 4, 3, 5, 1).reshape(b, h * w, P * P * C)
        z = _layernorm(patches, ln1_g, ln1_b)
        z = jnp.einsum('bnp,pe->bne', z, W_proj) + b_proj
        z = _layernorm(z, ln2_g, ln2_b)
        cls = jnp.broadcast_to(cls_token, (b, NCLS, ED))
        z = jnp.concatenate([cls, z], axis=1)
        z = z + pos_emb
        return z

    def _L0_attn_ref(x, wq, wk, wv):
        import jax, jax.numpy as jnp
        import numpy as np
        HIDDEN = 256
        N_HEAD = 16
        HEAD_DIM = HIDDEN // N_HEAD
        BATCH = 1
        SEQ = 1024
        THETA = 10000.0

        def _rope_cos_sin(seq_len, head_dim, dtype=jnp.float32):
            inv_freq = 1.0 / THETA ** (jnp.arange(0, head_dim, 2, dtype=dtype) / head_dim)
            t = jnp.arange(seq_len, dtype=dtype)
            freqs = jnp.outer(t, inv_freq)
            return (jnp.cos(freqs), jnp.sin(freqs))

        def _apply_rope(x, cos, sin):
            x2 = x.reshape(*x.shape[:-1], -1, 2)
            x_re, x_im = (x2[..., 0], x2[..., 1])
            c = cos[None, :, None, :]
            s = sin[None, :, None, :]
            out_re = x_re * c - x_im * s
            out_im = x_re * s + x_im * c
            out = jnp.stack([out_re, out_im], axis=-1)
            return out.reshape(x.shape)
        B, S, _ = x.shape
        xq = (x @ wq.T).reshape(B, S, N_HEAD, HEAD_DIM).astype(jnp.float32)
        xk = (x @ wk.T).reshape(B, S, N_HEAD, HEAD_DIM).astype(jnp.float32)
        xv = (x @ wv.T).reshape(B, S, N_HEAD, HEAD_DIM).astype(jnp.float32)
        cos, sin = _rope_cos_sin(S, HEAD_DIM)
        q = _apply_rope(xq, cos, sin)
        k = _apply_rope(xk, cos, sin)
        scores = jnp.einsum('bqhd,bkhd->bhqk', q, k) / jnp.sqrt(jnp.asarray(HEAD_DIM, dtype=q.dtype))
        attn = jax.nn.softmax(scores, axis=-1)
        out = jnp.einsum('bhqk,bkhd->bqhd', attn, xv)
        return out.reshape(B, S, N_HEAD * HEAD_DIM)

    def _L0_ffn_ref(x, moe_router, moe_w13, moe_w2):
        import jax, jax.numpy as jnp
        import numpy as np
        NUM_EXPERTS = 8
        TOP_K = 2
        MOE_DIM = 512

        def _moe_forward(x, moe_router, moe_w13, moe_w2):
            b, s, d = x.shape
            x_flat = x.reshape(b * s, d)
            router_logits = jnp.einsum('td,de->te', x_flat, moe_router)
            topk_logits, topk_idx = jax.lax.top_k(router_logits, TOP_K)
            topk_weights = jax.nn.softmax(topk_logits, axis=-1).astype(x.dtype)
            tokens = x_flat.shape[0]
            expert_ids = topk_idx.reshape(tokens * TOP_K)
            dispatch_weights = topk_weights.reshape(tokens * TOP_K)
            sort_idx = jnp.argsort(expert_ids, axis=0)
            token_ids = jnp.arange(tokens * TOP_K, dtype=jnp.int32) // TOP_K
            token_ids_sort = token_ids[sort_idx]
            x_sort = x_flat[token_ids_sort]
            w_sort = dispatch_weights[sort_idx].astype(x_flat.dtype)
            group_sizes = jnp.bincount(expert_ids, length=NUM_EXPERTS).astype(jnp.int32)
            w13_out = jax.lax.ragged_dot(x_sort, moe_w13, group_sizes)
            gate, up = jnp.split(w13_out, [MOE_DIM], axis=-1)
            hidden = jax.nn.silu(gate) * up
            out_dispatch = jax.lax.ragged_dot(hidden, moe_w2, group_sizes)
            out_flat = jnp.zeros_like(x_flat).at[token_ids_sort].add(out_dispatch * w_sort[:, None], mode='drop')
            return out_flat.reshape(b, s, d)
        return _moe_forward(x, moe_router, moe_w13, moe_w2)
    h = _L0_tok_ref(x, L0_tok_ln1_g, L0_tok_ln1_b, L0_tok_W_proj, L0_tok_b_proj, L0_tok_ln2_g, L0_tok_ln2_b, L0_tok_cls_token, L0_tok_pos_emb)
    h = jnp.concatenate([h, txt], axis=1)
    h = h + _L0_attn_ref(_layernorm(h, axis=-1), L0_attn_wq, L0_attn_wk, L0_attn_wv)
    h = h + _L0_ffn_ref(_layernorm(h, axis=-1), L0_ffn_moe_router, L0_ffn_moe_w13, L0_ffn_moe_w2)
    return h

_drawn_inputs = setup_inputs


def setup_inputs(seed=0):
    import zlib

    import numpy as np

    out = dict(_drawn_inputs(seed))
    spreads = {'L0_tok_ln1_g': (1.0, 0.2),
     'L0_tok_ln1_b': (0.0, 0.1),
     'L0_tok_b_proj': (0.0, 0.1),
     'L0_tok_ln2_g': (1.0, 0.2),
     'L0_tok_ln2_b': (0.0, 0.1)}
    factors = {'L0_ffn_moe_router': 5.618, 'L0_ffn_moe_w13': 4.814, 'L0_ffn_moe_w2': 4.801}
    for name, (base, spread) in spreads.items():
        noise = np.random.default_rng([zlib.crc32(name.encode()), seed]).standard_normal(out[name].shape)
        drawn = base * np.exp(spread * noise) if base else spread * noise
        out[name] = jnp.asarray(drawn.astype(out[name].dtype))
    for name, factor in factors.items():
        out[name] = (out[name] * factor).astype(out[name].dtype)
    return out
```

```python
from contextlib import ExitStack

import numpy as np
import concourse.bass as bass
from concourse import mybir

BATCH, CHANNELS, IMAGE, PATCH = 64, 3, 96, 16
GRID = IMAGE // PATCH
PATCHES = GRID * GRID
DIM, TEXT = 256, 32
SEQ = 1 + PATCHES + TEXT
TOKENS = BATCH * SEQ
PATCH_DIM = CHANNELS * PATCH * PATCH
HEADS, HEAD_DIM = 16, 16
EXPERTS, HIDDEN, TOP_K = 8, 512, 2
EPS = 1e-5
P = 128
TILES_TOK = BATCH * PATCHES // P
KT = PATCH_DIM // P
KD = DIM // P
KH = HIDDEN // P
PAD = 32
CH = HEADS * PAD // P
TILES_MOE = (TOKENS * TOP_K + EXPERTS * (P - 1)) // P
SPARE = P
BANK = 512


def build(nc, patches, txt, ln1_g, ln1_b, w_proj, b_proj, ln2_g, ln2_b, cls_token, pos_emb,
          wqkv, router, w13, w2, ident, rope, prefix, out):
    fp32, i32 = mybir.dt.float32, mybir.dt.int32
    ALU, ACT, AX = mybir.AluOpType, mybir.ActivationFunctionType, mybir.AxisListType
    ctx = ExitStack()
    with ctx:
        def sb(name, shape, dt=fp32):
            return ctx.enter_context(nc.sbuf_tensor(name, shape, dt))

        def sem(name):
            return ctx.enter_context(nc.semaphore(name))

        patch_rows = nc.dram_tensor("patch_rows", (BATCH * PATCHES, DIM), fp32).ap()
        h_rows = nc.dram_tensor("h_rows", (TOKENS, DIM), fp32).ap()
        xn_rows = nc.dram_tensor("xn_rows", (TOKENS + SPARE, DIM), fp32).ap()

        bank = [ctx.enter_context(nc.psum_tensor(f"bank{i}", [P, BANK], fp32)) for i in range(4, 8)]
        quad = ctx.enter_context(nc.psum_tensor("quad", [P, 4, BANK], fp32))
        b4, b5, b6, b7 = bank

        idt = sb("idt", [P, P])
        eps_pow = sb("eps_pow", [P, 1])
        wqkv_sb = sb("wqkv_sb", [P, KD, 3 * DIM])
        router_sb = sb("router_sb", [P, KD, EXPERTS])
        rope_sb = sb("rope_sb", [SEQ, 2, 2 * DIM])
        prefix_sb = sb("prefix_sb", [SEQ, SEQ])
        ones = sb("ones", [P, P])
        w13_sb = sb("w13_sb", [P, EXPERTS * KD * 2 * HIDDEN])
        w2_sb = sb("w2_sb", [P, EXPERTS * KH * DIM])
        scale_rows = sb("scale_rows", [SEQ, DIM])
        shift_rows = sb("shift_rows", [SEQ, DIM])
        shift_add = sb("shift_add", [SEQ, DIM])
        logits = sb("logits", [SEQ, BATCH, EXPERTS])
        expert_of = sb("expert_of", [P, TILES_MOE], i32)
        token_of = sb("token_of", [P, TILES_MOE], i32)
        weight_of = sb("weight_of", [P, TILES_MOE])

        held = {e: sem("held_" + e) for e in ("dve", "pool", "pe", "sp")}

        def tokenizer():
            with ExitStack() as st:
                def tb(name, shape, dt=fp32):
                    return st.enter_context(nc.sbuf_tensor(name, shape, dt))

                wp = tb("wp", [P, KT, DIM])
                wg = tb("wg", [P, KT, DIM])
                g1 = tb("g1", [P, KT])
                b1 = tb("b1", [P, KT])
                b1_wide = tb("b1_wide", [P, KT, P])
                bp = tb("bp", [P, DIM])
                bias = tb("bias", [P, DIM])
                xt = [tb(f"xt{i}", [P, PATCH_DIM]) for i in range(2)]
                xc = [tb(f"xc{i}", [P, PATCH_DIM]) for i in range(2)]
                xcT = [tb(f"xcT{i}", [P, PATCH_DIM]) for i in range(2)]
                st1 = tb("st1", [P, 2, 6])
                mv1 = [tb(f"tmv1{i}", [P, 2]) for i in range(2)]
                ve1 = tb("tve1", [P, 1])
                rs1 = [tb(f"trs1{i}", [P, 1]) for i in range(2)]
                z = [tb(f"z{i}", [P, DIM]) for i in range(2)]
                st2 = tb("tst2", [P, 6])
                mv2 = [tb(f"tmv2{i}", [P, 2]) for i in range(2)]
                ve2 = tb("tve2", [P, 1])
                rs2 = [tb(f"trs2{i}", [P, 1]) for i in range(2)]
                zn = [tb(f"zn{i}", [P, DIM]) for i in range(2)]

                names = """t_const t_small t_wg t_wide t_bias_mm t_bias x_turned xT_ready z_mm stats1 mv1_ready eps1 rstd1
                    xc_ready z_ready stats2 mv2_ready eps2 rstd2 zn_ready t_ones t_pow
                    sc_init sc_load sh_done zero_spare""".split()
                s = {n: sem("a_" + n) for n in names}
                x_loaded = [sem(f"a_x_loaded{i}") for i in range(2)]
                z_stored = [sem(f"a_z_stored{i}") for i in range(2)]
                spare_stored, weights_in, table_in = sem("a_spare_stored"), sem("a_weights_in"), sem("a_table_in")

                N = TILES_TOK
                FIRST, LAST = 2, (N - 2) // 2

                def pairs(eng, step, lo, hi):
                    for t in range(lo, 2 * FIRST):
                        step(t // 2, t % 2)
                    with eng.Fori(FIRST, LAST) as i:
                        for par in range(2):
                            step(i, par)
                    for t in range(2 * LAST, hi):
                        step(t // 2, t % 2)

                def live(i, off):
                    return not isinstance(i, int) or 0 <= 2 * i + off < N

                def later(i, off, back=2):
                    return not isinstance(i, int) or 2 * i + off >= back

                with nc.Block() as block:
                    @block.sync
                    def _(sp):
                        sp.dma_start(idt[:, :], ident).then_inc(s["t_const"], 16)
                        sp.dma_start(wp[:, :, :], w_proj).then_inc(s["t_const"], 16)
                        sp.dma_start(g1[:, :], ln1_g).then_inc(s["t_const"], 16)
                        sp.dma_start(b1[:, :], ln1_b).then_inc(s["t_const"], 16)
                        sp.dma_start(bp[:, :], b_proj[None, :].broadcast_to([P, DIM])).then_inc(s["t_const"], 16)

                        def step(i, par):
                            if live(i, par):
                                n = 2 * i + par
                                if later(i, par):
                                    sp.wait_ge(s["xc_ready"], n - 1)
                                sp.sem_inc(held["sp"], 1)
                                sp.dma_start(xt[par][:, :], patches[bass.ds(n * P, P), :]).then_inc(x_loaded[par], 16)
                            off = par - 4
                            if live(i, off):
                                n = 2 * i + off
                                sp.wait_ge(s["zn_ready"], n + 1)
                                sp.sem_inc(held["sp"], 1)
                                sp.dma_start(patch_rows[bass.ds(n * P, P), :], zn[off % 2][:, :]).then_inc(z_stored[off % 2], 16)
                        pairs(sp, step, 0, N + 4)
                        sp.dma_start(wqkv_sb[:, :, :], wqkv).then_inc(weights_in, 16)
                        sp.dma_start(router_sb[:, :, :], router).then_inc(weights_in, 16)
                        sp.dma_start(rope_sb[:, :, :], rope).then_inc(weights_in, 16)
                        sp.dma_start(prefix_sb[:, :], prefix).then_inc(weights_in, 16)
                        for e in range(EXPERTS):
                            sp.dma_start(w13_sb[:, e * KD * 2 * HIDDEN:(e + 1) * KD * 2 * HIDDEN], w13[e]).then_inc(experts_in, 16)
                            sp.dma_start(w2_sb[:, e * KH * DIM:(e + 1) * KH * DIM], w2[e]).then_inc(experts_in, 16)
                        for par in range(2):
                            sp.wait_ge(z_stored[par], 16 * (N // 2))
                        sp.wait_ge(weights_in, 64)
                        sp.wait_ge(table_in, 16 * 5)
                        sp.wait_ge(spare_stored, 16)

                    @block.gpsimd
                    def _(pool):
                        nc.gpsimd.memset(eps_pow[:, :], -0.5).then_inc(s["t_pow"], 1)
                        nc.gpsimd.memset(ones[:, :], 1.0).then_inc(s["t_ones"], 1)
                        nc.gpsimd.memset(scale_rows[:, :], 1.0).then_inc(s["sc_init"], 1)
                        nc.gpsimd.memset(shift_rows[:, :], 0.0).then_inc(s["sc_init"], 1)
                        nc.gpsimd.memset(shift_add[:, :], 0.0).then_inc(s["sc_init"], 1)
                        pool.wait_ge(s["sc_init"], 3)
                        pool.dma_start(scale_rows[1:1 + PATCHES, :], ln2_g[None, :].broadcast_to([PATCHES, DIM])).then_inc(table_in, 16)
                        pool.dma_start(shift_rows[1:1 + PATCHES, :], ln2_b[None, :].broadcast_to([PATCHES, DIM])).then_inc(table_in, 16)
                        pool.dma_start(shift_rows[0:1, :], cls_token).then_inc(table_in, 16)
                        pool.dma_start(shift_add[0:1 + PATCHES, :], pos_emb).then_inc(table_in, 16)
                        pool.wait_ge(s["t_ones"], 1)
                        nc.gpsimd.memset(zero_tile[:, :], 0.0).then_inc(s["zero_spare"], 1)
                        pool.wait_ge(s["zero_spare"], 1)
                        pool.dma_start(xn_rows[TOKENS:TOKENS + SPARE, :], zero_tile[:, :]).then_inc(spare_stored, 16)
                        pool.dma_start(out[TOKENS:TOKENS + SPARE, :], zero_tile[:, :]).then_inc(table_in, 16)

                        def step(i, par):
                            if live(i, par + 2):
                                n, q = 2 * i + par + 2, par
                                pool.wait_ge(s["mv1_ready"], n + 1)
                                if later(i, par + 2):
                                    pool.wait_ge(s["xc_ready"], n - 1)
                                pool.sem_inc(held["pool"], 1)
                                nc.gpsimd.tensor_scalar(ve1[:, :], mv1[q][:, 1:2], EPS, None, ALU.add).then_inc(s["eps1"], 1)
                                pool.wait_ge(s["eps1"], n + 1)
                                nc.gpsimd.tensor_tensor(rs1[q][:, :], ve1[:, :], eps_pow[:, :], ALU.pow).then_inc(s["rstd1"], 1)
                            if live(i, par - 1):
                                n, q = 2 * i + par - 1, (par - 1) % 2
                                pool.wait_ge(s["mv2_ready"], n + 1)
                                pool.sem_inc(held["pool"], 1)
                                nc.gpsimd.tensor_scalar(ve2[:, :], mv2[q][:, 1:2], EPS, None, ALU.add).then_inc(s["eps2"], 1)
                                pool.wait_ge(s["eps2"], n + 1)
                                nc.gpsimd.tensor_tensor(rs2[q][:, :], ve2[:, :], eps_pow[:, :], ALU.pow).then_inc(s["rstd2"], 1)
                        pairs(pool, step, -2, N + 1)
                        pool.wait_ge(table_in, 16 * 5)
                        nc.gpsimd.tensor_tensor(shift_rows[:, :], shift_rows[:, :], shift_add[:, :], ALU.add).then_inc(s["sh_done"], 1)
                        pool.wait_ge(s["sh_done"], 1)

                    @block.vector
                    def _(dve):
                        dve.wait_ge(s["t_const"], 80)
                        dve.wait_ge(s["t_ones"], 1)
                        for k in range(KT):
                            nc.vector.tensor_scalar(wg[:, k, :], wp[:, k, :], g1[:, k:k + 1], None, ALU.mult).then_inc(s["t_wg"], 1)
                            nc.vector.tensor_scalar(b1_wide[:, k, :], ones[:, :], b1[:, k:k + 1], None, ALU.mult).then_inc(s["t_wide"], 1)
                        dve.wait_ge(s["t_bias_mm"], 1)
                        nc.vector.tensor_tensor(bias[:, :], b4[:, 0:DIM], bp[:, :], ALU.add).then_inc(s["t_bias"], 1)
                        dve.wait_ge(s["t_bias"], 1)

                        def step(i, par):
                            if live(i, par + 2):
                                n, q = 2 * i + par + 2, par
                                half = i + 1
                                dve.wait_ge(x_loaded[q], 16 * (half + 1))
                                for c in range(2):
                                    nc.vector.bn_stats(st1[:, c, :], xt[q][:, c * 384:(c + 1) * 384]).then_inc(s["stats1"], 1)
                                dve.wait_ge(s["stats1"], 2 * n + 2)
                                dve.sem_inc(held["dve"], 1)
                                nc.vector.bn_aggr(mv1[q][:, :], st1[:, :, :].rearrange("p a b -> p (a b)")).then_inc(s["mv1_ready"], 1)
                            if live(i, par - 1):
                                n, q = 2 * i + par - 1, (par - 1) % 2
                                dve.wait_ge(s["z_mm"], n + 1)
                                nc.vector.tensor_tensor(z[q][:, :], bank[q][:, 0:DIM], bias[:, :], ALU.add).then_inc(s["z_ready"], 1)
                                dve.wait_ge(s["z_ready"], n + 1)
                                nc.vector.bn_stats(st2[:, :], z[q][:, :]).then_inc(s["stats2"], 1)
                                dve.wait_ge(s["stats2"], n + 1)
                                dve.sem_inc(held["dve"], 1)
                                nc.vector.bn_aggr(mv2[q][:, :], st2[:, :]).then_inc(s["mv2_ready"], 1)
                            if live(i, par + 2):
                                n, q = 2 * i + par + 2, par
                                dve.wait_ge(s["rstd1"], n + 1)
                                if later(i, par + 2):
                                    dve.wait_ge(s["x_turned"], n - 1)
                                dve.wait_ge(s["mv1_ready"], n + 1)
                                nc.vector.tensor_scalar(xc[q][:, :], xt[q][:, :], mv1[q][:, 0:1], rs1[q][:, :],
                                                        ALU.subtract, ALU.mult).then_inc(s["xc_ready"], 1)
                            if live(i, par - 1):
                                n, q = 2 * i + par - 1, (par - 1) % 2
                                half = i + (par - 1) // 2
                                dve.wait_ge(s["rstd2"], n + 1)
                                dve.wait_ge(s["mv2_ready"], n + 1)
                                if later(i, par - 1):
                                    dve.wait_ge(z_stored[q], 16 * half)
                                nc.vector.tensor_scalar(zn[q][:, :], z[q][:, :], mv2[q][:, 0:1], rs2[q][:, :],
                                                        ALU.subtract, ALU.mult).then_inc(s["zn_ready"], 1)
                        pairs(dve, step, -2, N + 1)

                    @block.scalar
                    def _(act):
                        def step(i, par):
                            if live(i, par + 1):
                                n, q = 2 * i + par + 1, (par + 1) % 2
                                act.wait_ge(s["x_turned"], n + 1)
                                if later(i, par + 1):
                                    act.wait_ge(s["z_mm"], n - 1)
                                nc.scalar.activation(xcT[q][:, :].rearrange("p (a b) -> p a b", a=2),
                                                     quad[:, 2 * q:2 * q + 2, 0:384], ACT.Copy).then_inc(s["xT_ready"], 1)
                        pairs(act, step, -1, N)

                    @block.tensor
                    def _(pe):
                        pe.wait_ge(s["t_wide"], KT)
                        pe.wait_ge(s["t_const"], 80)
                        for k in range(KT):
                            last = nc.tensor.matmul(b4[:, 0:DIM], b1_wide[:, k, :], wp[:, k, :], start=(k == 0), stop=(k == KT - 1))
                        last.then_inc(s["t_bias_mm"], 1)
                        pe.wait_ge(s["t_wg"], KT)
                        pe.wait_ge(s["t_bias"], 1)

                        def step(i, par):
                            if live(i, par + 1):
                                n, q = 2 * i + par + 1, (par + 1) % 2
                                pe.wait_ge(s["xc_ready"], n + 1)
                                if later(i, par + 1):
                                    pe.wait_ge(s["xT_ready"], n - 1)
                                for k in range(KT):
                                    last = nc.tensor.transpose(quad[:, 2 * q + k // 3, (k % 3) * P:(k % 3 + 1) * P],
                                                               xc[q][:, k * P:(k + 1) * P], idt[:, :])
                                last.then_inc(s["x_turned"], 1)
                            if live(i, par):
                                n, q = 2 * i + par, par
                                pe.wait_ge(s["xT_ready"], n + 1)
                                if later(i, par):
                                    pe.wait_ge(s["z_ready"], n - 1)
                                for k in range(KT):
                                    last = nc.tensor.matmul(bank[q][:, 0:DIM], xcT[q][:, k * P:(k + 1) * P], wg[:, k, :],
                                                            start=(k == 0), stop=(k == KT - 1))
                                last.then_inc(s["z_mm"], 1)
                        pairs(pe, step, -1, N)

        def attention():
            with ExitStack() as st:
                def tb(name, shape, dt=fp32):
                    return st.enter_context(nc.sbuf_tensor(name, shape, dt))

                def ring(name, shape, dt=fp32):
                    return [tb(f"{name}{i}", shape, dt) for i in range(2)]

                tok, h, xn = ring("tok", [SEQ, DIM]), ring("h", [SEQ, DIM]), ring("xn", [SEQ, DIM])
                h_scaled = tb("h_scaled", [SEQ, DIM])
                stats, stats2 = tb("stats", [SEQ, 6]), tb("stats2", [SEQ, 6])
                mv, mv2 = ring("mv", [SEQ, 2]), ring("mv2", [SEQ, 2])
                ve, ve2 = tb("ve", [SEQ, 1]), tb("ve2", [SEQ, 1])
                rs, rs2 = ring("rs", [SEQ, 1]), ring("rs2", [SEQ, 1])
                xnT, xn2T = ring("xnT", [P, KD, SEQ]), ring("xn2T", [P, KD, SEQ])
                rot = ring("rot", [SEQ, 2, 2 * DIM])
                qk = ring("qk", [SEQ, 2 * HEADS, PAD])
                qT, kT, qmT = ring("qT", [P, CH, SEQ]), ring("kT", [P, CH, SEQ]), ring("qmT", [P, CH, SEQ])
                v = ring("v", [SEQ, HEADS, PAD])
                probs = ring("probs", [SEQ, 4, CH, SEQ])
                oT = ring("oT", [P, CH, SEQ])
                denom = ring("denom", [SEQ, HEADS])
                att, h_back, h2, xn2 = ring("att", [SEQ, DIM]), ring("h_back", [SEQ, DIM]), ring("h2", [SEQ, DIM]), ring("xn2", [SEQ, DIM])

                names = """init tok_scaled h_ready stats_done mv_ready eps_added rstd_ready xn_ready xn_turned xnT_ready
                    qk_mm v_mm rot_mul qk_ready q_turned k_turned qT_ready kT_ready v_ready s_mm max_ready qm_turned qmT_ready
                    st_mm probs_ready o_mm oT_ready o_turned denom_ready att_ready h2_ready stats2_done mv2_ready eps2_added
                    rstd2_ready xn2_ready xn2_turned xn2T_ready logits_mm logits_saved""".split()
                s = {n: sem("b_" + n) for n in names}
                tok_loaded = [sem(f"b_tok_loaded{i}") for i in range(2)]
                h_stored = [sem(f"b_h_stored{i}") for i in range(2)]
                h_loaded = [sem(f"b_h_loaded{i}") for i in range(2)]
                h2_stored = [sem(f"b_h2_stored{i}") for i in range(2)]
                xn2_stored = [sem(f"b_xn2_stored{i}") for i in range(2)]
                INIT = 6

                N = BATCH
                FIRST, LAST = 3, 30

                def pairs(eng, step):
                    for t in range(-4, 2 * FIRST):
                        step(t // 2, t % 2)
                    with eng.Fori(FIRST, LAST) as i:
                        for par in range(2):
                            step(i, par)
                    for t in range(2 * LAST, N + 5):
                        step(t // 2, t % 2)

                def part(i, off):
                    if isinstance(i, int):
                        b = 2 * i + off
                        return b, off % 2, i + off // 2, 0 <= b < N, lambda k: 0 <= b + k < N
                    return 2 * i + off, off % 2, i + off // 2, True, lambda k: True

                with nc.Block() as block:
                    @block.sync
                    def _(sp):
                        sp.wait_ge(s["init"], INIT)

                        def step(i, par):
                            b, q, half, on, has = part(i, par + 3)
                            if on:
                                if has(-2):
                                    sp.wait_ge(s["tok_scaled"], b - 1)
                                sp.sem_inc(held["sp"], 1)
                                sp.dma_start(tok[q][1:1 + PATCHES, :], patch_rows[bass.ds(b * PATCHES, PATCHES), :]).then_inc(tok_loaded[q], 16)
                                sp.sem_inc(held["sp"], 1)
                                sp.dma_start(tok[q][1 + PATCHES:SEQ, :], txt[bass.ds(b * TEXT, TEXT), :]).then_inc(tok_loaded[q], 16)
                            b, q, half, on, has = part(i, par + 2)
                            if on:
                                sp.wait_ge(s["h_ready"], b + 1)
                                sp.sem_inc(held["sp"], 1)
                                sp.dma_start(h_rows[bass.ds(b * SEQ, SEQ), :], h[q][:, :]).then_inc(h_stored[q], 16)
                            b, q, half, on, has = part(i, par - 2)
                            if on:
                                sp.wait_ge(h_stored[q], 16 * (half + 1))
                                sp.sem_inc(held["sp"], 1)
                                if has(-2):
                                    sp.wait_ge(s["h2_ready"], b - 1)
                                sp.sem_inc(held["sp"], 1)
                                sp.dma_start(h_back[q][:, :], h_rows[bass.ds(b * SEQ, SEQ), :]).then_inc(h_loaded[q], 16)
                            b, q, half, on, has = part(i, par - 3)
                            if on:
                                sp.wait_ge(s["h2_ready"], b + 1)
                                sp.sem_inc(held["sp"], 1)
                                sp.dma_start(out[bass.ds(b * SEQ, SEQ), :], h2[q][:, :]).then_inc(h2_stored[q], 16)
                                sp.wait_ge(s["xn2_ready"], b + 1)
                                sp.sem_inc(held["sp"], 1)
                                sp.dma_start(xn_rows[bass.ds(b * SEQ, SEQ), :], xn2[q][:, :]).then_inc(xn2_stored[q], 16)
                        pairs(sp, step)
                        for par in range(2):
                            sp.wait_ge(h2_stored[par], 16 * (N // 2))
                            sp.wait_ge(xn2_stored[par], 16 * (N // 2))

                    @block.gpsimd
                    def _(pool):
                        for q in range(2):
                            nc.gpsimd.memset(tok[q][0:1, :], 0.0).then_inc(s["init"], 1)
                            nc.gpsimd.memset(qk[q][:, :, :], 0.0).then_inc(s["init"], 1)
                            nc.gpsimd.memset(v[q][:, :, :], 0.0).then_inc(s["init"], 1)
                        pool.wait_ge(s["init"], INIT)
                        for q in range(2):
                            nc.gpsimd.memset(qk[q][:, HEADS:, HEAD_DIM:HEAD_DIM + 1], 1.0).then_inc(s["init"], 1)
                            nc.gpsimd.memset(v[q][:, :, HEAD_DIM:HEAD_DIM + 1], 1.0).then_inc(s["init"], 1)
                        pool.wait_ge(s["init"], INIT + 4)

                        def step(i, par):
                            b, q, half, on, has = part(i, par - 3)
                            if on:
                                pool.wait_ge(s["att_ready"], b + 1)
                                pool.wait_ge(h_loaded[q], 16 * (half + 1))
                                if has(-2):
                                    pool.wait_ge(s["xn2_ready"], b - 1)
                                    pool.wait_ge(h2_stored[q], 16 * half)
                                nc.gpsimd.tensor_tensor(h2[q][:, :], h_back[q][:, :], att[q][:, :], ALU.add).then_inc(s["h2_ready"], 1)
                            b, q, half, on, has = part(i, par + 1)
                            if on:
                                pool.wait_ge(s["mv_ready"], b + 1)
                                if has(-2):
                                    pool.wait_ge(s["xn_ready"], b - 1)
                                pool.sem_inc(held["pool"], 1)
                                nc.gpsimd.tensor_scalar(ve[:, :], mv[q][:, 1:2], EPS, None, ALU.add).then_inc(s["eps_added"], 1)
                                pool.wait_ge(s["eps_added"], b + 1)
                                nc.gpsimd.tensor_tensor(rs[q][:, :], ve[:, :], eps_pow[0:SEQ, :], ALU.pow).then_inc(s["rstd_ready"], 1)
                            b, q, half, on, has = part(i, par - 3)
                            if on:
                                pool.wait_ge(s["mv2_ready"], b + 1)
                                pool.sem_inc(held["pool"], 1)
                                nc.gpsimd.tensor_scalar(ve2[:, :], mv2[q][:, 1:2], EPS, None, ALU.add).then_inc(s["eps2_added"], 1)
                                pool.wait_ge(s["eps2_added"], b + 1)
                                nc.gpsimd.tensor_tensor(rs2[q][:, :], ve2[:, :], eps_pow[0:SEQ, :], ALU.pow).then_inc(s["rstd2_ready"], 1)
                            b, q, half, on, has = part(i, par + 2)
                            if on:
                                pool.wait_ge(tok_loaded[q], 32 * (half + 1))
                                if has(-1):
                                    pool.wait_ge(s["h_ready"], b)
                                nc.gpsimd.tensor_tensor(h_scaled[:, :], tok[q][:, :], scale_rows[:, :], ALU.mult).then_inc(s["tok_scaled"], 1)
                                pool.wait_ge(s["tok_scaled"], b + 1)
                                if has(-2):
                                    pool.wait_ge(s["xn_ready"], b - 1)
                                    pool.wait_ge(h_stored[q], 16 * half)
                                nc.gpsimd.tensor_tensor(h[q][:, :], h_scaled[:, :], shift_rows[:, :], ALU.add).then_inc(s["h_ready"], 1)
                            b, q, half, on, has = part(i, par)
                            if on:
                                pool.wait_ge(s["rot_mul"], b + 1)
                                if has(-2):
                                    pool.wait_ge(s["qm_turned"], b - 1)
                                cosv = rot[q][:, 0, :].rearrange("p (n d two) -> p n d two", d=8, two=2)
                                sinv = rot[q][:, 1, :].rearrange("p (n d two) -> p n d two", d=8, two=2)
                                dst = qk[q][:, :, 0:HEAD_DIM].rearrange("p n (d two) -> p n d two", two=2)
                                for c in range(2):
                                    nc.gpsimd.tensor_tensor(dst[:, :, :, c], cosv[:, :, :, c], sinv[:, :, :, 1 - c], ALU.add).then_inc(s["qk_ready"], 1)
                        pairs(pool, step)

                    @block.vector
                    def _(dve):
                        def step(i, par):
                            b, q, half, on, has = part(i, par - 4)
                            if on:
                                dve.wait_ge(s["logits_mm"], b + 1)
                                nc.vector.tensor_copy(logits[:, :, :].rearrange("p b e -> p (b e)")[:, bass.ds(b * EXPERTS, EXPERTS)],
                                                      b7[0:SEQ, 0:EXPERTS]).then_inc(s["logits_saved"], 1)
                            b, q, half, on, has = part(i, par - 3)
                            if on:
                                dve.wait_ge(s["o_turned"], b + 1)
                                o = b4[0:SEQ, :].rearrange("p (n d) -> p n d", d=PAD)
                                if has(-2):
                                    dve.wait_ge(s["h2_ready"], b - 1)
                                    dve.wait_ge(s["att_ready"], b - 1)
                                nc.vector.reciprocal(denom[q][:, :], o[:, :, HEAD_DIM]).then_inc(s["denom_ready"], 1)
                                dve.wait_ge(s["denom_ready"], b + 1)
                                nc.vector.tensor_tensor(att[q][:, :].rearrange("p (n d) -> p n d", d=HEAD_DIM), o[:, :, 0:HEAD_DIM],
                                                        denom[q][:, :, None].broadcast_to([SEQ, HEADS, HEAD_DIM]), ALU.mult).then_inc(s["att_ready"], 1)
                            b, q, half, on, has = part(i, par + 1)
                            if on:
                                dve.wait_ge(s["h_ready"], b + 1)
                                if has(-1):
                                    dve.wait_ge(s["mv_ready"], b)
                                nc.vector.bn_stats(stats[:, :], h[q][:, :]).then_inc(s["stats_done"], 1)
                                dve.wait_ge(s["stats_done"], b + 1)
                                dve.sem_inc(held["dve"], 1)
                                nc.vector.bn_aggr(mv[q][:, :], stats[:, :]).then_inc(s["mv_ready"], 1)
                            b, q, half, on, has = part(i, par - 3)
                            if on:
                                dve.wait_ge(s["h2_ready"], b + 1)
                                if has(-1):
                                    dve.wait_ge(s["mv2_ready"], b)
                                nc.vector.bn_stats(stats2[:, :], h2[q][:, :]).then_inc(s["stats2_done"], 1)
                                dve.wait_ge(s["stats2_done"], b + 1)
                                dve.sem_inc(held["dve"], 1)
                                nc.vector.bn_aggr(mv2[q][:, :], stats2[:, :]).then_inc(s["mv2_ready"], 1)
                            b, q, half, on, has = part(i, par)
                            if on:
                                dve.wait_ge(s["qk_mm"], b + 1)
                                if has(-2):
                                    dve.wait_ge(s["qk_ready"], 2 * (b - 1))
                                nc.vector.tensor_tensor(rot[q][:, :, :], b4[0:SEQ, None, :].broadcast_to([SEQ, 2, 2 * DIM]),
                                                        rope_sb[:, :, :], ALU.mult).then_inc(s["rot_mul"], 1)
                            b, q, half, on, has = part(i, par + 1)
                            if on:
                                dve.wait_ge(s["rstd_ready"], b + 1)
                                dve.wait_ge(s["mv_ready"], b + 1)
                                if has(-2):
                                    dve.wait_ge(s["xn_turned"], b - 1)
                                nc.vector.tensor_scalar(xn[q][:, :], h[q][:, :], mv[q][:, 0:1], rs[q][:, :],
                                                        ALU.subtract, ALU.mult).then_inc(s["xn_ready"], 1)
                            b, q, half, on, has = part(i, par - 3)
                            if on:
                                dve.wait_ge(s["rstd2_ready"], b + 1)
                                dve.wait_ge(s["mv2_ready"], b + 1)
                                if has(-2):
                                    dve.wait_ge(s["xn2_turned"], b - 1)
                                    dve.wait_ge(xn2_stored[q], 16 * half)
                                nc.vector.tensor_scalar(xn2[q][:, :], h2[q][:, :], mv2[q][:, 0:1], rs2[q][:, :],
                                                        ALU.subtract, ALU.mult).then_inc(s["xn2_ready"], 1)
                            b, q, half, on, has = part(i, par - 1)
                            if on:
                                dve.wait_ge(s["s_mm"], b + 1)
                                dve.wait_ge(s["qk_ready"], 2 * (b + 1))
                                nc.vector.tensor_reduce(qk[q][:, 0:HEADS, HEAD_DIM].rearrange("p (c g) -> p g c", g=4),
                                                        quad[0:SEQ, :, 0:CH * SEQ].rearrange("p g (c k) -> p g c k", k=SEQ),
                                                        AX.X, ALU.max, negate=True).then_inc(s["max_ready"], 1)
                        pairs(dve, step)

                    @block.scalar
                    def _(act):
                        def evac(dst, src, signal):
                            nc.scalar.activation(dst, src, ACT.Copy).then_inc(signal, 1)

                        def step(i, par):
                            b, q, half, on, has = part(i, par - 1)
                            if on:
                                act.wait_ge(s["q_turned"], b + 1)
                                if has(-2):
                                    act.wait_ge(s["s_mm"], b - 1)
                                evac(qT[q][:, :, :], b6[:, 0:CH * SEQ].rearrange("p (c n) -> p c n", c=CH), s["qT_ready"])
                                act.wait_ge(s["k_turned"], b + 1)
                                if has(-2):
                                    act.wait_ge(s["st_mm"], b - 1)
                                evac(kT[q][:, :, :], b7[:, 0:CH * SEQ].rearrange("p (c n) -> p c n", c=CH), s["kT_ready"])
                            b, q, half, on, has = part(i, par - 2)
                            if on:
                                act.wait_ge(s["st_mm"], b + 1)
                                if has(-2):
                                    act.wait_ge(s["o_mm"], b - 1)
                                nc.scalar.activation(probs[q][:, :, :, :].rearrange("p g c n -> p g (c n)"), quad[0:SEQ, :, 0:CH * SEQ],
                                                     ACT.Exp, scale=HEAD_DIM ** -0.5).then_inc(s["probs_ready"], 1)
                                act.wait_ge(s["o_mm"], b + 1)
                                if has(-2):
                                    act.wait_ge(s["o_turned"], b - 1)
                                evac(oT[q][:, :, :], b6[:, 0:CH * SEQ].rearrange("p (c n) -> p c n", c=CH), s["oT_ready"])
                            b, q, half, on, has = part(i, par)
                            if on:
                                act.wait_ge(s["v_mm"], b + 1)
                                if has(-2):
                                    act.wait_ge(s["o_mm"], b - 1)
                                evac(v[q][:, :, 0:HEAD_DIM], b5[0:SEQ, 0:DIM].rearrange("p (n d) -> p n d", d=HEAD_DIM), s["v_ready"])
                            b, q, half, on, has = part(i, par + 1)
                            if on:
                                act.wait_ge(s["xn_turned"], b + 1)
                                if has(-2):
                                    act.wait_ge(s["v_mm"], b - 1)
                                evac(xnT[q][:, :, :], b7[:, 0:KD * SEQ].rearrange("p (c n) -> p c n", c=KD), s["xnT_ready"])
                            b, q, half, on, has = part(i, par - 1)
                            if on:
                                act.wait_ge(s["qm_turned"], b + 1)
                                if has(-2):
                                    act.wait_ge(s["st_mm"], b - 1)
                                evac(qmT[q][:, :, :], b5[:, 0:CH * SEQ].rearrange("p (c n) -> p c n", c=CH), s["qmT_ready"])
                            b, q, half, on, has = part(i, par - 3)
                            if on:
                                act.wait_ge(s["xn2_turned"], b + 1)
                                if has(-2):
                                    act.wait_ge(s["logits_mm"], b - 1)
                                evac(xn2T[q][:, :, :], b6[:, 0:KD * SEQ].rearrange("p (c n) -> p c n", c=KD), s["xn2T_ready"])
                        pairs(act, step)

                    @block.tensor
                    def _(pe):
                        def turn(dst, src, n, rows, signal):
                            for c in range(n):
                                last = nc.tensor.transpose(dst[:, c * rows:(c + 1) * rows], src[:, c * P:(c + 1) * P], idt[0:rows, 0:rows])
                            last.then_inc(signal, 1)

                        def step(i, par):
                            b, q, half, on, has = part(i, par - 1)
                            if on:
                                pe.wait_ge(s["qk_ready"], 2 * (b + 1))
                                if has(-3):
                                    pe.wait_ge(s["xn2T_ready"], b - 2)
                                    pe.wait_ge(s["logits_saved"], b - 2)
                                if b is not None and has(1):
                                    pe.wait_ge(s["xnT_ready"], b + 2)
                                flat = qk[q][:, :, :].rearrange("p n d -> p (n d)")
                                turn(b6, flat[:, 0:HEADS * PAD], CH, SEQ, s["q_turned"])
                                turn(b7, flat[:, HEADS * PAD:], CH, SEQ, s["k_turned"])
                            b, q, half, on, has = part(i, par - 2)
                            if on:
                                pe.wait_ge(s["qmT_ready"], b + 1)
                                pe.wait_ge(s["kT_ready"], b + 1)
                                for c in range(CH):
                                    for g in range(4):
                                        rows = slice(PAD * g, PAD * g + HEAD_DIM + 1)
                                        last = nc.tensor.matmul(quad[0:SEQ, g, c * SEQ:(c + 1) * SEQ], kT[q][rows, c, :], qmT[q][rows, c, :],
                                                                start=True, stop=True)
                                last.then_inc(s["st_mm"], 1)
                            b, q, half, on, has = part(i, par)
                            if on:
                                pe.wait_ge(s["xnT_ready"], b + 1)
                                if has(-3):
                                    pe.wait_ge(s["att_ready"], b - 2)
                                for k in range(KD):
                                    last = nc.tensor.matmul(b4[0:SEQ, :], xnT[q][:, k, :], wqkv_sb[:, k, 0:2 * DIM], start=(k == 0), stop=(k == KD - 1))
                                last.then_inc(s["qk_mm"], 1)
                                if has(-2):
                                    pe.wait_ge(s["qmT_ready"], b - 1)
                                for k in range(KD):
                                    last = nc.tensor.matmul(b5[0:SEQ, 0:DIM], xnT[q][:, k, :], wqkv_sb[:, k, 2 * DIM:], start=(k == 0), stop=(k == KD - 1))
                                last.then_inc(s["v_mm"], 1)
                            b, q, half, on, has = part(i, par - 1)
                            if on:
                                pe.wait_ge(s["qT_ready"], b + 1)
                                pe.wait_ge(s["kT_ready"], b + 1)
                                if has(-1):
                                    pe.wait_ge(s["probs_ready"], b)
                                for c in range(CH):
                                    for g in range(4):
                                        rows = slice(PAD * g, PAD * g + HEAD_DIM)
                                        last = nc.tensor.matmul(quad[0:SEQ, g, c * SEQ:(c + 1) * SEQ], qT[q][rows, c, :], kT[q][rows, c, :],
                                                                start=True, stop=True)
                                last.then_inc(s["s_mm"], 1)
                            b, q, half, on, has = part(i, par - 2)
                            if on:
                                pe.wait_ge(s["probs_ready"], b + 1)
                                pe.wait_ge(s["v_ready"], b + 1)
                                if has(1):
                                    pe.wait_ge(s["qT_ready"], b + 2)
                                for c in range(CH):
                                    for g in range(4):
                                        last = nc.tensor.matmul(b6[PAD * g:PAD * (g + 1), c * SEQ:(c + 1) * SEQ], v[q][:, 4 * c + g, :], probs[q][:, g, c, :],
                                                                start=True, stop=True)
                                last.then_inc(s["o_mm"], 1)
                            b, q, half, on, has = part(i, par + 1)
                            if on:
                                pe.wait_ge(s["xn_ready"], b + 1)
                                if has(-2):
                                    pe.wait_ge(s["kT_ready"], b - 1)
                                turn(b7, xn[q], KD, SEQ, s["xn_turned"])
                            b, q, half, on, has = part(i, par - 1)
                            if on:
                                pe.wait_ge(s["max_ready"], b + 1)
                                if has(1):
                                    pe.wait_ge(s["v_ready"], b + 2)
                                turn(b5, qk[q][:, :, :].rearrange("p n d -> p (n d)")[:, 0:HEADS * PAD], CH, SEQ, s["qm_turned"])
                            b, q, half, on, has = part(i, par - 3)
                            if on:
                                pe.wait_ge(s["xn2_ready"], b + 1)
                                if has(1):
                                    pe.wait_ge(s["oT_ready"], b + 2)
                                turn(b6, xn2[q], KD, SEQ, s["xn2_turned"])
                            b, q, half, on, has = part(i, par - 2)
                            if on:
                                pe.wait_ge(s["oT_ready"], b + 1)
                                if has(2):
                                    pe.wait_ge(s["rot_mul"], b + 3)
                                for c in range(CH):
                                    last = nc.tensor.transpose(b4[0:SEQ, c * P:(c + 1) * P], oT[q][:, c, :], idt[:, :])
                                last.then_inc(s["o_turned"], 1)
                            b, q, half, on, has = part(i, par - 3)
                            if on:
                                pe.wait_ge(s["xn2T_ready"], b + 1)
                                if has(4):
                                    pe.wait_ge(s["xnT_ready"], b + 5)
                                elif has(2):
                                    pe.wait_ge(s["kT_ready"], b + 3)
                                for k in range(KD):
                                    last = nc.tensor.matmul(b7[0:SEQ, 0:EXPERTS], xn2T[q][:, k, :], router_sb[:, k, :], start=(k == 0), stop=(k == KD - 1))
                                last.then_inc(s["logits_mm"], 1)
                        pairs(pe, step)

        def routing():
            with ExitStack() as st:
                def tb(name, shape, dt=fp32):
                    return st.enter_context(nc.sbuf_tensor(name, shape, dt))

                BE = [SEQ, BATCH, EXPERTS]
                rev = tb("rev", [P, EXPERTS])
                lanes = tb("lanes", [P, P])
                places = tb("places", [P, TILES_MOE])
                id_part = tb("id_part", [P, BATCH])
                spare_id = tb("spare_id", [P, 1])
                best, second = tb("best", [SEQ, BATCH]), tb("second", [SEQ, BATCH])
                hit, key, rest = tb("hit", BE), tb("key", BE), tb("rest", BE)
                key_max = tb("key_max", [SEQ, BATCH])
                pick = [tb(f"pick{j}", BE) for j in range(2)]
                both, before = tb("both", BE), tb("before", BE)
                total = tb("total", [P, BATCH, EXPERTS])
                scan = [tb(f"scan{j}", [P, BATCH, EXPERTS]) for j in range(2)]
                count_i, tiles_f = tb("count_i", [P, EXPERTS], i32), tb("tiles_f", [P, EXPERTS])
                tile_end = tb("tile_end", [P, EXPERTS + 1])
                first_slot = tb("first_slot", [P, EXPERTS])
                passed = tb("passed", [P, TILES_MOE, EXPERTS])
                expert_f = tb("expert_f", [P, TILES_MOE])
                slot_f = [tb(f"slot_f{j}", [SEQ, BATCH]) for j in range(2)]
                slot_i = [tb(f"slot_i{j}", [SEQ, BATCH], i32) for j in range(2)]
                tile_i, lane_i = tb("tile_i", [SEQ, BATCH], i32), tb("lane_i", [SEQ, BATCH], i32)
                tile_f = [tb(f"tile_f{j}", [SEQ, BATCH]) for j in range(2)]
                lane_f = [tb(f"lane_f{j}", [SEQ, BATCH]) for j in range(2)]
                gap, gate = tb("gap", [SEQ, BATCH]), [tb(f"gate{j}", [SEQ, BATCH]) for j in range(2)]
                field = [tb(f"field{j}", [SEQ, BATCH]) for j in range(2)]
                at_lane = [tb(f"at_lane{j}", [SEQ, P]) for j in range(2)]
                at_tile = [tb(f"at_tile{j}", [SEQ, 2, TILES_MOE]) for j in range(2)]
                tok_f = tb("tok_f", [P, TILES_MOE])
                step_done, counted, consts, exp_in, exp_out, spread, placed = (sem("c_" + n) for n in
                    ("step_done", "counted", "consts", "exp_in", "exp_out", "spread", "placed"))

                with nc.Block() as block:
                    @block.gpsimd
                    def _(pool):
                        i_ = dict(allow_small_or_imprecise_dtypes=True)
                        nc.gpsimd.iota(rev[:, :], [[-1, EXPERTS]], base=EXPERTS, channel_multiplier=0, **i_).then_inc(consts, 1)
                        nc.gpsimd.iota(lanes[:, :], [[1, P]], base=0, channel_multiplier=0, **i_).then_inc(consts, 1)
                        nc.gpsimd.iota(places[:, :], [[1, TILES_MOE]], base=0, channel_multiplier=0, **i_).then_inc(consts, 1)
                        nc.gpsimd.iota(id_part[:, :], [[SEQ, BATCH]], base=-TOKENS, channel_multiplier=1, **i_).then_inc(consts, 1)
                        nc.gpsimd.iota(spare_id[:, :], [[0, 1]], base=TOKENS, channel_multiplier=1, **i_).then_inc(consts, 1)

                    @block.vector
                    def _(dve):
                        done = [0]

                        def then(ins):
                            done[0] += 1
                            ins.then_inc(step_done, 1)
                            dve.wait_ge(step_done, done[0])

                        def per_token(ap):
                            return ap[:, :, None].broadcast_to(BE)

                        dve.wait_ge(consts, 5)
                        revb = rev[0:SEQ, None, :].broadcast_to(BE)
                        for j, (src, top) in enumerate(((logits, best), (rest, second))):
                            then(nc.vector.tensor_reduce(top[:, :], src[:, :, :], AX.X, ALU.max))
                            then(nc.vector.tensor_tensor(hit[:, :, :], src[:, :, :], per_token(top), ALU.is_equal))
                            then(nc.vector.tensor_tensor(key[:, :, :], hit[:, :, :], revb, ALU.mult))
                            then(nc.vector.tensor_reduce(key_max[:, :], key[:, :, :], AX.X, ALU.max))
                            then(nc.vector.tensor_tensor(pick[j][:, :, :], revb, per_token(key_max), ALU.is_equal))
                            if j == 0:
                                then(nc.vector.scalar_tensor_tensor(out=rest[:, :, :], in0=pick[0][:, :, :], scalar=-3.0e38,
                                                                    in1=logits[:, :, :], op0=ALU.mult, op1=ALU.add))
                        nc.vector.tensor_tensor(gap[:, :], second[:, :], best[:, :], ALU.subtract).then_inc(exp_in, 1)
                        then(nc.vector.tensor_tensor(both[:, :, :], pick[0][:, :, :], pick[1][:, :, :], ALU.add))
                        dve.wait_ge(counted, 2)
                        then(nc.vector.tensor_copy(before[:, :, :], b4[0:SEQ, :].rearrange("p (b e) -> p b e", e=EXPERTS)))
                        then(nc.vector.tensor_copy(total[:, :, :], b5[:, :].rearrange("p (b e) -> p b e", e=EXPERTS)))
                        src, k, turn = total, 1, 0
                        while k < BATCH:
                            dst = scan[turn]
                            then(nc.vector.tensor_copy(dst[:, 0:k, :], src[:, 0:k, :]))
                            then(nc.vector.tensor_tensor(dst[:, k:, :], src[:, k:, :], src[:, 0:BATCH - k, :], ALU.add))
                            src, k, turn = dst, 2 * k, 1 - turn
                        running = src
                        then(nc.vector.tensor_scalar(count_i[:, :], running[:, BATCH - 1, :], float(P - 1), None, ALU.add))
                        then(nc.vector.tensor_scalar(count_i[:, :], count_i[:, :], 7, None, ALU.arith_shift_right))
                        then(nc.vector.tensor_copy(tiles_f[:, :], count_i[:, :]))
                        then(nc.vector.memset(tile_end[:, :], 0.0))
                        for e in range(EXPERTS):
                            then(nc.vector.tensor_tensor(tile_end[:, e + 1:e + 2], tile_end[:, e:e + 1], tiles_f[:, e:e + 1], ALU.add))
                        then(nc.vector.tensor_scalar(first_slot[:, :], tile_end[:, 0:EXPERTS], float(P), None, ALU.mult))
                        TE = [P, TILES_MOE, EXPERTS]
                        then(nc.vector.tensor_tensor(passed[:, :, :], places[:, :, None].broadcast_to(TE),
                                                     tile_end[:, None, 1:].broadcast_to(TE), ALU.is_ge))
                        then(nc.vector.tensor_reduce(expert_f[:, :], passed[:, :, :], AX.X, ALU.add))
                        then(nc.vector.tensor_scalar(expert_of[:, :], expert_f[:, :], float(EXPERTS - 1), None, ALU.min))
                        then(nc.vector.tensor_tensor(before[:, :, :], before[:, :, :], running[0:SEQ, :, :], ALU.add))
                        then(nc.vector.tensor_tensor(before[:, :, :], before[:, :, :], total[0:SEQ, :, :], ALU.subtract))
                        then(nc.vector.tensor_tensor(before[:, :, :], before[:, :, :], first_slot[0:SEQ, None, :].broadcast_to(BE), ALU.add))
                        for j in range(2):
                            then(nc.vector.tensor_tensor(key[:, :, :], before[:, :, :], pick[j][:, :, :], ALU.mult))
                            then(nc.vector.tensor_reduce(slot_f[j][:, :], key[:, :, :], AX.X, ALU.add))
                            then(nc.vector.tensor_copy(slot_i[j][:, :], slot_f[j][:, :]))
                            then(nc.vector.tensor_scalar(tile_i[:, :], slot_i[j][:, :], 7, None, ALU.arith_shift_right))
                            then(nc.vector.tensor_scalar(lane_i[:, :], slot_i[j][:, :], P - 1, None, ALU.bitwise_and))
                            then(nc.vector.tensor_copy(tile_f[j][:, :], tile_i[:, :]))
                            then(nc.vector.tensor_copy(lane_f[j][:, :], lane_i[:, :]))
                            then(nc.vector.tensor_tensor(field[j][:, :], id_part[0:SEQ, :], lane_f[j][:, :], ALU.subtract))
                        dve.wait_ge(exp_out, 1)
                        then(nc.vector.tensor_scalar(key_max[:, :], gap[:, :], 1.0, None, ALU.add))
                        then(nc.vector.reciprocal(gate[0][:, :], key_max[:, :]))
                        then(nc.vector.tensor_tensor(gate[1][:, :], gate[0][:, :], gap[:, :], ALU.mult))
                        n = 0
                        for b in range(BATCH):
                            for j in range(2):
                                q = n % 2
                                if n >= 2:
                                    dve.wait_ge(placed, n - 1)
                                nc.vector.tensor_scalar(at_lane[q][:, :], lanes[0:SEQ, :], lane_f[j][:, b:b + 1], None, ALU.is_equal).then_inc(spread, 1)
                                for f, val in enumerate((field[j], gate[j])):
                                    nc.vector.tensor_scalar(at_tile[q][:, f, :], places[0:SEQ, :], tile_f[j][:, b:b + 1], val[:, b:b + 1],
                                                            ALU.is_equal, ALU.mult).then_inc(spread, 1)
                                n += 1
                        dve.wait_ge(placed, n)
                        then(nc.vector.tensor_copy(weight_of[:, :], b6[:, TILES_MOE:2 * TILES_MOE]))
                        then(nc.vector.tensor_scalar(token_of[:, :], b6[:, 0:TILES_MOE], spare_id[:, :], None, ALU.add))

                    @block.scalar
                    def _(act):
                        act.wait_ge(exp_in, 1)
                        nc.scalar.activation(gap[:, :], gap[:, :], ACT.Exp).then_inc(exp_out, 1)

                    @block.tensor
                    def _(pe):
                        pe.wait_ge(step_done, 12)
                        flat = both[:, :, :].rearrange("p b e -> p (b e)")
                        nc.tensor.matmul(b4[0:SEQ, :], prefix_sb[:, :], flat, start=True, stop=True).then_inc(counted, 1)
                        nc.tensor.matmul(b5[:, :], ones[0:SEQ, :], flat, start=True, stop=True).then_inc(counted, 1)
                        N = 2 * BATCH
                        for n in range(N):
                            pe.wait_ge(spread, 3 * (n + 1))
                            nc.tensor.matmul(b6[:, 0:2 * TILES_MOE], at_lane[n % 2][:, :], at_tile[n % 2][:, :, :].rearrange("p f t -> p (f t)"),
                                             start=(n == 0), stop=(n == N - 1)).then_inc(placed, 1)

        def experts():
            with ExitStack() as st:
                def tb(name, shape, dt=fp32):
                    return st.enter_context(nc.sbuf_tensor(name, shape, dt))

                def ring(name, shape, dt=fp32):
                    return [tb(f"{name}{i}", shape, dt) for i in range(2)]

                idx, idx_out = ring("idx", [P, 1], i32), ring("idx_out", [P, 1], i32)
                xg, xgT = ring("xg", [P, DIM]), ring("xgT", [P, KD, P])
                silu, hid, hidT, y = ring("silu", [P, HIDDEN]), ring("hid", [P, HIDDEN]), ring("hidT", [P, KH, P]), ring("y", [P, DIM])
                names = """idx_ready idx_out_ready x_turned xT_ready gate_mm up_mm silu_ready hid_ready hid_turned hidT_ready y_mm y_ready""".split()
                s = {n: sem("d_" + n) for n in names}
                gathered = [sem(f"d_gathered{i}") for i in range(2)]
                added = sem("d_added")
                N = TILES_MOE
                FIRST, LAST = 2, N // 2 - 1

                def pairs(eng, step, lo, hi):
                    for t in range(lo, 2 * FIRST):
                        step(t // 2, t % 2)
                    with eng.Fori(FIRST, LAST) as i:
                        for par in range(2):
                            step(i, par)
                    for t in range(2 * LAST, hi):
                        step(t // 2, t % 2)

                def part(i, off):
                    if isinstance(i, int):
                        n = 2 * i + off
                        return n, off % 2, i + off // 2, 0 <= n < N, lambda k: 0 <= n + k < N
                    return 2 * i + off, off % 2, i + off // 2, True, lambda k: True

                with nc.Block() as block:
                    @block.gpsimd
                    def _(pool):
                        def step(i, par):
                            n, q, half, on, has = part(i, par + 2)
                            if on:
                                if has(-2):
                                    pool.wait_ge(gathered[q], 16 * half)
                                    pool.wait_ge(s["x_turned"], n - 1)
                                pool.sem_inc(held["pool"], 1)
                                nc.gpsimd.tensor_copy(idx[q][:, :], token_of[:, bass.ds(n, 1)]).then_inc(s["idx_ready"], 1)
                                pool.wait_ge(s["idx_ready"], n + 1)
                                pool.sem_inc(held["pool"], 1)
                                nc.gpsimd.indirect_dma_start(xg[q][:, :], None, xn_rows, bass.IndirectOffsetOnAxis(idx[q][:, :], 0)).then_inc(gathered[q], 16)
                            n, q, half, on, has = part(i, par - 1)
                            if on:
                                if has(-1):
                                    pool.wait_ge(added, 16 * n)
                                pool.sem_inc(held["pool"], 1)
                                nc.gpsimd.tensor_copy(idx_out[q][:, :], token_of[:, bass.ds(n, 1)]).then_inc(s["idx_out_ready"], 1)
                                pool.wait_ge(s["idx_out_ready"], n + 1)
                                pool.wait_ge(s["y_ready"], n + 1)
                                pool.sem_inc(held["pool"], 1)
                                nc.gpsimd.indirect_dma_start(out, bass.IndirectOffsetOnAxis(idx_out[q][:, :], 0), y[q][:, :], None,
                                                             compute_op=ALU.add).then_inc(added, 16)
                        pairs(pool, step, -2, N + 1)
                        pool.wait_ge(added, 16 * N)

                    @block.scalar
                    def _(act):
                        def step(i, par):
                            n, q, half, on, has = part(i, par)
                            if on:
                                act.wait_ge(s["gate_mm"], n + 1)
                                if has(-2):
                                    act.wait_ge(s["hid_ready"], n - 1)
                                nc.scalar.activation(silu[q][:, :], quad[:, 2 * q, :], ACT.Silu).then_inc(s["silu_ready"], 1)
                            n, q, half, on, has = part(i, par - 1)
                            if on:
                                act.wait_ge(s["hid_turned"], n + 1)
                                if has(-2):
                                    act.wait_ge(s["y_mm"], n - 1)
                                nc.scalar.activation(hidT[q][:, :, :].rearrange("p c n -> p (c n)"), b4[:, :], ACT.Copy).then_inc(s["hidT_ready"], 1)
                            n, q, half, on, has = part(i, par + 1)
                            if on:
                                act.wait_ge(s["x_turned"], n + 1)
                                if has(-2):
                                    act.wait_ge(s["up_mm"], n - 1)
                                nc.scalar.activation(xgT[q][:, :, :].rearrange("p c n -> p (c n)"), b5[:, 0:DIM], ACT.Copy).then_inc(s["xT_ready"], 1)
                        pairs(act, step, -1, N + 1)

                    @block.vector
                    def _(dve):
                        def step(i, par):
                            n, q, half, on, has = part(i, par)
                            if on:
                                dve.wait_ge(s["up_mm"], n + 1)
                                dve.wait_ge(s["silu_ready"], n + 1)
                                if has(-2):
                                    dve.wait_ge(s["hid_turned"], n - 1)
                                nc.vector.tensor_tensor(hid[q][:, :], quad[:, 2 * q + 1, :], silu[q][:, :], ALU.mult).then_inc(s["hid_ready"], 1)
                            n, q, half, on, has = part(i, par - 1)
                            if on:
                                dve.wait_ge(s["y_mm"], n + 1)
                                if has(-2):
                                    dve.wait_ge(added, 16 * (n - 1))
                                nc.vector.tensor_scalar(y[q][:, :], (b6, b7)[q][:, 0:DIM], weight_of[:, bass.ds(n, 1)], None, ALU.mult).then_inc(s["y_ready"], 1)
                        pairs(dve, step, 0, N + 1)

                    @block.tensor
                    def _(pe):
                        pe.wait_ge(experts_in, 16 * 2 * EXPERTS)

                        def step(i, par):
                            n, q, half, on, has = part(i, par)
                            if on:
                                pe.wait_ge(s["xT_ready"], n + 1)
                                pe.sem_inc(held["pe"], 1)
                                e = pe.value_load(expert_of[0:1, bass.ds(n, 1)], min_val=0, max_val=EXPERTS - 1)
                                for up in range(2):
                                    if has(-2):
                                        pe.wait_ge(s["hid_ready"], n - 1)
                                    for k in range(KD):
                                        last = nc.tensor.matmul(quad[:, 2 * q + up, :], xgT[q][:, k, :],
                                                                w13_sb[:, bass.ds(e * (KD * 2 * HIDDEN) + (k * 2 + up) * HIDDEN, HIDDEN)],
                                                                start=(k == 0), stop=(k == KD - 1))
                                    last.then_inc(s["up_mm" if up else "gate_mm"], 1)
                            n, q, half, on, has = part(i, par - 1)
                            if on:
                                pe.wait_ge(s["hid_ready"], n + 1)
                                if has(-1):
                                    pe.wait_ge(s["hidT_ready"], n)
                                for k in range(KH):
                                    last = nc.tensor.transpose(b4[:, k * P:(k + 1) * P], hid[q][:, k * P:(k + 1) * P], idt[:, :])
                                last.then_inc(s["hid_turned"], 1)
                            n, q, half, on, has = part(i, par + 1)
                            if on:
                                pe.wait_ge(gathered[q], 16 * (half + 1))
                                if has(-1):
                                    pe.wait_ge(s["xT_ready"], n)
                                for k in range(KD):
                                    last = nc.tensor.transpose(b5[:, k * P:(k + 1) * P], xg[q][:, k * P:(k + 1) * P], idt[:, :])
                                last.then_inc(s["x_turned"], 1)
                            n, q, half, on, has = part(i, par - 1)
                            if on:
                                pe.wait_ge(s["hidT_ready"], n + 1)
                                if has(-2):
                                    pe.wait_ge(s["y_ready"], n - 1)
                                pe.sem_inc(held["pe"], 1)
                                e = pe.value_load(expert_of[0:1, bass.ds(n, 1)], min_val=0, max_val=EXPERTS - 1)
                                for k in range(KH):
                                    last = nc.tensor.matmul((b6, b7)[q][:, 0:DIM], hidT[q][:, k, :],
                                                            w2_sb[:, bass.ds(e * (KH * DIM) + k * DIM, DIM)], start=(k == 0), stop=(k == KH - 1))
                                last.then_inc(s["y_mm"], 1)
                        pairs(pe, step, -1, N + 1)

        experts_in = sem("experts_in")
        zero_tile = sb("zero_tile", [P, DIM])
        tokenizer()
        attention()
        routing()
        experts()


def kernel(**inputs):
    import concourse.bacc as bacc
    from concourse.bass_utils import run_bass_kernel_spmd

    a = {k: np.asarray(v) for k, v in inputs.items()}
    G, PT = GRID, PATCH
    patches = a["x"].reshape(BATCH, CHANNELS, G, PT, G, PT).transpose(0, 2, 4, 3, 5, 1).reshape(BATCH * PATCHES, PATCH_DIM)
    rows = lambda w: w.reshape(-1, P, w.shape[-1]).transpose(1, 0, 2)
    wqkv = np.concatenate([rows(a[f"L0_attn_w{c}"].T) for c in "qkv"], axis=2)
    freq = 1.0 / 10000.0 ** (np.arange(0, HEAD_DIM, 2, dtype=np.float32) / HEAD_DIM)
    angle = np.outer(np.arange(SEQ, dtype=np.float32), freq.astype(np.float32))
    cos, sin = np.cos(angle), np.sin(angle)
    rope = np.stack([np.tile(np.repeat(cos, 2, axis=1), (1, 2 * HEADS)),
                     np.tile(np.stack([sin, -sin], axis=2).reshape(SEQ, HEAD_DIM), (1, 2 * HEADS))], axis=1).astype(np.float32)
    w13 = a["L0_ffn_moe_w13"].reshape(EXPERTS, KD, P, 2 * HIDDEN).transpose(0, 2, 1, 3).reshape(EXPERTS, P, -1)
    w2 = a["L0_ffn_moe_w2"].reshape(EXPERTS, KH, P, DIM).transpose(0, 2, 1, 3).reshape(EXPERTS, P, -1)
    arrays = dict(
        patches=patches, txt=a["txt"].reshape(BATCH * TEXT, DIM),
        ln1_g=a["L0_tok_ln1_g"].reshape(KT, P).T, ln1_b=a["L0_tok_ln1_b"].reshape(KT, P).T,
        w_proj=rows(a["L0_tok_W_proj"]), b_proj=a["L0_tok_b_proj"], ln2_g=a["L0_tok_ln2_g"], ln2_b=a["L0_tok_ln2_b"],
        cls_token=a["L0_tok_cls_token"].reshape(1, DIM), pos_emb=a["L0_tok_pos_emb"].reshape(1 + PATCHES, DIM),
        wqkv=wqkv, router=rows(a["L0_ffn_moe_router"]), w13=w13, w2=w2,
        ident=np.eye(P, dtype=np.float32), rope=rope,
        prefix=np.triu(np.ones((SEQ, SEQ), np.float32), 1),
    )
    nc = bacc.Bacc("TRN2", target_bir_lowering=False, num_devices=1)
    sent, args = {}, {}
    for name, x in arrays.items():
        x = np.ascontiguousarray(x)
        sent[f"in_{name}"] = x
        args[name] = nc.dram_tensor(f"in_{name}", x.shape, mybir.dt.from_np(x.dtype), kind="ExternalInput").ap()
    out = nc.dram_tensor("out", (TOKENS + SPARE, DIM), mybir.dt.float32, kind="ExternalOutput").ap()
    build(nc, out=out, **args)
    got = run_bass_kernel_spmd(nc, [sent], core_ids=[0]).results[0]["out"]
    return got[:TOKENS].reshape(BATCH, SEQ, DIM)
```

```python
from contextlib import ExitStack

import numpy as np
import concourse.bass as bass
from concourse import mybir

BATCH, CHANNELS, IMAGE, PATCH = 64, 3, 96, 16
GRID = IMAGE // PATCH
PATCHES = GRID * GRID
DIM, TEXT = 256, 32
SEQ = 1 + PATCHES + TEXT
TOKENS = BATCH * SEQ
PATCH_DIM = CHANNELS * PATCH * PATCH
HEADS, HEAD_DIM = 16, 16
EXPERTS, HIDDEN, TOP_K = 8, 512, 2
EPS = 1e-5
P = 128
TILES_TOK = BATCH * PATCHES // P
KT = PATCH_DIM // P
KD = DIM // P
KH = HIDDEN // P
PAD = 32
CH = HEADS * PAD // P
TILES_MOE = (TOKENS * TOP_K + EXPERTS * (P - 1)) // P
SPARE = P
BANK = 512
W_EXPERT = KD * 2 * HIDDEN + KH * DIM
W_CHUNK = EXPERTS * W_EXPERT // BATCH
MAX_LOADS = 16


def build(nc, patches, txt, ln1_g, ln1_b, w_proj, b_proj, ln2_g, ln2_b, cls_token, pos_emb,
          wqkv, router, experts_w, ident, rope, prefix, out):
    fp32, i32, fp16, bf16 = mybir.dt.float32, mybir.dt.int32, mybir.dt.float16, mybir.dt.bfloat16
    ALU, ACT, AX = mybir.AluOpType, mybir.ActivationFunctionType, mybir.AxisListType
    ctx = ExitStack()
    with ctx:
        def sb(name, shape, dt=fp32):
            return ctx.enter_context(nc.sbuf_tensor(name, shape, dt))

        def sem(name):
            return ctx.enter_context(nc.semaphore(name))

        patch_rows = nc.dram_tensor("patch_rows", (BATCH * PATCHES, DIM), fp32).ap()
        h_rows = nc.dram_tensor("h_rows", (TOKENS, DIM), fp32).ap()
        xn_rows = nc.dram_tensor("xn_rows", (TOKENS + SPARE, DIM + EXPERTS), fp32).ap()

        bank = [ctx.enter_context(nc.psum_tensor(f"bank{i}", [P, BANK], fp32)) for i in range(4, 8)]
        quad = ctx.enter_context(nc.psum_tensor("quad", [P, 4, BANK], fp32))
        b4, b5, b6, b7 = bank

        idt = sb("idt", [P, P])
        eps_pow = sb("eps_pow", [P, 1])
        wqkv_hi, wqkv_lo = (sb(f"wqkv_{x}", [P, KD, 3 * DIM], fp16) for x in ("hi", "lo"))
        w_hi, w_lo = (sb(f"w_{x}", [P, EXPERTS * W_EXPERT], fp16) for x in ("hi", "lo"))
        scale = sb("scale", [P, 2])
        unscale = sb("unscale", [P, 2])
        up_scale, y_scale = sb("up_scale", [P, 1]), sb("y_scale", [P, 1])
        router_sb = sb("router_sb", [P, KD, EXPERTS])
        rope_sb = sb("rope_sb", [SEQ, 2, 2 * DIM])
        prefix_sb = sb("prefix_sb", [SEQ, SEQ])
        ones = sb("ones", [P, P])
        scale_rows = sb("scale_rows", [SEQ, DIM])
        shift_rows = sb("shift_rows", [SEQ, DIM])
        shift_add = sb("shift_add", [SEQ, DIM])
        logits = sb("logits", [SEQ, BATCH, EXPERTS])
        expert_of = sb("expert_of", [P, TILES_MOE], i32)
        token_of = sb("token_of", [P, TILES_MOE], i32)
        is_expert = sb("is_expert", [P, TILES_MOE, EXPERTS])

        held = {e: sem("held_" + e) for e in ("dve", "pool", "pe", "sp")}

        def tokenizer():
            with ExitStack() as st:
                def tb(name, shape, dt=fp32):
                    return st.enter_context(nc.sbuf_tensor(name, shape, dt))

                wp = tb("wp", [P, KT, DIM])
                wqkv_sb = tb("wqkv_sb", [P, KD, 3 * DIM])
                w_part = [tb(f"w_part{i}", [P, EXPERTS * W_EXPERT // MAX_LOADS]) for i in range(2)]
                largest, all_max = tb("largest", [P, MAX_LOADS + 1]), tb("all_max", [P, 2])
                peak = tb("peak", [P, 2])
                wg = tb("wg", [P, KT, DIM])
                g1 = tb("g1", [P, KT])
                b1 = tb("b1", [P, KT])
                b1_wide = tb("b1_wide", [P, KT, P])
                bp = tb("bp", [P, DIM])
                bias = tb("bias", [P, DIM])
                xt = [tb(f"xt{i}", [P, PATCH_DIM]) for i in range(2)]
                xc = [tb(f"xc{i}", [P, PATCH_DIM]) for i in range(2)]
                xcT = [tb(f"xcT{i}", [P, PATCH_DIM]) for i in range(2)]
                st1 = tb("st1", [P, 2, 6])
                mv1 = [tb(f"tmv1{i}", [P, 2]) for i in range(2)]
                ve1 = tb("tve1", [P, 1])
                rs1 = [tb(f"trs1{i}", [P, 1]) for i in range(2)]
                z = [tb(f"z{i}", [P, DIM]) for i in range(2)]
                st2 = tb("tst2", [P, 6])
                mv2 = [tb(f"tmv2{i}", [P, 2]) for i in range(2)]
                ve2 = tb("tve2", [P, 1])
                rs2 = [tb(f"trs2{i}", [P, 1]) for i in range(2)]
                zn = [tb(f"zn{i}", [P, DIM]) for i in range(2)]

                names = """t_const t_small t_wg t_wide t_bias_mm t_bias x_turned xT_ready z_mm stats1 mv1_ready eps1 rstd1
                    xc_ready z_ready stats2 mv2_ready eps2 rstd2 zn_ready t_ones t_pow
                    sc_init sh_done zero_spare part_max own_max peak_ready scale_step split_hi split_lo""".split()
                part_loaded = [sem(f"a_part_loaded{i}") for i in range(2)]
                s = {n: sem("a_" + n) for n in names}
                x_loaded = [sem(f"a_x_loaded{i}") for i in range(2)]
                z_stored = [sem(f"a_z_stored{i}") for i in range(2)]
                spare_stored, weights_in, rope_in, table_in = (sem("a_" + x) for x in ("spare_stored", "weights_in", "rope_in", "table_in"))

                N = TILES_TOK
                FIRST, LAST = 2, (N - 2) // 2
                WP = EXPERTS * W_EXPERT // MAX_LOADS

                def pairs(eng, step, lo, hi):
                    for t in range(lo, 2 * FIRST):
                        step(t // 2, t % 2)
                    with eng.Fori(FIRST, LAST) as i:
                        for par in range(2):
                            step(i, par)
                    for t in range(2 * LAST, hi):
                        step(t // 2, t % 2)

                def live(i, off):
                    return not isinstance(i, int) or 0 <= 2 * i + off < N

                def later(i, off, back=2):
                    return not isinstance(i, int) or 2 * i + off >= back

                with nc.Block() as block:
                    @block.sync
                    def _(sp):
                        sp.dma_start(idt[:, :], ident).then_inc(s["t_const"], 16)
                        sp.dma_start(wp[:, :, :], w_proj).then_inc(s["t_const"], 16)
                        sp.dma_start(g1[:, :], ln1_g).then_inc(s["t_const"], 16)
                        sp.dma_start(b1[:, :], ln1_b).then_inc(s["t_const"], 16)
                        sp.dma_start(bp[:, :], b_proj[None, :].broadcast_to([P, DIM])).then_inc(s["t_const"], 16)
                        sp.dma_start(wqkv_sb[:, :, :], wqkv).then_inc(weights_in, 16)

                        def step(i, par):
                            if live(i, par):
                                n = 2 * i + par
                                if later(i, par):
                                    sp.wait_ge(s["xc_ready"], n - 1)
                                sp.sem_inc(held["sp"], 1)
                                sp.dma_start(xt[par][:, :], patches[bass.ds(n * P, P), :]).then_inc(x_loaded[par], 16)
                            if live(i, par + 2):
                                n = 2 * i + par
                                if not isinstance(i, int) or 0 <= n < MAX_LOADS:
                                    if later(i, par):
                                        sp.wait_ge(s["part_max"], n - 1)
                                        sp.sem_inc(held["sp"], 1)
                                    sp.dma_start(w_part[par][:, :], experts_w[:, bass.ds(n * WP, WP)]).then_inc(part_loaded[par], 16)
                            off = par - 4
                            if live(i, off):
                                n = 2 * i + off
                                sp.wait_ge(s["zn_ready"], n + 1)
                                sp.sem_inc(held["sp"], 1)
                                sp.dma_start(patch_rows[bass.ds(n * P, P), :], zn[off % 2][:, :]).then_inc(z_stored[off % 2], 16)
                        pairs(sp, step, 0, N + 4)
                        sp.dma_start(router_sb[:, :, :], router).then_inc(weights_in, 16)
                        sp.dma_start(prefix_sb[:, :], prefix).then_inc(weights_in, 16)
                        for par in range(2):
                            sp.wait_ge(z_stored[par], 16 * (N // 2))
                        sp.wait_ge(weights_in, 48)
                        sp.wait_ge(table_in, 16 * 5)
                        sp.wait_ge(spare_stored, 16)

                    @block.gpsimd
                    def _(pool):
                        nc.gpsimd.memset(eps_pow[:, :], -0.5).then_inc(s["t_pow"], 1)
                        nc.gpsimd.memset(ones[:, :], 1.0).then_inc(s["t_ones"], 1)
                        nc.gpsimd.memset(scale_rows[:, :], 1.0).then_inc(s["sc_init"], 1)
                        nc.gpsimd.memset(shift_rows[:, :], 0.0).then_inc(s["sc_init"], 1)
                        nc.gpsimd.memset(shift_add[:, :], 0.0).then_inc(s["sc_init"], 1)
                        pool.wait_ge(s["sc_init"], 3)
                        pool.dma_start(scale_rows[1:1 + PATCHES, :], ln2_g[None, :].broadcast_to([PATCHES, DIM])).then_inc(table_in, 16)
                        pool.dma_start(shift_rows[1:1 + PATCHES, :], ln2_b[None, :].broadcast_to([PATCHES, DIM])).then_inc(table_in, 16)
                        pool.dma_start(shift_rows[0:1, :], cls_token).then_inc(table_in, 16)
                        pool.dma_start(shift_add[0:1 + PATCHES, :], pos_emb).then_inc(table_in, 16)
                        pool.dma_start(rope_sb[:, :, :], rope).then_inc(rope_in, 16)
                        pool.wait_ge(s["t_ones"], 1)
                        nc.gpsimd.memset(zero_tile[:, :], 0.0).then_inc(s["zero_spare"], 1)
                        pool.wait_ge(s["zero_spare"], 1)
                        pool.dma_start(xn_rows[TOKENS:TOKENS + SPARE, :], zero_tile[:, :]).then_inc(spare_stored, 16)
                        pool.dma_start(out[TOKENS:TOKENS + SPARE, :], zero_tile[:, 0:DIM]).then_inc(table_in, 16)

                        def step(i, par):
                            if live(i, par + 2):
                                n, q = 2 * i + par + 2, par
                                pool.wait_ge(s["mv1_ready"], n + 1)
                                if later(i, par + 2):
                                    pool.wait_ge(s["xc_ready"], n - 1)
                                pool.sem_inc(held["pool"], 1)
                                nc.gpsimd.tensor_scalar(ve1[:, :], mv1[q][:, 1:2], EPS, None, ALU.add).then_inc(s["eps1"], 1)
                                pool.wait_ge(s["eps1"], n + 1)
                                nc.gpsimd.tensor_tensor(rs1[q][:, :], ve1[:, :], eps_pow[:, :], ALU.pow).then_inc(s["rstd1"], 1)
                            if live(i, par - 1):
                                n, q = 2 * i + par - 1, (par - 1) % 2
                                pool.wait_ge(s["mv2_ready"], n + 1)
                                pool.sem_inc(held["pool"], 1)
                                nc.gpsimd.tensor_scalar(ve2[:, :], mv2[q][:, 1:2], EPS, None, ALU.add).then_inc(s["eps2"], 1)
                                pool.wait_ge(s["eps2"], n + 1)
                                nc.gpsimd.tensor_tensor(rs2[q][:, :], ve2[:, :], eps_pow[:, :], ALU.pow).then_inc(s["rstd2"], 1)
                        pairs(pool, step, -2, N + 1)
                        pool.wait_ge(table_in, 16 * 5)
                        nc.gpsimd.tensor_tensor(shift_rows[:, :], shift_rows[:, :], shift_add[:, :], ALU.add).then_inc(s["sh_done"], 1)
                        pool.wait_ge(s["sh_done"], 1)
                        pool.wait_ge(s["own_max"], 1)
                        nc.gpsimd.partition_all_reduce(peak[:, :], all_max[:, :], P, bass.bass_isa.ReduceOp.max).then_inc(s["peak_ready"], 1)

                    @block.vector
                    def _(dve):
                        dve.wait_ge(s["t_const"], 80)
                        dve.wait_ge(s["t_ones"], 1)
                        for k in range(KT):
                            nc.vector.tensor_scalar(wg[:, k, :], wp[:, k, :], g1[:, k:k + 1], None, ALU.mult).then_inc(s["t_wg"], 1)
                            nc.vector.tensor_scalar(b1_wide[:, k, :], ones[:, :], b1[:, k:k + 1], None, ALU.mult).then_inc(s["t_wide"], 1)
                        dve.wait_ge(s["t_bias_mm"], 1)
                        nc.vector.tensor_tensor(bias[:, :], b4[:, 0:DIM], bp[:, :], ALU.add).then_inc(s["t_bias"], 1)
                        dve.wait_ge(s["t_bias"], 1)

                        def step(i, par):
                            if live(i, par + 2):
                                n, q = 2 * i + par + 2, par
                                half = i + 1
                                dve.wait_ge(x_loaded[q], 16 * (half + 1))
                                for c in range(2):
                                    nc.vector.bn_stats(st1[:, c, :], xt[q][:, c * 384:(c + 1) * 384]).then_inc(s["stats1"], 1)
                                dve.wait_ge(s["stats1"], 2 * n + 2)
                                dve.sem_inc(held["dve"], 1)
                                nc.vector.bn_aggr(mv1[q][:, :], st1[:, :, :].rearrange("p a b -> p (a b)")).then_inc(s["mv1_ready"], 1)
                            if live(i, par - 1):
                                n, q = 2 * i + par - 1, (par - 1) % 2
                                dve.wait_ge(s["z_mm"], n + 1)
                                nc.vector.tensor_tensor(z[q][:, :], bank[q][:, 0:DIM], bias[:, :], ALU.add).then_inc(s["z_ready"], 1)
                                dve.wait_ge(s["z_ready"], n + 1)
                                nc.vector.bn_stats(st2[:, :], z[q][:, :]).then_inc(s["stats2"], 1)
                                dve.wait_ge(s["stats2"], n + 1)
                                dve.sem_inc(held["dve"], 1)
                                nc.vector.bn_aggr(mv2[q][:, :], st2[:, :]).then_inc(s["mv2_ready"], 1)
                            if live(i, par + 2):
                                n, q = 2 * i + par + 2, par
                                dve.wait_ge(s["rstd1"], n + 1)
                                if later(i, par + 2):
                                    dve.wait_ge(s["x_turned"], n - 1)
                                dve.wait_ge(s["mv1_ready"], n + 1)
                                nc.vector.tensor_scalar(xc[q][:, :], xt[q][:, :], mv1[q][:, 0:1], rs1[q][:, :],
                                                        ALU.subtract, ALU.mult).then_inc(s["xc_ready"], 1)
                            n = 2 * i + par
                            if not isinstance(i, int) or 0 <= n < MAX_LOADS:
                                dve.wait_ge(part_loaded[par], 16 * (i + 1))
                                nc.vector.tensor_reduce(largest[:, bass.ds(n, 1)], w_part[par][:, :], AX.X, ALU.max,
                                                        apply_absolute_value=True).then_inc(s["part_max"], 1)
                            if live(i, par - 1):
                                n, q = 2 * i + par - 1, (par - 1) % 2
                                half = i + (par - 1) // 2
                                dve.wait_ge(s["rstd2"], n + 1)
                                dve.wait_ge(s["mv2_ready"], n + 1)
                                if later(i, par - 1):
                                    dve.wait_ge(z_stored[q], 16 * half)
                                nc.vector.tensor_scalar(zn[q][:, :], z[q][:, :], mv2[q][:, 0:1], rs2[q][:, :],
                                                        ALU.subtract, ALU.mult).then_inc(s["zn_ready"], 1)
                        pairs(dve, step, -2, N + 1)

                        steps = [0]

                        def then(ins):
                            steps[0] += 1
                            ins.then_inc(s["scale_step"], 1)
                            dve.wait_ge(s["scale_step"], steps[0])

                        dve.wait_ge(s["part_max"], MAX_LOADS)
                        dve.wait_ge(weights_in, 48)
                        dve.wait_ge(rope_in, 16)
                        then(nc.vector.tensor_reduce(all_max[:, 0:1], wqkv_sb[:, :, :], AX.XY, ALU.max, apply_absolute_value=True))
                        nc.vector.tensor_reduce(all_max[:, 1:2], largest[:, 0:MAX_LOADS], AX.X, ALU.max).then_inc(s["own_max"], 1)
                        dve.wait_ge(s["peak_ready"], 1)
                        then(nc.vector.tensor_scalar(peak[:, :], peak[:, :], 2.0 ** -20, 2.0 ** 40, ALU.max, ALU.min))
                        then(nc.vector.reciprocal(scale[:, :], peak[:, :]))
                        then(nc.vector.tensor_scalar(scale[:, :], scale[:, :], 2.0 ** 14, None, ALU.mult))
                        then(nc.vector.tensor_scalar(scale[:, :].bitcast(i32), scale[:, :].bitcast(i32), 0x7F800000, None, ALU.bitwise_and))
                        then(nc.vector.reciprocal(unscale[:, :], scale[:, :]))
                        then(nc.vector.tensor_scalar(up_scale[:, :], scale[:, 1:2], 2.0 ** -29, None, ALU.mult))
                        then(nc.vector.tensor_scalar(y_scale[:, :], unscale[:, 1:2], unscale[:, 1:2], 2.0 ** 29, ALU.mult, ALU.mult))
                        then(nc.vector.tensor_scalar(y_scale[:, :], y_scale[:, :], unscale[:, 1:2], None, ALU.mult))
                        then(nc.vector.tensor_scalar(rope_sb[:, :, :], rope_sb[:, :, :], unscale[0:SEQ, 0:1], None, ALU.mult))
                        nc.vector.tensor_scalar(wqkv_hi[:, :, :], wqkv_sb[:, :, :], scale[:, 0:1], None, ALU.mult).then_inc(s["split_hi"], 1)
                        dve.wait_ge(s["split_hi"], 1)
                        nc.vector.scalar_tensor_tensor(out=wqkv_lo[:, :, :], in0=wqkv_sb[:, :, :], scalar=scale[:, 0:1], in1=wqkv_hi[:, :, :],
                                                       op0=ALU.mult, op1=ALU.subtract).then_inc(s["split_lo"], 1)
                        dve.wait_ge(s["split_lo"], 1)

                    @block.scalar
                    def _(act):
                        def step(i, par):
                            if live(i, par + 1):
                                n, q = 2 * i + par + 1, (par + 1) % 2
                                act.wait_ge(s["x_turned"], n + 1)
                                if later(i, par + 1):
                                    act.wait_ge(s["z_mm"], n - 1)
                                nc.scalar.activation(xcT[q][:, :].rearrange("p (a b) -> p a b", a=2),
                                                     quad[:, 2 * q:2 * q + 2, 0:384], ACT.Copy).then_inc(s["xT_ready"], 1)
                        pairs(act, step, -1, N)

                    @block.tensor
                    def _(pe):
                        pe.wait_ge(s["t_wide"], KT)
                        pe.wait_ge(s["t_const"], 80)
                        for k in range(KT):
                            last = nc.tensor.matmul(b4[:, 0:DIM], b1_wide[:, k, :], wp[:, k, :], start=(k == 0), stop=(k == KT - 1))
                        last.then_inc(s["t_bias_mm"], 1)
                        pe.wait_ge(s["t_wg"], KT)
                        pe.wait_ge(s["t_bias"], 1)

                        def step(i, par):
                            if live(i, par + 1):
                                n, q = 2 * i + par + 1, (par + 1) % 2
                                pe.wait_ge(s["xc_ready"], n + 1)
                                if later(i, par + 1):
                                    pe.wait_ge(s["xT_ready"], n - 1)
                                for k in range(KT):
                                    last = nc.tensor.transpose(quad[:, 2 * q + k // 3, (k % 3) * P:(k % 3 + 1) * P],
                                                               xc[q][:, k * P:(k + 1) * P], idt[:, :])
                                last.then_inc(s["x_turned"], 1)
                            if live(i, par):
                                n, q = 2 * i + par, par
                                pe.wait_ge(s["xT_ready"], n + 1)
                                if later(i, par):
                                    pe.wait_ge(s["z_ready"], n - 1)
                                for k in range(KT):
                                    last = nc.tensor.matmul(bank[q][:, 0:DIM], xcT[q][:, k * P:(k + 1) * P], wg[:, k, :],
                                                            start=(k == 0), stop=(k == KT - 1))
                                last.then_inc(s["z_mm"], 1)
                        pairs(pe, step, -1, N)

        def attention():
            with ExitStack() as st:
                def tb(name, shape, dt=fp32):
                    return st.enter_context(nc.sbuf_tensor(name, shape, dt))

                def ring(name, shape, dt=fp32):
                    return [tb(f"{name}{i}", shape, dt) for i in range(2)]

                tok, h, xn = ring("tok", [SEQ, DIM]), ring("h", [SEQ, DIM]), ring("xn", [SEQ, DIM])
                h_scaled = tb("h_scaled", [SEQ, DIM])
                stats, stats2 = tb("stats", [SEQ, 6]), tb("stats2", [SEQ, 6])
                mv, mv2 = ring("mv", [SEQ, 2]), ring("mv2", [SEQ, 2])
                ve, ve2 = tb("ve", [SEQ, 1]), tb("ve2", [SEQ, 1])
                rs, rs2 = ring("rs", [SEQ, 1]), ring("rs2", [SEQ, 1])
                x_hi, x_lo = ring("bx_hi", [P, KD, SEQ], fp16), ring("bx_lo", [P, KD, SEQ], fp16)
                xn2T = ring("xn2T", [P, KD, SEQ])
                rot = ring("rot", [SEQ, 2, 2 * DIM])
                qk = ring("qk", [SEQ, 2 * HEADS, PAD])
                q_h, k_h = ring("q_h", [P, CH, SEQ], fp16), ring("k_h", [P, CH, SEQ], fp16)
                kT = ring("kT", [P, CH, SEQ])
                qmT = ring("qmT", [P, CH, 4, SEQ])
                v = [tb(f"v{j}", [SEQ, HEADS, PAD]) for j in range(4)]
                probs = ring("probs", [SEQ, CH, 4, SEQ])
                oT = ring("oT", [P, CH, SEQ])
                denom = ring("denom", [SEQ, HEADS])
                att, h_back, h2, xn2 = ring("att", [SEQ, DIM]), ring("h_back", [SEQ, DIM]), ring("h2", [SEQ, DIM]), ring("xn2", [SEQ, DIM])
                w_raw = ring("w_raw", [P, W_CHUNK])

                names = """init tok_scaled h_ready stats_done mv_ready eps_added rstd_ready xn_ready xn_turned x_hi_ready x_lo_ready
                    qk_mm v_mm rot_mul qk_even qk_odd q_turned k_turned q_h_ready k_h_ready kT_ready v_ready s_mm max_ready qm_turned
                    qmT_ready st_mm probs_ready o_mm oT_ready o_turned denom_ready att_ready h2_ready stats2_done mv2_ready
                    eps2_added rstd2_ready xn2_ready xn2_turned xn2T_ready logits_mm logits_saved w_hi_ready w_lo_ready""".split()
                s = {n: sem("b_" + n) for n in names}
                tok_loaded = [sem(f"b_tok_loaded{i}") for i in range(2)]
                h_stored = [sem(f"b_h_stored{i}") for i in range(2)]
                h_loaded = [sem(f"b_h_loaded{i}") for i in range(2)]
                h2_stored = [sem(f"b_h2_stored{i}") for i in range(2)]
                xn2_stored = [sem(f"b_xn2_stored{i}") for i in range(2)]
                w_loaded = [sem(f"b_w_loaded{i}") for i in range(2)]
                INIT = 10

                N, UNROLL = BATCH, 4
                FIRST, LAST = 2, 15

                def steps(eng, step):
                    for t in range(-4, UNROLL * FIRST):
                        step(t // UNROLL, t % UNROLL)
                    with eng.Fori(FIRST, LAST) as i:
                        for u in range(UNROLL):
                            step(i, u)
                    for t in range(UNROLL * LAST, N + 5):
                        step(t // UNROLL, t % UNROLL)

                def part(i, off):
                    if isinstance(i, int):
                        b = UNROLL * i + off
                        return b, off % 2, 2 * i + off // 2, 0 <= b < N, lambda k: 0 <= b + k < N
                    return UNROLL * i + off, off % 2, 2 * i + off // 2, True, lambda k: True

                def rotary(eng, q, c):
                    cosines = rot[q][:, 0, :].rearrange("p (n d two) -> p n d two", d=8, two=2)
                    sines = rot[q][:, 1, :].rearrange("p (n d two) -> p n d two", d=8, two=2)
                    heads = qk[q][:, :, 0:HEAD_DIM].rearrange("p n (d two) -> p n d two", two=2)
                    return eng.tensor_tensor(heads[:, :, :, c], cosines[:, :, :, c], sines[:, :, :, 1 - c], ALU.add)

                with nc.Block() as block:
                    @block.sync
                    def _(sp):
                        sp.wait_ge(s["init"], INIT)

                        def step(i, u):
                            b, q, half, on, has = part(i, u - 3)
                            if on:
                                sp.wait_ge(h_stored[q], 16 * (half + 1))
                                sp.sem_inc(held["sp"], 1)
                                if has(-2):
                                    sp.wait_ge(s["h2_ready"], b - 1)
                                    sp.sem_inc(held["sp"], 1)
                                sp.dma_start(h_back[q][:, :], h_rows[bass.ds(b * SEQ, SEQ), :]).then_inc(h_loaded[q], 16)
                            b, q, half, on, has = part(i, u + 4)
                            if on:
                                if has(-2):
                                    sp.wait_ge(s["tok_scaled"], b - 1)
                                    sp.sem_inc(held["sp"], 1)
                                sp.dma_start(tok[q][1:1 + PATCHES, :], patch_rows[bass.ds(b * PATCHES, PATCHES), :]).then_inc(tok_loaded[q], 16)
                                sp.dma_start(tok[q][1 + PATCHES:SEQ, :], txt[bass.ds(b * TEXT, TEXT), :]).then_inc(tok_loaded[q], 16)
                            b, q, half, on, has = part(i, u + 1)
                            if on:
                                if has(-2):
                                    sp.wait_ge(s["w_lo_ready"], b - 1)
                                    sp.sem_inc(held["sp"], 1)
                                sp.dma_start(w_raw[q][:, :], experts_w[:, bass.ds(b * W_CHUNK, W_CHUNK)]).then_inc(w_loaded[q], 16)
                            b, q, half, on, has = part(i, u - 4)
                            if on:
                                sp.wait_ge(s["h2_ready"], b + 1)
                                sp.sem_inc(held["sp"], 1)
                                sp.dma_start(out[bass.ds(b * SEQ, SEQ), :], h2[q][:, :]).then_inc(h2_stored[q], 16)
                            b, q, half, on, has = part(i, u + 3)
                            if on:
                                sp.wait_ge(s["h_ready"], b + 1)
                                sp.sem_inc(held["sp"], 1)
                                sp.dma_start(h_rows[bass.ds(b * SEQ, SEQ), :], h[q][:, :]).then_inc(h_stored[q], 16)
                            b, q, half, on, has = part(i, u - 4)
                            if on:
                                sp.wait_ge(s["xn2_ready"], b + 1)
                                sp.sem_inc(held["sp"], 1)
                                sp.dma_start(xn_rows[bass.ds(b * SEQ, SEQ), 0:DIM], xn2[q][:, :]).then_inc(xn2_stored[q], 16)
                        steps(sp, step)
                        for par in range(2):
                            sp.wait_ge(h2_stored[par], 16 * (N // 2))
                            sp.wait_ge(xn2_stored[par], 16 * (N // 2))

                    @block.gpsimd
                    def _(pool):
                        for q in range(2):
                            nc.gpsimd.memset(tok[q][0:1, :], 0.0).then_inc(s["init"], 1)
                            nc.gpsimd.memset(qk[q][:, :, :], 0.0).then_inc(s["init"], 1)
                            nc.gpsimd.memset(qmT[q][:, :, :, :], 0.0).then_inc(s["init"], 1)
                        for j in range(4):
                            nc.gpsimd.memset(v[j][:, :, :], 0.0).then_inc(s["init"], 1)
                        pool.wait_ge(s["init"], INIT)
                        for q in range(2):
                            nc.gpsimd.memset(qk[q][:, HEADS:, HEAD_DIM:HEAD_DIM + 1], 1.0).then_inc(s["init"], 1)
                        for j in range(4):
                            nc.gpsimd.memset(v[j][:, :, HEAD_DIM:HEAD_DIM + 1], 1.0).then_inc(s["init"], 1)
                        pool.wait_ge(s["init"], INIT + 6)

                        def step(i, u):
                            b, q, half, on, has = part(i, u - 4)
                            if on:
                                pool.wait_ge(s["att_ready"], b + 1)
                                pool.wait_ge(h_loaded[q], 16 * (half + 1))
                                if has(-2):
                                    pool.wait_ge(s["xn2_ready"], b - 1)
                                    pool.wait_ge(h2_stored[q], 16 * half)
                                nc.gpsimd.tensor_tensor(h2[q][:, :], h_back[q][:, :], att[q][:, :], ALU.add).then_inc(s["h2_ready"], 1)
                            b, q, half, on, has = part(i, u + 2)
                            if on:
                                pool.wait_ge(s["mv_ready"], b + 1)
                                if has(-2):
                                    pool.wait_ge(s["xn_ready"], b - 1)
                                pool.sem_inc(held["pool"], 1)
                                nc.gpsimd.tensor_scalar(ve[:, :], mv[q][:, 1:2], EPS, None, ALU.add).then_inc(s["eps_added"], 1)
                                pool.wait_ge(s["eps_added"], b + 1)
                                nc.gpsimd.tensor_tensor(rs[q][:, :], ve[:, :], eps_pow[0:SEQ, :], ALU.pow).then_inc(s["rstd_ready"], 1)
                            b, q, half, on, has = part(i, u - 4)
                            if on:
                                pool.wait_ge(s["mv2_ready"], b + 1)
                                pool.sem_inc(held["pool"], 1)
                                nc.gpsimd.tensor_scalar(ve2[:, :], mv2[q][:, 1:2], EPS, None, ALU.add).then_inc(s["eps2_added"], 1)
                                pool.wait_ge(s["eps2_added"], b + 1)
                                nc.gpsimd.tensor_tensor(rs2[q][:, :], ve2[:, :], eps_pow[0:SEQ, :], ALU.pow).then_inc(s["rstd2_ready"], 1)
                            b, q, half, on, has = part(i, u + 3)
                            if on:
                                pool.wait_ge(tok_loaded[q], 32 * (half + 1))
                                if has(-1):
                                    pool.wait_ge(s["h_ready"], b)
                                nc.gpsimd.tensor_tensor(h_scaled[:, :], tok[q][:, :], scale_rows[:, :], ALU.mult).then_inc(s["tok_scaled"], 1)
                                pool.wait_ge(s["tok_scaled"], b + 1)
                                if has(-2):
                                    pool.wait_ge(s["xn_ready"], b - 1)
                                    pool.wait_ge(h_stored[q], 16 * half)
                                nc.gpsimd.tensor_tensor(h[q][:, :], h_scaled[:, :], shift_rows[:, :], ALU.add).then_inc(s["h_ready"], 1)
                            b, q, half, on, has = part(i, u)
                            if on:
                                pool.wait_ge(s["rot_mul"], b + 1)
                                if has(-2):
                                    pool.wait_ge(s["qm_turned"], b - 1)
                                rotary(nc.gpsimd, q, 1).then_inc(s["qk_odd"], 1)
                        steps(pool, step)

                    @block.vector
                    def _(dve):
                        def step(i, u):
                            b, q, half, on, has = part(i, u + 2)
                            if on:
                                dve.wait_ge(s["h_ready"], b + 1)
                                if has(-1):
                                    dve.wait_ge(s["mv_ready"], b)
                                nc.vector.bn_stats(stats[:, :], h[q][:, :]).then_inc(s["stats_done"], 1)
                                dve.wait_ge(s["stats_done"], b + 1)
                                dve.sem_inc(held["dve"], 1)
                                nc.vector.bn_aggr(mv[q][:, :], stats[:, :]).then_inc(s["mv_ready"], 1)
                            b, q, half, on, has = part(i, u - 4)
                            if on:
                                dve.wait_ge(s["h2_ready"], b + 1)
                                if has(-1):
                                    dve.wait_ge(s["mv2_ready"], b)
                                nc.vector.bn_stats(stats2[:, :], h2[q][:, :]).then_inc(s["stats2_done"], 1)
                                dve.wait_ge(s["stats2_done"], b + 1)
                                dve.sem_inc(held["dve"], 1)
                                nc.vector.bn_aggr(mv2[q][:, :], stats2[:, :]).then_inc(s["mv2_ready"], 1)
                            b, q, half, on, has = part(i, u - 1)
                            if on:
                                dve.wait_ge(s["s_mm"], b + 1)
                                nc.vector.tensor_reduce(qk[q][:, 0:HEADS, HEAD_DIM].rearrange("p (c g) -> p g c", g=4),
                                                        quad[0:SEQ, :, 0:CH * SEQ].rearrange("p g (c k) -> p g c k", k=SEQ),
                                                        AX.X, ALU.max, negate=True).then_inc(s["max_ready"], 1)
                            b, q, half, on, has = part(i, u)
                            if on:
                                dve.wait_ge(s["qk_mm"], b + 1)
                                if has(-2):
                                    dve.wait_ge(s["qk_odd"], b - 1)
                                    dve.wait_ge(s["qk_even"], b - 1)
                                nc.vector.tensor_tensor(rot[q][:, :, :], b4[0:SEQ, None, :].broadcast_to([SEQ, 2, 2 * DIM]),
                                                        rope_sb[:, :, :], ALU.mult).then_inc(s["rot_mul"], 1)
                                dve.wait_ge(s["rot_mul"], b + 1)
                                if has(-2):
                                    dve.wait_ge(s["qm_turned"], b - 1)
                                rotary(nc.vector, q, 0).then_inc(s["qk_even"], 1)
                            b, q, half, on, has = part(i, u + 1)
                            if on:
                                dve.wait_ge(s["x_hi_ready"], b + 1)
                                if has(-6):
                                    dve.wait_ge(s["xn2T_ready"], b - 5)
                                if has(-2):
                                    dve.wait_ge(s["v_mm"], b - 1)
                                    dve.wait_ge(s["qk_mm"], b - 1)
                                nc.vector.tensor_tensor(x_lo[q][:, :, :], b7[:, 0:KD * SEQ].rearrange("p (c n) -> p c n", c=KD), x_hi[q][:, :, :],
                                                        ALU.subtract).then_inc(s["x_lo_ready"], 1)
                            b, q, half, on, has = part(i, u + 2)
                            if on:
                                dve.wait_ge(s["rstd_ready"], b + 1)
                                dve.wait_ge(s["mv_ready"], b + 1)
                                if has(-2):
                                    dve.wait_ge(s["xn_turned"], b - 1)
                                nc.vector.tensor_scalar(xn[q][:, :], h[q][:, :], mv[q][:, 0:1], rs[q][:, :],
                                                        ALU.subtract, ALU.mult).then_inc(s["xn_ready"], 1)
                            b, q, half, on, has = part(i, u - 4)
                            if on:
                                dve.wait_ge(s["rstd2_ready"], b + 1)
                                dve.wait_ge(s["mv2_ready"], b + 1)
                                if has(-2):
                                    dve.wait_ge(s["xn2_turned"], b - 1)
                                    dve.wait_ge(xn2_stored[q], 16 * half)
                                nc.vector.tensor_scalar(xn2[q][:, :], h2[q][:, :], mv2[q][:, 0:1], rs2[q][:, :],
                                                        ALU.subtract, ALU.mult).then_inc(s["xn2_ready"], 1)
                            b, q, half, on, has = part(i, u - 3)
                            if on:
                                dve.wait_ge(s["o_turned"], b + 1)
                                o = b4[0:SEQ, :].rearrange("p (n d) -> p n d", d=PAD)
                                if has(-2):
                                    dve.wait_ge(s["h2_ready"], b - 1)
                                nc.vector.reciprocal(denom[q][:, :], o[:, :, HEAD_DIM]).then_inc(s["denom_ready"], 1)
                                dve.wait_ge(s["denom_ready"], b + 1)
                                nc.vector.tensor_tensor(att[q][:, :].rearrange("p (n d) -> p n d", d=HEAD_DIM), o[:, :, 0:HEAD_DIM],
                                                        denom[q][:, :, None].broadcast_to([SEQ, HEADS, HEAD_DIM]), ALU.mult).then_inc(s["att_ready"], 1)
                            b, q, half, on, has = part(i, u)
                            if on:
                                dve.wait_ge(w_loaded[q], 16 * (half + 1))
                                dve.wait_ge(s["w_hi_ready"], b + 1)
                                nc.vector.scalar_tensor_tensor(out=w_lo[:, bass.ds(b * W_CHUNK, W_CHUNK)], in0=w_raw[q][:, :], scalar=scale[:, 1:2],
                                                               in1=w_hi[:, bass.ds(b * W_CHUNK, W_CHUNK)], op0=ALU.mult,
                                                               op1=ALU.subtract).then_inc(s["w_lo_ready"], 1)
                        steps(dve, step)

                    @block.scalar
                    def _(act):
                        def evac(dst, src, signal, **kw):
                            nc.scalar.activation(dst, src, ACT.Copy, **kw).then_inc(signal, 1)

                        def chunks(ap, n):
                            return ap.rearrange("p (c n) -> p c n", c=n)

                        def step(i, u):
                            b, q, half, on, has = part(i, u - 1)
                            if on:
                                act.wait_ge(s["q_turned"], b + 1)
                                if has(-2):
                                    act.wait_ge(s["s_mm"], b - 1)
                                evac(q_h[q][:, :, :], chunks(b6[:, 0:CH * SEQ], CH), s["q_h_ready"])
                                act.wait_ge(s["k_turned"], b + 1)
                                evac(k_h[q][:, :, :], chunks(b7[:, 0:CH * SEQ], CH), s["k_h_ready"])
                                if has(-2):
                                    act.wait_ge(s["st_mm"], b - 1)
                                evac(kT[q][:, :, :], chunks(b7[:, 0:CH * SEQ], CH), s["kT_ready"])
                            b, q, half, on, has = part(i, u)
                            if on:
                                act.wait_ge(w_loaded[q], 16 * (half + 1))
                                evac(w_hi[:, bass.ds(b * W_CHUNK, W_CHUNK)], w_raw[q][:, :], s["w_hi_ready"], scale=scale[:, 1:2])
                            b, q, half, on, has = part(i, u + 1)
                            if on:
                                act.wait_ge(s["xn_turned"], b + 1)
                                if has(-6):
                                    act.wait_ge(s["xn2_turned"], b - 5)
                                if has(-2):
                                    act.wait_ge(s["v_mm"], b - 1)
                                    act.wait_ge(s["qk_mm"], b - 1)
                                evac(x_hi[q][:, :, :], chunks(b7[:, 0:KD * SEQ], KD), s["x_hi_ready"])
                            b, q, half, on, has = part(i, u - 5)
                            if on:
                                act.wait_ge(s["xn2_turned"], b + 1)
                                if has(-2):
                                    act.wait_ge(s["logits_mm"], b - 1)
                                evac(xn2T[q][:, :, :], chunks(b7[:, KD * SEQ:2 * KD * SEQ], KD), s["xn2T_ready"])
                            b, q, half, on, has = part(i, u)
                            if on:
                                act.wait_ge(s["v_mm"], b + 1)
                                if has(-5):
                                    act.wait_ge(s["logits_mm"], b - 4)
                                if has(-4):
                                    act.wait_ge(s["o_mm"], b - 3)
                                evac(v[u % 4][:, :, 0:HEAD_DIM], b5[0:SEQ, 0:DIM].rearrange("p (n d) -> p n d", d=HEAD_DIM), s["v_ready"],
                                     scale=unscale[0:SEQ, 0:1])
                            b, q, half, on, has = part(i, u - 5)
                            if on:
                                act.wait_ge(s["logits_mm"], b + 1)
                                evac(logits[:, :, :].rearrange("p b e -> p (b e)")[:, bass.ds(b * EXPERTS, EXPERTS)],
                                     b5[0:SEQ, DIM:DIM + EXPERTS], s["logits_saved"])
                            b, q, half, on, has = part(i, u - 3)
                            if on:
                                act.wait_ge(s["o_mm"], b + 1)
                                if has(-2):
                                    act.wait_ge(s["o_turned"], b - 1)
                                evac(oT[q][:, :, :], chunks(b6[:, 0:CH * SEQ], CH), s["oT_ready"])
                            b, q, half, on, has = part(i, u - 1)
                            if on:
                                act.wait_ge(s["qm_turned"], b + 1)
                                if has(-2):
                                    act.wait_ge(s["st_mm"], b - 1)
                                for g in range(4):
                                    rows = slice(PAD * g, PAD * (g + 1))
                                    evac(qmT[q][rows, :, g, :], chunks(b5[rows, 0:CH * SEQ], CH), s["qmT_ready"])
                            b, q, half, on, has = part(i, u - 2)
                            if on:
                                act.wait_ge(s["st_mm"], b + 1)
                                if has(-2):
                                    act.wait_ge(s["o_mm"], b - 1)
                                nc.scalar.activation(probs[q][:, :, :, :].rearrange("p c g n -> p c (g n)"), quad[0:SEQ, :, 0:4 * SEQ],
                                                     ACT.Exp, scale=HEAD_DIM ** -0.5).then_inc(s["probs_ready"], 1)
                        steps(act, step)

                    @block.tensor
                    def _(pe):
                        def turn(dst, src, n, rows, signal):
                            for c in range(n):
                                last = nc.tensor.transpose(dst[:, c * rows:(c + 1) * rows], src[:, c * P:(c + 1) * P], idt[0:rows, 0:rows])
                            last.then_inc(signal, 1)

                        def project(dst, q, cols):
                            for k in range(KD):
                                for m, (x, w) in enumerate(((x_hi, wqkv_hi), (x_hi, wqkv_lo), (x_lo, wqkv_hi))):
                                    last = nc.tensor.matmul(dst, x[q][:, k, :], w[:, k, cols], start=(k == 0 and m == 0), stop=(k == KD - 1 and m == 2))
                            return last

                        def scores(q, c):
                            return nc.tensor.matmul(quad[0:SEQ, c, 0:4 * SEQ], kT[q][:, c, :],
                                                    qmT[q][:, c, :, :].rearrange("p g n -> p (g n)"), start=True, stop=True)

                        def step(i, u):
                            b, q, half, on, has = part(i, u - 1)
                            if on:
                                pe.wait_ge(s["qk_even"], b + 1)
                                pe.wait_ge(s["qk_odd"], b + 1)
                                if has(-3):
                                    pe.wait_ge(s["oT_ready"], b - 2)
                                flat = qk[q][:, :, :].rearrange("p n d -> p (n d)")
                                turn(b6, flat[:, 0:HEADS * PAD], CH, SEQ, s["q_turned"])
                                if has(1):
                                    pe.wait_ge(s["x_lo_ready"], b + 2)
                                if has(-5):
                                    pe.wait_ge(s["xn2T_ready"], b - 4)
                                turn(b7, flat[:, HEADS * PAD:], CH, SEQ, s["k_turned"])
                            b, q, half, on, has = part(i, u)
                            if on:
                                pe.wait_ge(s["x_hi_ready"], b + 1)
                                pe.wait_ge(s["x_lo_ready"], b + 1)
                                if has(-4):
                                    pe.wait_ge(s["att_ready"], b - 3)
                                project(b4[0:SEQ, :], q, slice(0, 2 * DIM)).then_inc(s["qk_mm"], 1)
                            b, q, half, on, has = part(i, u - 1)
                            if on:
                                pe.wait_ge(s["q_h_ready"], b + 1)
                                pe.wait_ge(s["k_h_ready"], b + 1)
                                if has(-2):
                                    pe.wait_ge(s["probs_ready"], b - 1)
                                for c in range(CH):
                                    for g in range(4):
                                        rows = slice(PAD * g, PAD * g + HEAD_DIM)
                                        last = nc.tensor.matmul(quad[0:SEQ, g, c * SEQ:(c + 1) * SEQ], q_h[q][rows, c, :], k_h[q][rows, c, :],
                                                                start=True, stop=True)
                                last.then_inc(s["s_mm"], 1)
                            b, q, half, on, has = part(i, u + 1)
                            if on:
                                pe.wait_ge(s["xn_ready"], b + 1)
                                if has(-2):
                                    pe.wait_ge(s["kT_ready"], b - 1)
                                turn(b7, xn[q], KD, SEQ, s["xn_turned"])
                            b, q, half, on, has = part(i, u - 5)
                            if on:
                                pe.wait_ge(s["xn2_ready"], b + 1)
                                if has(4):
                                    pe.wait_ge(s["kT_ready"], b + 5)
                                if has(-1):
                                    pe.wait_ge(s["xn2T_ready"], b)
                                turn(b7[:, KD * SEQ:], xn2[q], KD, SEQ, s["xn2_turned"])
                            b, q, half, on, has = part(i, u)
                            if on:
                                if has(-2):
                                    pe.wait_ge(s["qmT_ready"], 4 * (b - 1))
                                project(b5[0:SEQ, 0:DIM], q, slice(2 * DIM, 3 * DIM)).then_inc(s["v_mm"], 1)
                            b, q, half, on, has = part(i, u - 5)
                            if on:
                                pe.wait_ge(s["xn2T_ready"], b + 1)
                                if has(3):
                                    pe.wait_ge(s["qmT_ready"], 4 * (b + 4))
                                if has(-1):
                                    pe.wait_ge(s["logits_saved"], b)
                                for k in range(KD):
                                    last = nc.tensor.matmul(b5[0:SEQ, DIM:DIM + EXPERTS], xn2T[q][:, k, :], router_sb[:, k, :], start=(k == 0), stop=(k == KD - 1))
                                last.then_inc(s["logits_mm"], 1)
                            b, q, half, on, has = part(i, u - 3)
                            if on:
                                pe.wait_ge(s["probs_ready"], b + 1)
                                pe.wait_ge(s["v_ready"], b + 1)
                                if has(2):
                                    pe.wait_ge(s["q_h_ready"], b + 3)
                                for c in range(CH):
                                    for g in range(4):
                                        last = nc.tensor.matmul(b6[PAD * g:PAD * (g + 1), c * SEQ:(c + 1) * SEQ], v[(u - 3) % 4][:, 4 * c + g, :], probs[q][:, c, g, :],
                                                                start=True, stop=True)
                                last.then_inc(s["o_mm"], 1)
                            b, q, half, on, has = part(i, u - 1)
                            if on:
                                pe.wait_ge(s["max_ready"], b + 1)
                                if has(1):
                                    pe.wait_ge(s["v_ready"], b + 2)
                                if has(-4):
                                    pe.wait_ge(s["logits_saved"], b - 3)
                                turn(b5, qk[q][:, :, :].rearrange("p n d -> p (n d)")[:, 0:HEADS * PAD], CH, SEQ, s["qm_turned"])
                            b, q, half, on, has = part(i, u - 2)
                            if on:
                                pe.wait_ge(s["qmT_ready"], 4 * (b + 1))
                                pe.wait_ge(s["kT_ready"], b + 1)
                                if has(1):
                                    pe.wait_ge(s["max_ready"], b + 2)
                                for c in range(CH // 2):
                                    scores(q, c)
                            b, q, half, on, has = part(i, u - 3)
                            if on:
                                pe.wait_ge(s["oT_ready"], b + 1)
                                if has(3):
                                    pe.wait_ge(s["rot_mul"], b + 4)
                                if has(-1):
                                    pe.wait_ge(s["att_ready"], b)
                                for c in range(CH):
                                    last = nc.tensor.transpose(b4[0:SEQ, c * P:(c + 1) * P], oT[q][:, c, :], idt[:, :])
                                last.then_inc(s["o_turned"], 1)
                            b, q, half, on, has = part(i, u - 2)
                            if on:
                                for c in range(CH // 2, CH):
                                    last = scores(q, c)
                                last.then_inc(s["st_mm"], 1)
                        steps(pe, step)

        def routing():
            with ExitStack() as st:
                def tb(name, shape, dt=fp32):
                    return st.enter_context(nc.sbuf_tensor(name, shape, dt))

                BE = [SEQ, BATCH, EXPERTS]
                rev = tb("rev", [P, EXPERTS])
                lanes = tb("lanes", [P, P])
                places = tb("places", [P, TILES_MOE])
                id_part = tb("id_part", [P, BATCH])
                spare_id = tb("spare_id", [P, 1])
                best, second = tb("best", [SEQ, BATCH]), tb("second", [SEQ, BATCH])
                hit, key, rest = tb("hit", BE), tb("key", BE), tb("rest", BE)
                key_max = tb("key_max", [SEQ, BATCH])
                pick = [tb(f"pick{j}", BE) for j in range(2)]
                both, before = tb("both", BE), tb("before", BE)
                total = tb("total", [P, BATCH, EXPERTS])
                scan = [tb(f"scan{j}", [P, BATCH, EXPERTS]) for j in range(2)]
                count_i, tiles_f = tb("count_i", [P, EXPERTS], i32), tb("tiles_f", [P, EXPERTS])
                tile_end = tb("tile_end", [P, EXPERTS + 1])
                first_slot = tb("first_slot", [P, EXPERTS])
                passed = tb("passed", [P, TILES_MOE, EXPERTS])
                expert_f = tb("expert_f", [P, TILES_MOE])
                slot_f = [tb(f"slot_f{j}", [SEQ, BATCH]) for j in range(2)]
                slot_i = [tb(f"slot_i{j}", [SEQ, BATCH], i32) for j in range(2)]
                tile_i, lane_i = tb("tile_i", [SEQ, BATCH], i32), tb("lane_i", [SEQ, BATCH], i32)
                tile_f = [tb(f"tile_f{j}", [SEQ, BATCH]) for j in range(2)]
                lane_f = [tb(f"lane_f{j}", [SEQ, BATCH]) for j in range(2)]
                gap, gate = tb("gap", [SEQ, BATCH]), [tb(f"gate{j}", [SEQ, BATCH]) for j in range(2)]
                field = [tb(f"field{j}", [SEQ, BATCH]) for j in range(2)]
                lanes_h, places_h = tb("lanes_h", [P, P], bf16), tb("places_h", [P, TILES_MOE], bf16)
                at_lane = [tb(f"at_lane{j}", [SEQ, P], bf16) for j in range(4)]
                at_tile = [tb(f"at_tile{j}", [SEQ, 2, TILES_MOE], bf16) for j in range(4)]
                experts_row = tb("experts_row", [P, EXPERTS])
                weights = tb("weights", BE)
                batch_less = tb("batch_less", [P, BATCH])
                tok_f = tb("tok_f", [P, TILES_MOE])
                weights_stored = sem("c_weights_stored")
                weights_ready = sem("c_weights_ready")
                step_done, counted, consts, exp_in, exp_out, spread, placed = (sem("c_" + n) for n in
                    ("step_done", "counted", "consts", "exp_in", "exp_out", "spread", "placed"))

                with nc.Block() as block:
                    @block.gpsimd
                    def _(pool):
                        i_ = dict(allow_small_or_imprecise_dtypes=True)
                        nc.gpsimd.iota(rev[:, :], [[-1, EXPERTS]], base=EXPERTS, channel_multiplier=0, **i_).then_inc(consts, 1)
                        nc.gpsimd.iota(lanes[:, :], [[1, P]], base=0, channel_multiplier=0, **i_).then_inc(consts, 1)
                        nc.gpsimd.iota(places[:, :], [[1, TILES_MOE]], base=0, channel_multiplier=0, **i_).then_inc(consts, 1)
                        nc.gpsimd.iota(id_part[:, :], [[0, BATCH]], base=0, channel_multiplier=1, **i_).then_inc(consts, 1)
                        nc.gpsimd.iota(experts_row[:, :], [[1, EXPERTS]], base=0, channel_multiplier=0, **i_).then_inc(consts, 1)
                        nc.gpsimd.iota(batch_less[:, :], [[1, BATCH]], base=-BATCH, channel_multiplier=0, **i_).then_inc(consts, 1)
                        nc.gpsimd.iota(spare_id[:, :], [[0, 1]], base=TOKENS, channel_multiplier=1, **i_).then_inc(consts, 1)

                    @block.vector
                    def _(dve):
                        done = [0]

                        def then(ins):
                            done[0] += 1
                            ins.then_inc(step_done, 1)
                            dve.wait_ge(step_done, done[0])

                        def per_token(ap):
                            return ap[:, :, None].broadcast_to(BE)

                        dve.wait_ge(consts, 7)
                        revb = rev[0:SEQ, None, :].broadcast_to(BE)
                        for j, (src, top) in enumerate(((logits, best), (rest, second))):
                            then(nc.vector.tensor_reduce(top[:, :], src[:, :, :], AX.X, ALU.max))
                            then(nc.vector.tensor_tensor(hit[:, :, :], src[:, :, :], per_token(top), ALU.is_equal))
                            then(nc.vector.tensor_tensor(key[:, :, :], hit[:, :, :], revb, ALU.mult))
                            then(nc.vector.tensor_reduce(key_max[:, :], key[:, :, :], AX.X, ALU.max))
                            then(nc.vector.tensor_tensor(pick[j][:, :, :], revb, per_token(key_max), ALU.is_equal))
                            if j == 0:
                                then(nc.vector.scalar_tensor_tensor(out=rest[:, :, :], in0=pick[0][:, :, :], scalar=-3.0e38,
                                                                    in1=logits[:, :, :], op0=ALU.mult, op1=ALU.add))
                        nc.vector.tensor_tensor(gap[:, :], second[:, :], best[:, :], ALU.subtract).then_inc(exp_in, 1)
                        then(nc.vector.tensor_tensor(both[:, :, :], pick[0][:, :, :], pick[1][:, :, :], ALU.add))
                        dve.wait_ge(exp_out, 1)
                        then(nc.vector.tensor_scalar(key_max[:, :], gap[:, :], 1.0, None, ALU.add))
                        then(nc.vector.reciprocal(gate[0][:, :], key_max[:, :]))
                        then(nc.vector.tensor_tensor(gate[1][:, :], gate[0][:, :], gap[:, :], ALU.mult))
                        then(nc.vector.tensor_tensor(key[:, :, :], pick[0][:, :, :], per_token(gate[0]), ALU.mult))
                        then(nc.vector.tensor_tensor(weights[:, :, :], pick[1][:, :, :], per_token(gate[1]), ALU.mult))
                        nc.vector.tensor_tensor(weights[:, :, :], weights[:, :, :], key[:, :, :], ALU.add).then_inc(weights_ready, 1)
                        dve.wait_ge(counted, 2)
                        then(nc.vector.tensor_copy(before[:, :, :], b4[0:SEQ, :].rearrange("p (b e) -> p b e", e=EXPERTS)))
                        then(nc.vector.tensor_copy(total[:, :, :], b5[:, :].rearrange("p (b e) -> p b e", e=EXPERTS)))
                        src, k, turn = total, 1, 0
                        while k < BATCH:
                            dst = scan[turn]
                            then(nc.vector.tensor_copy(dst[:, 0:k, :], src[:, 0:k, :]))
                            then(nc.vector.tensor_tensor(dst[:, k:, :], src[:, k:, :], src[:, 0:BATCH - k, :], ALU.add))
                            src, k, turn = dst, 2 * k, 1 - turn
                        running = src
                        then(nc.vector.tensor_scalar(count_i[:, :], running[:, BATCH - 1, :], float(P - 1), None, ALU.add))
                        then(nc.vector.tensor_scalar(count_i[:, :], count_i[:, :], 7, None, ALU.arith_shift_right))
                        then(nc.vector.tensor_copy(tiles_f[:, :], count_i[:, :]))
                        then(nc.vector.memset(tile_end[:, :], 0.0))
                        for e in range(EXPERTS):
                            then(nc.vector.tensor_tensor(tile_end[:, e + 1:e + 2], tile_end[:, e:e + 1], tiles_f[:, e:e + 1], ALU.add))
                        then(nc.vector.tensor_scalar(first_slot[:, :], tile_end[:, 0:EXPERTS], float(P), None, ALU.mult))
                        TE = [P, TILES_MOE, EXPERTS]
                        then(nc.vector.tensor_tensor(passed[:, :, :], places[:, :, None].broadcast_to(TE),
                                                     tile_end[:, None, 1:].broadcast_to(TE), ALU.is_ge))
                        then(nc.vector.tensor_reduce(expert_f[:, :], passed[:, :, :], AX.X, ALU.add))
                        then(nc.vector.tensor_scalar(expert_f[:, :], expert_f[:, :], float(EXPERTS - 1), None, ALU.min))
                        then(nc.vector.tensor_tensor(is_expert[:, :, :], expert_f[:, :, None].broadcast_to(TE),
                                                     experts_row[:, None, :].broadcast_to(TE), ALU.is_equal))
                        then(nc.vector.tensor_scalar(is_expert[:, :, :], is_expert[:, :, :], y_scale[:, :], None, ALU.mult))
                        then(nc.vector.tensor_scalar(expert_of[:, :], expert_f[:, :], float(EXPERTS - 1), None, ALU.min))
                        then(nc.vector.tensor_tensor(before[:, :, :], before[:, :, :], running[0:SEQ, :, :], ALU.add))
                        then(nc.vector.tensor_tensor(before[:, :, :], before[:, :, :], total[0:SEQ, :, :], ALU.subtract))
                        then(nc.vector.tensor_tensor(before[:, :, :], before[:, :, :], first_slot[0:SEQ, None, :].broadcast_to(BE), ALU.add))
                        for j in range(2):
                            then(nc.vector.tensor_tensor(key[:, :, :], before[:, :, :], pick[j][:, :, :], ALU.mult))
                            then(nc.vector.tensor_reduce(slot_f[j][:, :], key[:, :, :], AX.X, ALU.add))
                            then(nc.vector.tensor_copy(slot_i[j][:, :], slot_f[j][:, :]))
                            then(nc.vector.tensor_scalar(tile_i[:, :], slot_i[j][:, :], 7, None, ALU.arith_shift_right))
                            then(nc.vector.tensor_scalar(lane_i[:, :], slot_i[j][:, :], P - 1, None, ALU.bitwise_and))
                            then(nc.vector.tensor_copy(tile_f[j][:, :], tile_i[:, :]))
                            then(nc.vector.tensor_copy(lane_f[j][:, :], lane_i[:, :]))
                            then(nc.vector.tensor_tensor(field[j][:, :], id_part[0:SEQ, :], lane_f[j][:, :], ALU.subtract))
                        then(nc.vector.tensor_copy(lanes_h[:, :], lanes[:, :]))
                        then(nc.vector.tensor_copy(places_h[:, :], places[:, :]))
                        n = 0
                        for b in range(BATCH):
                            for j in range(2):
                                q = n % 4
                                if n >= 4:
                                    dve.wait_ge(placed, n - 3)
                                nc.vector.tensor_scalar(at_lane[q][:, :], lanes_h[0:SEQ, :], lane_f[j][:, b:b + 1], None, ALU.is_equal).then_inc(spread, 1)
                                for f, val in enumerate((field[j], batch_less)):
                                    nc.vector.tensor_scalar(at_tile[q][:, f, :], places_h[0:SEQ, :], tile_f[j][:, b:b + 1], val[0:SEQ, b:b + 1],
                                                            ALU.is_equal, ALU.mult).then_inc(spread, 1)
                                n += 1
                        dve.wait_ge(placed, n)
                        then(nc.vector.tensor_scalar(tok_f[:, :], b6[:, TILES_MOE:2 * TILES_MOE], float(SEQ), spare_id[:, :], ALU.mult, ALU.add))
                        then(nc.vector.tensor_tensor(token_of[:, :], b6[:, 0:TILES_MOE], tok_f[:, :], ALU.add))

                    @block.sync
                    def _(sp):
                        sp.wait_ge(weights_ready, 1)
                        sp.dma_start(xn_rows[0:TOKENS, DIM:].rearrange("(b p) e -> p b e", p=SEQ), weights[:, :, :]).then_inc(weights_stored, 16)
                        sp.wait_ge(weights_stored, 16)

                    @block.scalar
                    def _(act):
                        act.wait_ge(exp_in, 1)
                        nc.scalar.activation(gap[:, :], gap[:, :], ACT.Exp).then_inc(exp_out, 1)

                    @block.tensor
                    def _(pe):
                        pe.wait_ge(step_done, 12)
                        flat = both[:, :, :].rearrange("p b e -> p (b e)")
                        nc.tensor.matmul(b4[0:SEQ, :], prefix_sb[:, :], flat, start=True, stop=True).then_inc(counted, 1)
                        nc.tensor.matmul(b5[:, :], ones[0:SEQ, :], flat, start=True, stop=True).then_inc(counted, 1)
                        N = 2 * BATCH
                        for n in range(N):
                            pe.wait_ge(spread, 3 * (n + 1))
                            nc.tensor.matmul(b6[:, 0:2 * TILES_MOE], at_lane[n % 4][:, :], at_tile[n % 4][:, :, :].rearrange("p f t -> p (f t)"),
                                             start=(n == 0), stop=(n == N - 1)).then_inc(placed, 1)

        def experts():
            with ExitStack() as st:
                def tb(name, shape, dt=fp32):
                    return st.enter_context(nc.sbuf_tensor(name, shape, dt))

                def ring(name, shape, dt=fp32):
                    return [tb(f"{name}{i}", shape, dt) for i in range(2)]

                idx, idx_out = ring("idx", [P, 1], i32), ring("idx_out", [P, 1], i32)
                xg = ring("xg", [P, DIM + EXPERTS])
                x_hi, x_lo = ring("x_hi", [P, KD, P], fp16), ring("x_lo", [P, KD, P], fp16)
                silu, hid, y = ring("silu", [P, HIDDEN]), ring("hid", [P, HIDDEN]), ring("y", [P, DIM])
                hid_hi, hid_lo = ring("hid_hi", [P, KH, P], fp16), ring("hid_lo", [P, KH, P], fp16)
                own, weight = tb("own", [P, EXPERTS]), ring("weight", [P, 1])
                names = """idx_ready idx_out_ready x_turned x_hi_ready x_lo_ready gate_mm up_mm silu_ready hid_ready
                    hid_turned hid_hi_ready hid_lo_ready y_mm y_ready own_ready weight_ready""".split()
                s = {n: sem("d_" + n) for n in names}
                gathered = [sem(f"d_gathered{i}") for i in range(2)]
                added = sem("d_added")
                N = TILES_MOE
                FIRST, LAST = 2, N // 2 - 1

                def pairs(eng, step, lo, hi):
                    for t in range(lo, 2 * FIRST):
                        step(t // 2, t % 2)
                    with eng.Fori(FIRST, LAST) as i:
                        for par in range(2):
                            step(i, par)
                    for t in range(2 * LAST, hi):
                        step(t // 2, t % 2)

                def part(i, off):
                    if isinstance(i, int):
                        n = 2 * i + off
                        return n, off % 2, i + off // 2, 0 <= n < N, lambda k: 0 <= n + k < N
                    return 2 * i + off, off % 2, i + off // 2, True, lambda k: True

                with nc.Block() as block:
                    @block.gpsimd
                    def _(pool):
                        def step(i, par):
                            n, q, half, on, has = part(i, par + 2)
                            if on:
                                if has(-2):
                                    pool.wait_ge(gathered[q], 16 * half)
                                    pool.wait_ge(s["x_turned"], n - 1)
                                    pool.wait_ge(s["own_ready"], n - 1)
                                pool.sem_inc(held["pool"], 1)
                                nc.gpsimd.tensor_copy(idx[q][:, :], token_of[:, bass.ds(n, 1)]).then_inc(s["idx_ready"], 1)
                                pool.wait_ge(s["idx_ready"], n + 1)
                                pool.sem_inc(held["pool"], 1)
                                nc.gpsimd.indirect_dma_start(xg[q][:, :], None, xn_rows, bass.IndirectOffsetOnAxis(idx[q][:, :], 0)).then_inc(gathered[q], 16)
                            n, q, half, on, has = part(i, par - 1)
                            if on:
                                if has(-1):
                                    pool.wait_ge(added, 16 * n)
                                pool.sem_inc(held["pool"], 1)
                                nc.gpsimd.tensor_copy(idx_out[q][:, :], token_of[:, bass.ds(n, 1)]).then_inc(s["idx_out_ready"], 1)
                                pool.wait_ge(s["idx_out_ready"], n + 1)
                                pool.wait_ge(s["y_ready"], n + 1)
                                pool.sem_inc(held["pool"], 1)
                                nc.gpsimd.indirect_dma_start(out, bass.IndirectOffsetOnAxis(idx_out[q][:, :], 0), y[q][:, :], None,
                                                             compute_op=ALU.add).then_inc(added, 16)
                        pairs(pool, step, -2, N + 1)
                        pool.wait_ge(added, 16 * N)

                    @block.scalar
                    def _(act):
                        def step(i, par):
                            n, q, half, on, has = part(i, par)
                            if on:
                                act.wait_ge(s["gate_mm"], n + 1)
                                if has(-2):
                                    act.wait_ge(s["hid_ready"], n - 1)
                                nc.scalar.activation(silu[q][:, :], quad[:, 2 * q, :], ACT.Silu, scale=unscale[:, 1:2]).then_inc(s["silu_ready"], 1)
                            n, q, half, on, has = part(i, par - 1)
                            if on:
                                act.wait_ge(s["hid_turned"], n + 1)
                                if has(-2):
                                    act.wait_ge(s["y_mm"], n - 1)
                                nc.scalar.activation(hid_hi[q][:, :, :].rearrange("p c n -> p (c n)"), b4[:, :], ACT.Copy).then_inc(s["hid_hi_ready"], 1)
                            n, q, half, on, has = part(i, par + 1)
                            if on:
                                act.wait_ge(s["x_turned"], n + 1)
                                if has(-2):
                                    act.wait_ge(s["up_mm"], n - 1)
                                nc.scalar.activation(x_hi[q][:, :, :].rearrange("p c n -> p (c n)"), b5[:, 0:DIM], ACT.Copy).then_inc(s["x_hi_ready"], 1)
                        pairs(act, step, -1, N + 1)

                    @block.vector
                    def _(dve):
                        def step(i, par):
                            n, q, half, on, has = part(i, par - 1)
                            if on:
                                dve.wait_ge(s["hid_hi_ready"], n + 1)
                                if has(-2):
                                    dve.wait_ge(s["y_mm"], n - 1)
                                nc.vector.tensor_tensor(hid_lo[q][:, :, :].rearrange("p c n -> p (c n)"), b4[:, :],
                                                        hid_hi[q][:, :, :].rearrange("p c n -> p (c n)"), ALU.subtract).then_inc(s["hid_lo_ready"], 1)
                            n, q, half, on, has = part(i, par)
                            if on:
                                dve.wait_ge(s["up_mm"], n + 1)
                                dve.wait_ge(s["silu_ready"], n + 1)
                                if has(-2):
                                    dve.wait_ge(s["hid_turned"], n - 1)
                                nc.vector.scalar_tensor_tensor(out=hid[q][:, :], in0=quad[:, 2 * q + 1, :], scalar=up_scale[:, :], in1=silu[q][:, :],
                                                               op0=ALU.mult, op1=ALU.mult).then_inc(s["hid_ready"], 1)
                            n, q, half, on, has = part(i, par + 1)
                            if on:
                                dve.wait_ge(s["x_hi_ready"], n + 1)
                                if has(-2):
                                    dve.wait_ge(s["up_mm"], n - 1)
                                nc.vector.tensor_tensor(x_lo[q][:, :, :].rearrange("p c n -> p (c n)"), b5[:, 0:DIM],
                                                        x_hi[q][:, :, :].rearrange("p c n -> p (c n)"), ALU.subtract).then_inc(s["x_lo_ready"], 1)
                            n, q, half, on, has = part(i, par - 1)
                            if on:
                                dve.wait_ge(s["y_mm"], n + 1)
                                dve.wait_ge(s["weight_ready"], n + 1)
                                if has(-2):
                                    dve.wait_ge(added, 16 * (n - 1))
                                nc.vector.tensor_scalar(y[q][:, :], (b6, b7)[q][:, 0:DIM], weight[q][:, :], None, ALU.mult).then_inc(s["y_ready"], 1)
                            n, q, half, on, has = part(i, par + 1)
                            if on:
                                dve.wait_ge(gathered[q], 16 * (half + 1))
                                if has(-1):
                                    dve.wait_ge(s["weight_ready"], n)
                                nc.vector.tensor_tensor(own[:, :], xg[q][:, DIM:], is_expert[:, :, :].rearrange("p t e -> p (t e)")[:, bass.ds(n * EXPERTS, EXPERTS)],
                                                        ALU.mult).then_inc(s["own_ready"], 1)
                                dve.wait_ge(s["own_ready"], n + 1)
                                if has(-2):
                                    dve.wait_ge(s["y_ready"], n - 1)
                                nc.vector.tensor_reduce(weight[q][:, :], own[:, :], AX.X, ALU.add).then_inc(s["weight_ready"], 1)
                        pairs(dve, step, -1, N + 1)

                    @block.tensor
                    def _(pe):
                        def terms(dst, hi, lo, chunks, col, width):
                            for k in range(chunks):
                                for m, (x, w) in enumerate(((hi, w_hi), (hi, w_lo), (lo, w_hi))):
                                    last = nc.tensor.matmul(dst, x[:, k, :], w[:, bass.ds(col + k * (2 * width if width == HIDDEN else width), width)],
                                                            start=(k == 0 and m == 0), stop=(k == chunks - 1 and m == 2))
                            return last

                        def step(i, par):
                            n, q, half, on, has = part(i, par)
                            if on:
                                e = pe.value_load(expert_of[0:1, bass.ds(n, 1)], min_val=0, max_val=EXPERTS - 1)
                            m, r, _, before, had = part(i, par - 1)
                            if before:
                                f = pe.value_load(expert_of[0:1, bass.ds(m, 1)], min_val=0, max_val=EXPERTS - 1)
                            if on:
                                pe.wait_ge(s["x_hi_ready"], n + 1)
                                pe.wait_ge(s["x_lo_ready"], n + 1)
                                for up in range(2):
                                    if has(-2):
                                        pe.wait_ge(s["hid_ready"], n - 1)
                                    terms(quad[:, 2 * q + up, :], x_hi[q], x_lo[q], KD, e * W_EXPERT + up * HIDDEN,
                                          HIDDEN).then_inc(s["up_mm" if up else "gate_mm"], 1)
                                    if up == 0 and before:
                                        pe.wait_ge(s["hid_ready"], m + 1)
                                        if had(-1):
                                            pe.wait_ge(s["hid_lo_ready"], m)
                                        for k in range(KH):
                                            last = nc.tensor.transpose(b4[:, k * P:(k + 1) * P], hid[r][:, k * P:(k + 1) * P], idt[:, :])
                                        last.then_inc(s["hid_turned"], 1)
                            elif before:
                                pe.wait_ge(s["hid_ready"], m + 1)
                                pe.wait_ge(s["hid_lo_ready"], m)
                                for k in range(KH):
                                    last = nc.tensor.transpose(b4[:, k * P:(k + 1) * P], hid[r][:, k * P:(k + 1) * P], idt[:, :])
                                last.then_inc(s["hid_turned"], 1)
                            n, q, half, on, has = part(i, par + 1)
                            if on:
                                pe.wait_ge(gathered[q], 16 * (half + 1))
                                if has(-1):
                                    pe.wait_ge(s["x_lo_ready"], n)
                                for k in range(KD):
                                    last = nc.tensor.transpose(b5[:, k * P:(k + 1) * P], xg[q][:, k * P:(k + 1) * P], idt[:, :])
                                last.then_inc(s["x_turned"], 1)
                            if before:
                                pe.wait_ge(s["hid_hi_ready"], m + 1)
                                pe.wait_ge(s["hid_lo_ready"], m + 1)
                                if had(-2):
                                    pe.wait_ge(s["y_ready"], m - 1)
                                terms((b6, b7)[r][:, 0:DIM], hid_hi[r], hid_lo[r], KH, f * W_EXPERT + KD * 2 * HIDDEN,
                                      DIM).then_inc(s["y_mm"], 1)
                        pairs(pe, step, -1, N + 1)

        zero_tile = sb("zero_tile", [P, DIM + EXPERTS])
        tokenizer()
        attention()
        routing()
        experts()


def kernel(**inputs):
    import concourse.bacc as bacc
    from concourse.bass_utils import run_bass_kernel_spmd

    a = {k: np.asarray(v) for k, v in inputs.items()}
    G, PT = GRID, PATCH
    patches = a["x"].reshape(BATCH, CHANNELS, G, PT, G, PT).transpose(0, 2, 4, 3, 5, 1).reshape(BATCH * PATCHES, PATCH_DIM)
    rows = lambda w: w.reshape(-1, P, w.shape[-1]).transpose(1, 0, 2)
    wqkv = np.concatenate([rows(a[f"L0_attn_w{c}"].T) for c in "qkv"], axis=2)
    freq = 1.0 / 10000.0 ** (np.arange(0, HEAD_DIM, 2, dtype=np.float32) / HEAD_DIM)
    angle = np.outer(np.arange(SEQ, dtype=np.float32), freq.astype(np.float32))
    cos, sin = np.cos(angle), np.sin(angle)
    rope = np.stack([np.tile(np.repeat(cos, 2, axis=1), (1, 2 * HEADS)),
                     np.tile(np.stack([sin, -sin], axis=2).reshape(SEQ, HEAD_DIM), (1, 2 * HEADS))], axis=1).astype(np.float32)
    w13 = a["L0_ffn_moe_w13"].reshape(EXPERTS, KD, P, 2 * HIDDEN).transpose(2, 0, 1, 3).reshape(P, EXPERTS, -1)
    w2 = a["L0_ffn_moe_w2"].reshape(EXPERTS, KH, P, DIM).transpose(2, 0, 1, 3).reshape(P, EXPERTS, -1)
    experts_w = np.concatenate([w13, w2], axis=2).reshape(P, -1)
    arrays = dict(
        patches=patches, txt=a["txt"].reshape(BATCH * TEXT, DIM),
        ln1_g=a["L0_tok_ln1_g"].reshape(KT, P).T, ln1_b=a["L0_tok_ln1_b"].reshape(KT, P).T,
        w_proj=rows(a["L0_tok_W_proj"]), b_proj=a["L0_tok_b_proj"], ln2_g=a["L0_tok_ln2_g"], ln2_b=a["L0_tok_ln2_b"],
        cls_token=a["L0_tok_cls_token"].reshape(1, DIM), pos_emb=a["L0_tok_pos_emb"].reshape(1 + PATCHES, DIM),
        wqkv=wqkv, router=rows(a["L0_ffn_moe_router"]), experts_w=experts_w,
        ident=np.eye(P, dtype=np.float32), rope=rope,
        prefix=np.triu(np.ones((SEQ, SEQ), np.float32), 1),
    )
    nc = bacc.Bacc("TRN2", target_bir_lowering=False, num_devices=1)
    sent, args = {}, {}
    for name, x in arrays.items():
        x = np.ascontiguousarray(x)
        sent[f"in_{name}"] = x
        args[name] = nc.dram_tensor(f"in_{name}", x.shape, mybir.dt.from_np(x.dtype), kind="ExternalInput").ap()
    out = nc.dram_tensor("out", (TOKENS + SPARE, DIM), mybir.dt.float32, kind="ExternalOutput").ap()
    build(nc, out=out, **args)
    got = run_bass_kernel_spmd(nc, [sent], core_ids=[0]).results[0]["out"]
    return got[:TOKENS].reshape(BATCH, SEQ, DIM)
```

```python
from contextlib import ExitStack

import numpy as np
import concourse.bass as bass
from concourse import mybir

BATCH, CHANNELS, IMAGE, PATCH = 64, 3, 96, 16
GRID = IMAGE // PATCH
PATCHES = GRID * GRID
DIM, TEXT = 256, 32
SEQ = 1 + PATCHES + TEXT
TOKENS = BATCH * SEQ
PATCH_DIM = CHANNELS * PATCH * PATCH
HEADS, HEAD_DIM = 16, 16
EXPERTS, HIDDEN, TOP_K = 8, 512, 2
EPS = 1e-5
P = 128
TILES_TOK = BATCH * PATCHES // P
KT = PATCH_DIM // P
KD = DIM // P
KH = HIDDEN // P
PAD = 32
CH = HEADS * PAD // P
TILES_MOE = (TOKENS * TOP_K + EXPERTS * (P - 1)) // P
SPARE = P
BANK = 512
W_EXPERT = KD * 2 * HIDDEN + KH * DIM
W_CHUNK = EXPERTS * W_EXPERT // BATCH
MAX_LOADS = 16


def build(nc, patches, txt, ln1_g, ln1_b, w_proj, b_proj, ln2_g, ln2_b, cls_token, pos_emb,
          wqkv, router, experts_w, ident, rope, prefix, out):
    fp32, i32, fp16 = mybir.dt.float32, mybir.dt.int32, mybir.dt.float16
    ALU, ACT, AX = mybir.AluOpType, mybir.ActivationFunctionType, mybir.AxisListType
    ctx = ExitStack()
    with ctx:
        def sb(name, shape, dt=fp32):
            return ctx.enter_context(nc.sbuf_tensor(name, shape, dt))

        def sem(name):
            return ctx.enter_context(nc.semaphore(name))

        patch_rows = nc.dram_tensor("patch_rows", (BATCH * PATCHES, DIM), fp32).ap()
        h_rows = nc.dram_tensor("h_rows", (TOKENS, DIM), fp32).ap()
        xn_rows = nc.dram_tensor("xn_rows", (TOKENS + SPARE, DIM + EXPERTS), fp32).ap()

        bank = [ctx.enter_context(nc.psum_tensor(f"bank{i}", [P, BANK], fp32)) for i in range(4, 8)]
        quad = ctx.enter_context(nc.psum_tensor("quad", [P, 4, BANK], fp32))
        b4, b5, b6, b7 = bank

        idt = sb("idt", [P, P])
        eps_pow = sb("eps_pow", [P, 1])
        wqkv_hi, wqkv_lo = (sb(f"wqkv_{x}", [P, KD, 3 * DIM], fp16) for x in ("hi", "lo"))
        w_hi, w_lo = (sb(f"w_{x}", [P, EXPERTS * W_EXPERT], fp16) for x in ("hi", "lo"))
        scale = sb("scale", [P, 2])
        unscale = sb("unscale", [P, 2])
        up_scale, y_scale = sb("up_scale", [P, 1]), sb("y_scale", [P, 1])
        router_sb = sb("router_sb", [P, KD, EXPERTS])
        rope_sb = sb("rope_sb", [SEQ, 2, 2 * DIM])
        prefix_sb = sb("prefix_sb", [SEQ, SEQ])
        ones = sb("ones", [P, P])
        scale_rows = sb("scale_rows", [SEQ, DIM])
        shift_rows = sb("shift_rows", [SEQ, DIM])
        shift_add = sb("shift_add", [SEQ, DIM])
        logits = sb("logits", [SEQ, BATCH, EXPERTS])
        expert_of = sb("expert_of", [P, TILES_MOE], i32)
        token_of = sb("token_of", [P, TILES_MOE], i32)
        is_expert = sb("is_expert", [P, TILES_MOE, EXPERTS])

        held = {e: sem("held_" + e) for e in ("dve", "pool", "pe", "sp")}

        def tokenizer():
            with ExitStack() as st:
                def tb(name, shape, dt=fp32):
                    return st.enter_context(nc.sbuf_tensor(name, shape, dt))

                wp = tb("wp", [P, KT, DIM])
                wqkv_sb = tb("wqkv_sb", [P, KD, 3 * DIM])
                w_part = [tb(f"w_part{i}", [P, EXPERTS * W_EXPERT // MAX_LOADS]) for i in range(2)]
                largest, all_max = tb("largest", [P, MAX_LOADS + 1]), tb("all_max", [P, 2])
                peak = tb("peak", [P, 2])
                wg = tb("wg", [P, KT, DIM])
                g1 = tb("g1", [P, KT])
                b1 = tb("b1", [P, KT])
                b1_wide = tb("b1_wide", [P, KT, P])
                bp = tb("bp", [P, DIM])
                bias = tb("bias", [P, DIM])
                xt = [tb(f"xt{i}", [P, PATCH_DIM]) for i in range(2)]
                xc = [tb(f"xc{i}", [P, PATCH_DIM]) for i in range(2)]
                xcT = [tb(f"xcT{i}", [P, PATCH_DIM]) for i in range(2)]
                st1 = tb("st1", [P, 2, 6])
                mv1 = [tb(f"tmv1{i}", [P, 2]) for i in range(2)]
                ve1 = tb("tve1", [P, 1])
                rs1 = [tb(f"trs1{i}", [P, 1]) for i in range(2)]
                z = [tb(f"z{i}", [P, DIM]) for i in range(2)]
                st2 = tb("tst2", [P, 6])
                mv2 = [tb(f"tmv2{i}", [P, 2]) for i in range(2)]
                ve2 = tb("tve2", [P, 1])
                rs2 = [tb(f"trs2{i}", [P, 1]) for i in range(2)]
                zn = [tb(f"zn{i}", [P, DIM]) for i in range(2)]

                names = """t_const t_small t_wg t_wide t_bias_mm t_bias x_turned xT_ready z_mm stats1 mv1_ready eps1 rstd1
                    xc_ready z_ready stats2 mv2_ready eps2 rstd2 zn_ready t_ones t_pow
                    sc_init sh_done zero_spare part_max own_max peak_ready scale_step split_hi split_lo""".split()
                part_loaded = [sem(f"a_part_loaded{i}") for i in range(2)]
                s = {n: sem("a_" + n) for n in names}
                x_loaded = [sem(f"a_x_loaded{i}") for i in range(2)]
                z_stored = [sem(f"a_z_stored{i}") for i in range(2)]
                spare_stored, weights_in, late_in, rope_in, table_in = (sem("a_" + x) for x in ("spare_stored", "weights_in", "late_in", "rope_in", "table_in"))

                N = TILES_TOK
                FIRST, LAST = 2, (N - 2) // 2
                WP = EXPERTS * W_EXPERT // MAX_LOADS

                def pairs(eng, step, lo, hi):
                    for t in range(lo, 2 * FIRST):
                        step(t // 2, t % 2)
                    with eng.Fori(FIRST, LAST) as i:
                        for par in range(2):
                            step(i, par)
                    for t in range(2 * LAST, hi):
                        step(t // 2, t % 2)

                def live(i, off):
                    return not isinstance(i, int) or 0 <= 2 * i + off < N

                def later(i, off, back=2):
                    return not isinstance(i, int) or 2 * i + off >= back

                with nc.Block() as block:
                    @block.sync
                    def _(sp):
                        sp.dma_start(idt[:, :], ident).then_inc(s["t_const"], 16)
                        sp.dma_start(wp[:, :, :], w_proj).then_inc(s["t_const"], 16)
                        sp.dma_start(g1[:, :], ln1_g).then_inc(s["t_const"], 16)
                        sp.dma_start(b1[:, :], ln1_b).then_inc(s["t_const"], 16)
                        sp.dma_start(bp[:, :], b_proj[None, :].broadcast_to([P, DIM])).then_inc(s["t_const"], 16)
                        sp.dma_start(wqkv_sb[:, :, :], wqkv).then_inc(weights_in, 16)

                        def step(i, par):
                            if live(i, par):
                                n = 2 * i + par
                                if later(i, par):
                                    sp.wait_ge(s["xc_ready"], n - 1)
                                sp.sem_inc(held["sp"], 1)
                                sp.dma_start(xt[par][:, :], patches[bass.ds(n * P, P), :]).then_inc(x_loaded[par], 16)
                            n = 2 * i + par - 2
                            if not isinstance(i, int) or 0 <= n < MAX_LOADS:
                                if later(i, par - 2):
                                    sp.wait_ge(s["part_max"], n - 1)
                                    sp.sem_inc(held["sp"], 1)
                                sp.dma_start(w_part[par][:, :], experts_w[:, bass.ds(n * WP, WP)]).then_inc(part_loaded[par], 16)
                            off = par - 4
                            if live(i, off):
                                n = 2 * i + off
                                sp.wait_ge(s["zn_ready"], n + 1)
                                sp.sem_inc(held["sp"], 1)
                                sp.dma_start(patch_rows[bass.ds(n * P, P), :], zn[off % 2][:, :]).then_inc(z_stored[off % 2], 16)
                        pairs(sp, step, 0, N + 4)
                        sp.dma_start(router_sb[:, :, :], router).then_inc(late_in, 16)
                        sp.dma_start(prefix_sb[:, :], prefix).then_inc(late_in, 16)
                        for par in range(2):
                            sp.wait_ge(z_stored[par], 16 * (N // 2))
                        sp.wait_ge(late_in, 32)
                        sp.wait_ge(table_in, 16 * 5)
                        sp.wait_ge(spare_stored, 16)

                    @block.gpsimd
                    def _(pool):
                        nc.gpsimd.memset(eps_pow[:, :], -0.5).then_inc(s["t_pow"], 1)
                        nc.gpsimd.memset(ones[:, :], 1.0).then_inc(s["t_ones"], 1)
                        nc.gpsimd.memset(scale_rows[:, :], 1.0).then_inc(s["sc_init"], 1)
                        nc.gpsimd.memset(shift_rows[:, :], 0.0).then_inc(s["sc_init"], 1)
                        nc.gpsimd.memset(shift_add[:, :], 0.0).then_inc(s["sc_init"], 1)
                        pool.wait_ge(s["sc_init"], 3)
                        pool.dma_start(scale_rows[1:1 + PATCHES, :], ln2_g[None, :].broadcast_to([PATCHES, DIM])).then_inc(table_in, 16)
                        pool.dma_start(shift_rows[1:1 + PATCHES, :], ln2_b[None, :].broadcast_to([PATCHES, DIM])).then_inc(table_in, 16)
                        pool.dma_start(shift_rows[0:1, :], cls_token).then_inc(table_in, 16)
                        pool.dma_start(shift_add[0:1 + PATCHES, :], pos_emb).then_inc(table_in, 16)
                        pool.dma_start(rope_sb[:, :, :], rope).then_inc(rope_in, 16)
                        pool.wait_ge(s["t_ones"], 1)
                        nc.gpsimd.memset(zero_tile[:, :], 0.0).then_inc(s["zero_spare"], 1)
                        pool.wait_ge(s["zero_spare"], 1)
                        pool.dma_start(xn_rows[TOKENS:TOKENS + SPARE, :], zero_tile[:, :]).then_inc(spare_stored, 16)
                        pool.dma_start(out[TOKENS:TOKENS + SPARE, :], zero_tile[:, 0:DIM]).then_inc(table_in, 16)

                        def step(i, par):
                            if live(i, par + 2):
                                n, q = 2 * i + par + 2, par
                                pool.wait_ge(s["mv1_ready"], n + 1)
                                if later(i, par + 2):
                                    pool.wait_ge(s["xc_ready"], n - 1)
                                pool.sem_inc(held["pool"], 1)
                                nc.gpsimd.tensor_scalar(ve1[:, :], mv1[q][:, 1:2], EPS, None, ALU.add).then_inc(s["eps1"], 1)
                                pool.wait_ge(s["eps1"], n + 1)
                                nc.gpsimd.tensor_tensor(rs1[q][:, :], ve1[:, :], eps_pow[:, :], ALU.pow).then_inc(s["rstd1"], 1)
                            if live(i, par - 1):
                                n, q = 2 * i + par - 1, (par - 1) % 2
                                pool.wait_ge(s["mv2_ready"], n + 1)
                                pool.sem_inc(held["pool"], 1)
                                nc.gpsimd.tensor_scalar(ve2[:, :], mv2[q][:, 1:2], EPS, None, ALU.add).then_inc(s["eps2"], 1)
                                pool.wait_ge(s["eps2"], n + 1)
                                nc.gpsimd.tensor_tensor(rs2[q][:, :], ve2[:, :], eps_pow[:, :], ALU.pow).then_inc(s["rstd2"], 1)
                        pairs(pool, step, -2, N + 1)
                        pool.wait_ge(table_in, 16 * 5)
                        nc.gpsimd.tensor_tensor(shift_rows[:, :], shift_rows[:, :], shift_add[:, :], ALU.add).then_inc(s["sh_done"], 1)
                        pool.wait_ge(s["sh_done"], 1)
                        pool.wait_ge(s["own_max"], 2)
                        nc.gpsimd.partition_all_reduce(peak[:, :], all_max[:, :], P, bass.bass_isa.ReduceOp.max).then_inc(s["peak_ready"], 1)

                    @block.vector
                    def _(dve):
                        dve.wait_ge(s["t_const"], 80)
                        dve.wait_ge(s["t_ones"], 1)
                        for k in range(KT):
                            nc.vector.tensor_scalar(wg[:, k, :], wp[:, k, :], g1[:, k:k + 1], None, ALU.mult).then_inc(s["t_wg"], 1)
                            nc.vector.tensor_scalar(b1_wide[:, k, :], ones[:, :], b1[:, k:k + 1], None, ALU.mult).then_inc(s["t_wide"], 1)
                        dve.wait_ge(s["t_bias_mm"], 1)
                        nc.vector.tensor_tensor(bias[:, :], b4[:, 0:DIM], bp[:, :], ALU.add).then_inc(s["t_bias"], 1)
                        dve.wait_ge(s["t_bias"], 1)
                        dve.wait_ge(weights_in, 16)
                        nc.vector.tensor_reduce(all_max[:, 0:1], wqkv_sb[:, :, :], AX.XY, ALU.max, apply_absolute_value=True).then_inc(s["own_max"], 1)

                        def step(i, par):
                            if live(i, par + 2):
                                n, q = 2 * i + par + 2, par
                                half = i + 1
                                dve.wait_ge(x_loaded[q], 16 * (half + 1))
                                for c in range(2):
                                    nc.vector.bn_stats(st1[:, c, :], xt[q][:, c * 384:(c + 1) * 384]).then_inc(s["stats1"], 1)
                                dve.wait_ge(s["stats1"], 2 * n + 2)
                                dve.sem_inc(held["dve"], 1)
                                nc.vector.bn_aggr(mv1[q][:, :], st1[:, :, :].rearrange("p a b -> p (a b)")).then_inc(s["mv1_ready"], 1)
                            if live(i, par - 1):
                                n, q = 2 * i + par - 1, (par - 1) % 2
                                dve.wait_ge(s["z_mm"], n + 1)
                                nc.vector.tensor_tensor(z[q][:, :], bank[q][:, 0:DIM], bias[:, :], ALU.add).then_inc(s["z_ready"], 1)
                                dve.wait_ge(s["z_ready"], n + 1)
                                nc.vector.bn_stats(st2[:, :], z[q][:, :]).then_inc(s["stats2"], 1)
                                dve.wait_ge(s["stats2"], n + 1)
                                dve.sem_inc(held["dve"], 1)
                                nc.vector.bn_aggr(mv2[q][:, :], st2[:, :]).then_inc(s["mv2_ready"], 1)
                            if live(i, par + 2):
                                n, q = 2 * i + par + 2, par
                                dve.wait_ge(s["rstd1"], n + 1)
                                if later(i, par + 2):
                                    dve.wait_ge(s["x_turned"], n - 1)
                                dve.wait_ge(s["mv1_ready"], n + 1)
                                nc.vector.tensor_scalar(xc[q][:, :], xt[q][:, :], mv1[q][:, 0:1], rs1[q][:, :],
                                                        ALU.subtract, ALU.mult).then_inc(s["xc_ready"], 1)
                            n = 2 * i + par
                            if not isinstance(i, int) or 0 <= n < MAX_LOADS:
                                dve.wait_ge(part_loaded[par], 16 * (i + 1))
                                nc.vector.tensor_reduce(largest[:, bass.ds(n, 1)], w_part[par][:, :], AX.X, ALU.max,
                                                        apply_absolute_value=True).then_inc(s["part_max"], 1)
                            if live(i, par - 1):
                                n, q = 2 * i + par - 1, (par - 1) % 2
                                half = i + (par - 1) // 2
                                dve.wait_ge(s["rstd2"], n + 1)
                                dve.wait_ge(s["mv2_ready"], n + 1)
                                if later(i, par - 1):
                                    dve.wait_ge(z_stored[q], 16 * half)
                                nc.vector.tensor_scalar(zn[q][:, :], z[q][:, :], mv2[q][:, 0:1], rs2[q][:, :],
                                                        ALU.subtract, ALU.mult).then_inc(s["zn_ready"], 1)
                        pairs(dve, step, -2, N + 1)

                        steps = [0]

                        def then(ins):
                            steps[0] += 1
                            ins.then_inc(s["scale_step"], 1)
                            dve.wait_ge(s["scale_step"], steps[0])

                        dve.wait_ge(s["part_max"], MAX_LOADS)
                        dve.wait_ge(rope_in, 16)
                        nc.vector.tensor_reduce(all_max[:, 1:2], largest[:, 0:MAX_LOADS], AX.X, ALU.max).then_inc(s["own_max"], 1)
                        dve.wait_ge(s["peak_ready"], 1)
                        then(nc.vector.tensor_scalar(peak[:, :], peak[:, :], 2.0 ** -20, 2.0 ** 40, ALU.max, ALU.min))
                        then(nc.vector.reciprocal(scale[:, :], peak[:, :]))
                        then(nc.vector.tensor_scalar(scale[:, :], scale[:, :], 2.0 ** 14, None, ALU.mult))
                        then(nc.vector.tensor_scalar(scale[:, :].bitcast(i32), scale[:, :].bitcast(i32), 0x7F800000, None, ALU.bitwise_and))
                        then(nc.vector.reciprocal(unscale[:, :], scale[:, :]))
                        then(nc.vector.tensor_scalar(up_scale[:, :], scale[:, 1:2], 2.0 ** -29, None, ALU.mult))
                        then(nc.vector.tensor_scalar(y_scale[:, :], unscale[:, 1:2], unscale[:, 1:2], 2.0 ** 29, ALU.mult, ALU.mult))
                        then(nc.vector.tensor_scalar(y_scale[:, :], y_scale[:, :], unscale[:, 1:2], None, ALU.mult))
                        then(nc.vector.tensor_scalar(rope_sb[:, :, :], rope_sb[:, :, :], unscale[0:SEQ, 0:1], None, ALU.mult))
                        nc.vector.tensor_scalar(wqkv_hi[:, :, :], wqkv_sb[:, :, :], scale[:, 0:1], None, ALU.mult).then_inc(s["split_hi"], 1)
                        dve.wait_ge(s["split_hi"], 1)
                        nc.vector.scalar_tensor_tensor(out=wqkv_lo[:, :, :], in0=wqkv_sb[:, :, :], scalar=scale[:, 0:1], in1=wqkv_hi[:, :, :],
                                                       op0=ALU.mult, op1=ALU.subtract).then_inc(s["split_lo"], 1)
                        dve.wait_ge(s["split_lo"], 1)

                    @block.scalar
                    def _(act):
                        def step(i, par):
                            if live(i, par + 1):
                                n, q = 2 * i + par + 1, (par + 1) % 2
                                act.wait_ge(s["x_turned"], n + 1)
                                if later(i, par + 1):
                                    act.wait_ge(s["z_mm"], n - 1)
                                nc.scalar.activation(xcT[q][:, :].rearrange("p (a b) -> p a b", a=2),
                                                     quad[:, 2 * q:2 * q + 2, 0:384], ACT.Copy).then_inc(s["xT_ready"], 1)
                        pairs(act, step, -1, N)

                    @block.tensor
                    def _(pe):
                        pe.wait_ge(s["t_wide"], KT)
                        pe.wait_ge(s["t_const"], 80)
                        for k in range(KT):
                            last = nc.tensor.matmul(b4[:, 0:DIM], b1_wide[:, k, :], wp[:, k, :], start=(k == 0), stop=(k == KT - 1))
                        last.then_inc(s["t_bias_mm"], 1)
                        pe.wait_ge(s["t_wg"], KT)
                        pe.wait_ge(s["t_bias"], 1)

                        def step(i, par):
                            if live(i, par + 1):
                                n, q = 2 * i + par + 1, (par + 1) % 2
                                pe.wait_ge(s["xc_ready"], n + 1)
                                if later(i, par + 1):
                                    pe.wait_ge(s["xT_ready"], n - 1)
                                for k in range(KT):
                                    last = nc.tensor.transpose(quad[:, 2 * q + k // 3, (k % 3) * P:(k % 3 + 1) * P],
                                                               xc[q][:, k * P:(k + 1) * P], idt[:, :])
                                last.then_inc(s["x_turned"], 1)
                            if live(i, par):
                                n, q = 2 * i + par, par
                                pe.wait_ge(s["xT_ready"], n + 1)
                                if later(i, par):
                                    pe.wait_ge(s["z_ready"], n - 1)
                                for k in range(KT):
                                    last = nc.tensor.matmul(bank[q][:, 0:DIM], xcT[q][:, k * P:(k + 1) * P], wg[:, k, :],
                                                            start=(k == 0), stop=(k == KT - 1))
                                last.then_inc(s["z_mm"], 1)
                        pairs(pe, step, -1, N)

        def attention():
            with ExitStack() as st:
                def tb(name, shape, dt=fp32):
                    return st.enter_context(nc.sbuf_tensor(name, shape, dt))

                def ring(name, shape, dt=fp32):
                    return [tb(f"{name}{i}", shape, dt) for i in range(2)]

                tok, h, xn = ring("tok", [SEQ, DIM]), ring("h", [SEQ, DIM]), ring("xn", [SEQ, DIM])
                h_scaled = tb("h_scaled", [SEQ, DIM])
                stats, stats2 = tb("stats", [SEQ, 6]), tb("stats2", [SEQ, 6])
                mv, mv2 = ring("mv", [SEQ, 2]), ring("mv2", [SEQ, 2])
                ve, ve2 = tb("ve", [SEQ, 1]), tb("ve2", [SEQ, 1])
                rs, rs2 = ring("rs", [SEQ, 1]), ring("rs2", [SEQ, 1])
                x_hi, x_lo = ring("bx_hi", [P, KD, SEQ], fp16), ring("bx_lo", [P, KD, SEQ], fp16)
                xn2T = ring("xn2T", [P, KD, SEQ])
                rot = ring("rot", [SEQ, 2, 2 * DIM])
                qk = ring("qk", [SEQ, 2 * HEADS, PAD])
                q_h, k_h = ring("q_h", [P, CH, SEQ], fp16), ring("k_h", [P, CH, SEQ], fp16)
                kT = ring("kT", [P, CH, SEQ])
                qmT = ring("qmT", [P, CH, 4, SEQ])
                v = [tb(f"v{j}", [SEQ, HEADS, PAD]) for j in range(4)]
                probs = ring("probs", [SEQ, CH, 4, SEQ])
                oT = ring("oT", [P, CH, SEQ])
                denom = ring("denom", [SEQ, HEADS])
                att, h_back, h2, xn2 = ring("att", [SEQ, DIM]), ring("h_back", [SEQ, DIM]), ring("h2", [SEQ, DIM]), ring("xn2", [SEQ, DIM])
                w_raw = ring("w_raw", [P, W_CHUNK])

                names = """zeroed_pool zeroed_dve init tok_scaled h_ready stats_done mv_ready eps_added rstd_ready xn_ready xn_turned x_hi_ready x_lo_ready
                    qk_mm v_mm rot_mul qk_even qk_odd q_turned k_turned q_h_ready k_h_ready kT_ready v_ready s_mm max_ready qm_turned
                    qmT_ready st_mm probs_ready o_mm oT_ready o_turned denom_ready att_ready h2_ready stats2_done mv2_ready
                    eps2_added rstd2_ready xn2_ready xn2_turned xn2T_ready logits_mm logits_saved w_hi_ready w_lo_ready""".split()
                s = {n: sem("b_" + n) for n in names}
                tok_loaded = [sem(f"b_tok_loaded{i}") for i in range(2)]
                h_stored = [sem(f"b_h_stored{i}") for i in range(2)]
                h_loaded = [sem(f"b_h_loaded{i}") for i in range(2)]
                h2_stored = [sem(f"b_h2_stored{i}") for i in range(2)]
                xn2_stored = [sem(f"b_xn2_stored{i}") for i in range(2)]
                w_loaded = [sem(f"b_w_loaded{i}") for i in range(2)]
                INIT = 10

                N, UNROLL = BATCH, 4
                FIRST, LAST = 2, 15

                def steps(eng, step):
                    for t in range(-4, UNROLL * FIRST):
                        step(t // UNROLL, t % UNROLL)
                    with eng.Fori(FIRST, LAST) as i:
                        for u in range(UNROLL):
                            step(i, u)
                    for t in range(UNROLL * LAST, N + 5):
                        step(t // UNROLL, t % UNROLL)

                def part(i, off):
                    if isinstance(i, int):
                        b = UNROLL * i + off
                        return b, off % 2, 2 * i + off // 2, 0 <= b < N, lambda k: 0 <= b + k < N
                    return UNROLL * i + off, off % 2, 2 * i + off // 2, True, lambda k: True

                def rotary(eng, q, c):
                    cosines = rot[q][:, 0, :].rearrange("p (n d two) -> p n d two", d=8, two=2)
                    sines = rot[q][:, 1, :].rearrange("p (n d two) -> p n d two", d=8, two=2)
                    heads = qk[q][:, :, 0:HEAD_DIM].rearrange("p n (d two) -> p n d two", two=2)
                    return eng.tensor_tensor(heads[:, :, :, c], cosines[:, :, :, c], sines[:, :, :, 1 - c], ALU.add)

                with nc.Block() as block:
                    @block.sync
                    def _(sp):
                        def step(i, u):
                            b, q, half, on, has = part(i, u - 3)
                            if on:
                                sp.wait_ge(h_stored[q], 16 * (half + 1))
                                sp.sem_inc(held["sp"], 1)
                                if has(-2):
                                    sp.wait_ge(s["h2_ready"], b - 1)
                                    sp.sem_inc(held["sp"], 1)
                                sp.dma_start(h_back[q][:, :], h_rows[bass.ds(b * SEQ, SEQ), :]).then_inc(h_loaded[q], 16)
                            b, q, half, on, has = part(i, u + 4)
                            if on:
                                if has(-2):
                                    sp.wait_ge(s["tok_scaled"], b - 1)
                                    sp.sem_inc(held["sp"], 1)
                                sp.dma_start(tok[q][1:1 + PATCHES, :], patch_rows[bass.ds(b * PATCHES, PATCHES), :]).then_inc(tok_loaded[q], 16)
                                sp.dma_start(tok[q][1 + PATCHES:SEQ, :], txt[bass.ds(b * TEXT, TEXT), :]).then_inc(tok_loaded[q], 16)
                            b, q, half, on, has = part(i, u + 1)
                            if on:
                                if has(-2):
                                    sp.wait_ge(s["w_lo_ready"], b - 1)
                                    sp.sem_inc(held["sp"], 1)
                                sp.dma_start(w_raw[q][:, :], experts_w[:, bass.ds(b * W_CHUNK, W_CHUNK)]).then_inc(w_loaded[q], 16)
                            b, q, half, on, has = part(i, u - 4)
                            if on:
                                sp.wait_ge(s["h2_ready"], b + 1)
                                sp.sem_inc(held["sp"], 1)
                                sp.dma_start(out[bass.ds(b * SEQ, SEQ), :], h2[q][:, :]).then_inc(h2_stored[q], 16)
                            b, q, half, on, has = part(i, u + 3)
                            if on:
                                sp.wait_ge(s["h_ready"], b + 1)
                                sp.sem_inc(held["sp"], 1)
                                sp.dma_start(h_rows[bass.ds(b * SEQ, SEQ), :], h[q][:, :]).then_inc(h_stored[q], 16)
                            b, q, half, on, has = part(i, u - 4)
                            if on:
                                sp.wait_ge(s["xn2_ready"], b + 1)
                                sp.sem_inc(held["sp"], 1)
                                sp.dma_start(xn_rows[bass.ds(b * SEQ, SEQ), 0:DIM], xn2[q][:, :]).then_inc(xn2_stored[q], 16)
                        steps(sp, step)
                        for par in range(2):
                            sp.wait_ge(h2_stored[par], 16 * (N // 2))
                            sp.wait_ge(xn2_stored[par], 16 * (N // 2))

                    @block.gpsimd
                    def _(pool):
                        for q in range(2):
                            nc.gpsimd.memset(tok[q][0:1, :], 0.0).then_inc(s["init"], 1)
                            nc.gpsimd.memset(qk[q][:, :, :], 0.0).then_inc(s["zeroed_pool"], 1)
                        pool.wait_ge(s["zeroed_pool"], 2)
                        for q in range(2):
                            nc.gpsimd.memset(qk[q][:, HEADS:, HEAD_DIM:HEAD_DIM + 1], 1.0).then_inc(s["init"], 1)
                        pool.wait_ge(s["init"], INIT)

                        def step(i, u):
                            b, q, half, on, has = part(i, u - 4)
                            if on:
                                pool.wait_ge(s["att_ready"], b + 1)
                                pool.wait_ge(h_loaded[q], 16 * (half + 1))
                                if has(-2):
                                    pool.wait_ge(s["xn2_ready"], b - 1)
                                    pool.wait_ge(h2_stored[q], 16 * half)
                                nc.gpsimd.tensor_tensor(h2[q][:, :], h_back[q][:, :], att[q][:, :], ALU.add).then_inc(s["h2_ready"], 1)
                            b, q, half, on, has = part(i, u + 2)
                            if on:
                                pool.wait_ge(s["mv_ready"], b + 1)
                                if has(-2):
                                    pool.wait_ge(s["xn_ready"], b - 1)
                                pool.sem_inc(held["pool"], 1)
                                nc.gpsimd.tensor_scalar(ve[:, :], mv[q][:, 1:2], EPS, None, ALU.add).then_inc(s["eps_added"], 1)
                                pool.wait_ge(s["eps_added"], b + 1)
                                nc.gpsimd.tensor_tensor(rs[q][:, :], ve[:, :], eps_pow[0:SEQ, :], ALU.pow).then_inc(s["rstd_ready"], 1)
                            b, q, half, on, has = part(i, u - 4)
                            if on:
                                pool.wait_ge(s["mv2_ready"], b + 1)
                                pool.sem_inc(held["pool"], 1)
                                nc.gpsimd.tensor_scalar(ve2[:, :], mv2[q][:, 1:2], EPS, None, ALU.add).then_inc(s["eps2_added"], 1)
                                pool.wait_ge(s["eps2_added"], b + 1)
                                nc.gpsimd.tensor_tensor(rs2[q][:, :], ve2[:, :], eps_pow[0:SEQ, :], ALU.pow).then_inc(s["rstd2_ready"], 1)
                            b, q, half, on, has = part(i, u + 3)
                            if on:
                                pool.wait_ge(tok_loaded[q], 32 * (half + 1))
                                if has(-1):
                                    pool.wait_ge(s["h_ready"], b)
                                nc.gpsimd.tensor_tensor(h_scaled[:, :], tok[q][:, :], scale_rows[:, :], ALU.mult).then_inc(s["tok_scaled"], 1)
                                pool.wait_ge(s["tok_scaled"], b + 1)
                                if has(-2):
                                    pool.wait_ge(s["xn_ready"], b - 1)
                                    pool.wait_ge(h_stored[q], 16 * half)
                                nc.gpsimd.tensor_tensor(h[q][:, :], h_scaled[:, :], shift_rows[:, :], ALU.add).then_inc(s["h_ready"], 1)
                            b, q, half, on, has = part(i, u)
                            if on:
                                pool.wait_ge(s["rot_mul"], b + 1)
                                if has(-2):
                                    pool.wait_ge(s["qm_turned"], b - 1)
                                rotary(nc.gpsimd, q, 1).then_inc(s["qk_odd"], 1)
                        steps(pool, step)

                    @block.vector
                    def _(dve):
                        for j in range(4):
                            nc.vector.memset(v[j][:, :, :], 0.0).then_inc(s["zeroed_dve"], 1)
                        for q in range(2):
                            nc.vector.memset(qmT[q][:, :, :, :], 0.0).then_inc(s["init"], 1)
                        dve.wait_ge(s["zeroed_dve"], 4)
                        for j in range(4):
                            nc.vector.memset(v[j][:, :, HEAD_DIM:HEAD_DIM + 1], 1.0).then_inc(s["init"], 1)
                        dve.wait_ge(s["init"], INIT)

                        def step(i, u):
                            b, q, half, on, has = part(i, u - 1)
                            if on:
                                dve.wait_ge(s["q_turned"], b + 1)
                                if has(-2):
                                    dve.wait_ge(s["s_mm"], b - 1)
                                nc.vector.tensor_copy(q_h[q][:, :, :].rearrange("p c n -> p (c n)"), b6[:, 0:CH * SEQ]).then_inc(s["q_h_ready"], 1)
                            b, q, half, on, has = part(i, u + 2)
                            if on:
                                dve.wait_ge(s["h_ready"], b + 1)
                                if has(-1):
                                    dve.wait_ge(s["mv_ready"], b)
                                nc.vector.bn_stats(stats[:, :], h[q][:, :]).then_inc(s["stats_done"], 1)
                                dve.wait_ge(s["stats_done"], b + 1)
                                dve.sem_inc(held["dve"], 1)
                                nc.vector.bn_aggr(mv[q][:, :], stats[:, :]).then_inc(s["mv_ready"], 1)
                            b, q, half, on, has = part(i, u - 4)
                            if on:
                                dve.wait_ge(s["h2_ready"], b + 1)
                                if has(-1):
                                    dve.wait_ge(s["mv2_ready"], b)
                                nc.vector.bn_stats(stats2[:, :], h2[q][:, :]).then_inc(s["stats2_done"], 1)
                                dve.wait_ge(s["stats2_done"], b + 1)
                                dve.sem_inc(held["dve"], 1)
                                nc.vector.bn_aggr(mv2[q][:, :], stats2[:, :]).then_inc(s["mv2_ready"], 1)
                            b, q, half, on, has = part(i, u - 1)
                            if on:
                                dve.wait_ge(s["s_mm"], b + 1)
                                nc.vector.tensor_reduce(qk[q][:, 0:HEADS, HEAD_DIM].rearrange("p (c g) -> p g c", g=4),
                                                        quad[0:SEQ, :, 0:CH * SEQ].rearrange("p g (c k) -> p g c k", k=SEQ),
                                                        AX.X, ALU.max, negate=True).then_inc(s["max_ready"], 1)
                            b, q, half, on, has = part(i, u)
                            if on:
                                dve.wait_ge(s["qk_mm"], b + 1)
                                if has(-2):
                                    dve.wait_ge(s["qk_odd"], b - 1)
                                    dve.wait_ge(s["qk_even"], b - 1)
                                nc.vector.tensor_tensor(rot[q][:, :, :], b4[0:SEQ, None, :].broadcast_to([SEQ, 2, 2 * DIM]),
                                                        rope_sb[:, :, :], ALU.mult).then_inc(s["rot_mul"], 1)
                                dve.wait_ge(s["rot_mul"], b + 1)
                                if has(-2):
                                    dve.wait_ge(s["qm_turned"], b - 1)
                                rotary(nc.vector, q, 0).then_inc(s["qk_even"], 1)
                            b, q, half, on, has = part(i, u + 1)
                            if on:
                                dve.wait_ge(s["x_hi_ready"], b + 1)
                                if has(-6):
                                    dve.wait_ge(s["xn2T_ready"], b - 5)
                                if has(-2):
                                    dve.wait_ge(s["v_mm"], b - 1)
                                    dve.wait_ge(s["qk_mm"], b - 1)
                                nc.vector.tensor_tensor(x_lo[q][:, :, :], b7[:, 0:KD * SEQ].rearrange("p (c n) -> p c n", c=KD), x_hi[q][:, :, :],
                                                        ALU.subtract).then_inc(s["x_lo_ready"], 1)
                            b, q, half, on, has = part(i, u + 2)
                            if on:
                                dve.wait_ge(s["rstd_ready"], b + 1)
                                dve.wait_ge(s["mv_ready"], b + 1)
                                if has(-2):
                                    dve.wait_ge(s["xn_turned"], b - 1)
                                nc.vector.tensor_scalar(xn[q][:, :], h[q][:, :], mv[q][:, 0:1], rs[q][:, :],
                                                        ALU.subtract, ALU.mult).then_inc(s["xn_ready"], 1)
                            b, q, half, on, has = part(i, u - 4)
                            if on:
                                dve.wait_ge(s["rstd2_ready"], b + 1)
                                dve.wait_ge(s["mv2_ready"], b + 1)
                                if has(-2):
                                    dve.wait_ge(s["xn2_turned"], b - 1)
                                    dve.wait_ge(xn2_stored[q], 16 * half)
                                nc.vector.tensor_scalar(xn2[q][:, :], h2[q][:, :], mv2[q][:, 0:1], rs2[q][:, :],
                                                        ALU.subtract, ALU.mult).then_inc(s["xn2_ready"], 1)
                            b, q, half, on, has = part(i, u - 3)
                            if on:
                                dve.wait_ge(s["o_turned"], b + 1)
                                o = b4[0:SEQ, :].rearrange("p (n d) -> p n d", d=PAD)
                                if has(-2):
                                    dve.wait_ge(s["h2_ready"], b - 1)
                                nc.vector.reciprocal(denom[q][:, :], o[:, :, HEAD_DIM]).then_inc(s["denom_ready"], 1)
                                dve.wait_ge(s["denom_ready"], b + 1)
                                nc.vector.tensor_tensor(att[q][:, :].rearrange("p (n d) -> p n d", d=HEAD_DIM), o[:, :, 0:HEAD_DIM],
                                                        denom[q][:, :, None].broadcast_to([SEQ, HEADS, HEAD_DIM]), ALU.mult).then_inc(s["att_ready"], 1)
                            b, q, half, on, has = part(i, u)
                            if on:
                                dve.wait_ge(w_loaded[q], 16 * (half + 1))
                                dve.wait_ge(s["w_hi_ready"], b + 1)
                                nc.vector.scalar_tensor_tensor(out=w_lo[:, bass.ds(b * W_CHUNK, W_CHUNK)], in0=w_raw[q][:, :], scalar=scale[:, 1:2],
                                                               in1=w_hi[:, bass.ds(b * W_CHUNK, W_CHUNK)], op0=ALU.mult,
                                                               op1=ALU.subtract).then_inc(s["w_lo_ready"], 1)
                        steps(dve, step)

                    @block.scalar
                    def _(act):
                        def evac(dst, src, signal, **kw):
                            nc.scalar.activation(dst, src, ACT.Copy, **kw).then_inc(signal, 1)

                        def chunks(ap, n):
                            return ap.rearrange("p (c n) -> p c n", c=n)

                        act.wait_ge(s["init"], INIT)

                        def step(i, u):
                            b, q, half, on, has = part(i, u - 1)
                            if on:
                                act.wait_ge(s["k_turned"], b + 1)
                                if has(-2):
                                    act.wait_ge(s["s_mm"], b - 1)
                                evac(k_h[q][:, :, :], chunks(b7[:, 0:CH * SEQ], CH), s["k_h_ready"])
                                if has(-2):
                                    act.wait_ge(s["st_mm"], b - 1)
                                evac(kT[q][:, :, :], chunks(b7[:, 0:CH * SEQ], CH), s["kT_ready"])
                            b, q, half, on, has = part(i, u)
                            if on:
                                act.wait_ge(w_loaded[q], 16 * (half + 1))
                                evac(w_hi[:, bass.ds(b * W_CHUNK, W_CHUNK)], w_raw[q][:, :], s["w_hi_ready"], scale=scale[:, 1:2])
                            b, q, half, on, has = part(i, u + 1)
                            if on:
                                act.wait_ge(s["xn_turned"], b + 1)
                                if has(-6):
                                    act.wait_ge(s["xn2_turned"], b - 5)
                                if has(-2):
                                    act.wait_ge(s["v_mm"], b - 1)
                                    act.wait_ge(s["qk_mm"], b - 1)
                                evac(x_hi[q][:, :, :], chunks(b7[:, 0:KD * SEQ], KD), s["x_hi_ready"])
                            b, q, half, on, has = part(i, u - 5)
                            if on:
                                act.wait_ge(s["xn2_turned"], b + 1)
                                if has(-2):
                                    act.wait_ge(s["logits_mm"], b - 1)
                                evac(xn2T[q][:, :, :], chunks(b7[:, KD * SEQ:2 * KD * SEQ], KD), s["xn2T_ready"])
                            b, q, half, on, has = part(i, u)
                            if on:
                                act.wait_ge(s["v_mm"], b + 1)
                                if has(-5):
                                    act.wait_ge(s["logits_mm"], b - 4)
                                if has(-4):
                                    act.wait_ge(s["o_mm"], b - 3)
                                evac(v[u % 4][:, :, 0:HEAD_DIM], b5[0:SEQ, 0:DIM].rearrange("p (n d) -> p n d", d=HEAD_DIM), s["v_ready"],
                                     scale=unscale[0:SEQ, 0:1])
                            b, q, half, on, has = part(i, u - 5)
                            if on:
                                act.wait_ge(s["logits_mm"], b + 1)
                                evac(logits[:, :, :].rearrange("p b e -> p (b e)")[:, bass.ds(b * EXPERTS, EXPERTS)],
                                     b5[0:SEQ, DIM:DIM + EXPERTS], s["logits_saved"])
                            b, q, half, on, has = part(i, u - 3)
                            if on:
                                act.wait_ge(s["o_mm"], b + 1)
                                if has(-2):
                                    act.wait_ge(s["o_turned"], b - 1)
                                evac(oT[q][:, :, :], chunks(b6[:, 0:CH * SEQ], CH), s["oT_ready"])
                            b, q, half, on, has = part(i, u - 1)
                            if on:
                                act.wait_ge(s["qm_turned"], b + 1)
                                if has(-2):
                                    act.wait_ge(s["st_mm"], b - 1)
                                for g in range(4):
                                    rows = slice(PAD * g, PAD * (g + 1))
                                    evac(qmT[q][rows, :, g, :], chunks(b5[rows, 0:CH * SEQ], CH), s["qmT_ready"])
                            b, q, half, on, has = part(i, u - 2)
                            if on:
                                act.wait_ge(s["st_mm"], b + 1)
                                if has(-2):
                                    act.wait_ge(s["o_mm"], b - 1)
                                nc.scalar.activation(probs[q][:, :, :, :].rearrange("p c g n -> p c (g n)"), quad[0:SEQ, :, 0:4 * SEQ],
                                                     ACT.Exp, scale=HEAD_DIM ** -0.5).then_inc(s["probs_ready"], 1)
                        steps(act, step)

                    @block.tensor
                    def _(pe):
                        def turn(dst, src, n, rows, signal):
                            for c in range(n):
                                last = nc.tensor.transpose(dst[:, c * rows:(c + 1) * rows], src[:, c * P:(c + 1) * P], idt[0:rows, 0:rows])
                            last.then_inc(signal, 1)

                        def project(dst, q, cols):
                            for k in range(KD):
                                for m, (x, w) in enumerate(((x_hi, wqkv_hi), (x_hi, wqkv_lo), (x_lo, wqkv_hi))):
                                    last = nc.tensor.matmul(dst, x[q][:, k, :], w[:, k, cols], start=(k == 0 and m == 0), stop=(k == KD - 1 and m == 2))
                            return last

                        def scores(q, c):
                            return nc.tensor.matmul(quad[0:SEQ, c, 0:4 * SEQ], kT[q][:, c, :],
                                                    qmT[q][:, c, :, :].rearrange("p g n -> p (g n)"), start=True, stop=True)

                        def step(i, u):
                            b, q, half, on, has = part(i, u - 1)
                            if on:
                                pe.wait_ge(s["qk_even"], b + 1)
                                pe.wait_ge(s["qk_odd"], b + 1)
                                if has(-3):
                                    pe.wait_ge(s["oT_ready"], b - 2)
                                flat = qk[q][:, :, :].rearrange("p n d -> p (n d)")
                                turn(b6, flat[:, 0:HEADS * PAD], CH, SEQ, s["q_turned"])
                                if has(1):
                                    pe.wait_ge(s["x_lo_ready"], b + 2)
                                if has(-5):
                                    pe.wait_ge(s["xn2T_ready"], b - 4)
                                turn(b7, flat[:, HEADS * PAD:], CH, SEQ, s["k_turned"])
                            b, q, half, on, has = part(i, u)
                            if on:
                                pe.wait_ge(s["x_hi_ready"], b + 1)
                                pe.wait_ge(s["x_lo_ready"], b + 1)
                                if has(-4):
                                    pe.wait_ge(s["att_ready"], b - 3)
                                project(b4[0:SEQ, :], q, slice(0, 2 * DIM)).then_inc(s["qk_mm"], 1)
                            b, q, half, on, has = part(i, u - 1)
                            if on:
                                pe.wait_ge(s["q_h_ready"], b + 1)
                                pe.wait_ge(s["k_h_ready"], b + 1)
                                if has(-2):
                                    pe.wait_ge(s["probs_ready"], b - 1)
                                for c in range(CH):
                                    for g in range(4):
                                        rows = slice(PAD * g, PAD * g + HEAD_DIM)
                                        last = nc.tensor.matmul(quad[0:SEQ, g, c * SEQ:(c + 1) * SEQ], q_h[q][rows, c, :], k_h[q][rows, c, :],
                                                                start=True, stop=True)
                                last.then_inc(s["s_mm"], 1)
                            b, q, half, on, has = part(i, u + 1)
                            if on:
                                pe.wait_ge(s["xn_ready"], b + 1)
                                if has(-2):
                                    pe.wait_ge(s["kT_ready"], b - 1)
                                turn(b7, xn[q], KD, SEQ, s["xn_turned"])
                            b, q, half, on, has = part(i, u - 5)
                            if on:
                                pe.wait_ge(s["xn2_ready"], b + 1)
                                if has(4):
                                    pe.wait_ge(s["kT_ready"], b + 5)
                                if has(-1):
                                    pe.wait_ge(s["xn2T_ready"], b)
                                turn(b7[:, KD * SEQ:], xn2[q], KD, SEQ, s["xn2_turned"])
                            b, q, half, on, has = part(i, u)
                            if on:
                                if has(-2):
                                    pe.wait_ge(s["qmT_ready"], 4 * (b - 1))
                                project(b5[0:SEQ, 0:DIM], q, slice(2 * DIM, 3 * DIM)).then_inc(s["v_mm"], 1)
                            b, q, half, on, has = part(i, u - 5)
                            if on:
                                pe.wait_ge(s["xn2T_ready"], b + 1)
                                if has(3):
                                    pe.wait_ge(s["qmT_ready"], 4 * (b + 4))
                                if has(-1):
                                    pe.wait_ge(s["logits_saved"], b)
                                for k in range(KD):
                                    last = nc.tensor.matmul(b5[0:SEQ, DIM:DIM + EXPERTS], xn2T[q][:, k, :], router_sb[:, k, :], start=(k == 0), stop=(k == KD - 1))
                                last.then_inc(s["logits_mm"], 1)
                            b, q, half, on, has = part(i, u - 3)
                            if on:
                                pe.wait_ge(s["probs_ready"], b + 1)
                                pe.wait_ge(s["v_ready"], b + 1)
                                if has(2):
                                    pe.wait_ge(s["q_h_ready"], b + 3)
                                for c in range(CH):
                                    for g in range(4):
                                        last = nc.tensor.matmul(b6[PAD * g:PAD * (g + 1), c * SEQ:(c + 1) * SEQ], v[(u - 3) % 4][:, 4 * c + g, :], probs[q][:, c, g, :],
                                                                start=True, stop=True)
                                last.then_inc(s["o_mm"], 1)
                            b, q, half, on, has = part(i, u - 1)
                            if on:
                                pe.wait_ge(s["max_ready"], b + 1)
                                if has(1):
                                    pe.wait_ge(s["v_ready"], b + 2)
                                if has(-4):
                                    pe.wait_ge(s["logits_saved"], b - 3)
                                turn(b5, qk[q][:, :, :].rearrange("p n d -> p (n d)")[:, 0:HEADS * PAD], CH, SEQ, s["qm_turned"])
                            b, q, half, on, has = part(i, u - 2)
                            if on:
                                pe.wait_ge(s["qmT_ready"], 4 * (b + 1))
                                pe.wait_ge(s["kT_ready"], b + 1)
                                if has(1):
                                    pe.wait_ge(s["max_ready"], b + 2)
                                for c in range(CH // 2):
                                    scores(q, c)
                            b, q, half, on, has = part(i, u - 3)
                            if on:
                                pe.wait_ge(s["oT_ready"], b + 1)
                                if has(3):
                                    pe.wait_ge(s["rot_mul"], b + 4)
                                if has(-1):
                                    pe.wait_ge(s["att_ready"], b)
                                for c in range(CH):
                                    last = nc.tensor.transpose(b4[0:SEQ, c * P:(c + 1) * P], oT[q][:, c, :], idt[:, :])
                                last.then_inc(s["o_turned"], 1)
                            b, q, half, on, has = part(i, u - 2)
                            if on:
                                for c in range(CH // 2, CH):
                                    last = scores(q, c)
                                last.then_inc(s["st_mm"], 1)
                        steps(pe, step)

        def routing():
            with ExitStack() as st:
                def tb(name, shape, dt=fp32):
                    return st.enter_context(nc.sbuf_tensor(name, shape, dt))

                BE = [SEQ, BATCH, EXPERTS]
                rev = tb("rev", [P, EXPERTS])
                lanes = tb("lanes", [P, P])
                places = tb("places", [P, TILES_MOE])
                id_part = tb("id_part", [P, BATCH])
                spare_id = tb("spare_id", [P, 1])
                best, second = tb("best", [SEQ, BATCH]), tb("second", [SEQ, BATCH])
                hit, key, rest = tb("hit", BE), tb("key", BE), tb("rest", BE)
                key_max = tb("key_max", [SEQ, BATCH])
                pick = [tb(f"pick{j}", BE) for j in range(2)]
                both, before = tb("both", BE, fp16), tb("before", BE)
                prefix_h, ones_h = tb("prefix_h", [SEQ, SEQ], fp16), tb("ones_h", [SEQ, P], fp16)
                total = tb("total", [P, BATCH, EXPERTS])
                scan = [tb(f"scan{j}", [P, BATCH, EXPERTS]) for j in range(2)]
                count_i, tiles_f = tb("count_i", [P, EXPERTS], i32), tb("tiles_f", [P, EXPERTS])
                tile_end = tb("tile_end", [P, EXPERTS + 1])
                first_slot = tb("first_slot", [P, EXPERTS])
                passed = tb("passed", [P, TILES_MOE, EXPERTS])
                expert_f = tb("expert_f", [P, TILES_MOE])
                slot_f = [tb(f"slot_f{j}", [SEQ, BATCH]) for j in range(2)]
                slot_i = [tb(f"slot_i{j}", [SEQ, BATCH], i32) for j in range(2)]
                tile_i, lane_i = tb("tile_i", [SEQ, BATCH], i32), tb("lane_i", [SEQ, BATCH], i32)
                tile_f = [tb(f"tile_f{j}", [SEQ, BATCH]) for j in range(2)]
                lane_f = [tb(f"lane_f{j}", [SEQ, BATCH]) for j in range(2)]
                gap, gate = tb("gap", [SEQ, BATCH]), [tb(f"gate{j}", [SEQ, BATCH]) for j in range(2)]
                RUN = 24
                RUNS = -(-BATCH // RUN)
                assert RUN * SEQ <= 2 ** 11
                field = tb("field", [SEQ, BATCH], fp16)
                found = tb("found", [P, RUNS, TILES_MOE])
                GROUP, RING = 4, 3
                LANES, TILES = [SEQ, GROUP, P], [SEQ, GROUP, TILES_MOE]
                at_lane = [tb(f"at_lane{j}", LANES, fp16) for j in range(RING)]
                in_tile = [tb(f"in_tile{j}", TILES, fp16) for j in range(RING)]
                at_tile = [tb(f"at_tile{j}", TILES, fp16) for j in range(RING)]
                experts_row = tb("experts_row", [P, EXPERTS])
                weights, first_part = tb("weights", BE), tb("first_part", BE)
                weights_stored = sem("c_weights_stored")
                halves_ready, gates_ready, parts_ready, weights_ready = (
                    sem("c_" + n) for n in ("halves_ready", "gates_ready", "parts_ready", "weights_ready"))
                step_done, counted, consts, exp_in, exp_out, lane_spread, tile_found, tile_spread, placed = (sem("c_" + n) for n in
                    "step_done counted consts exp_in exp_out lane_spread tile_found tile_spread placed".split())

                def groups():
                    for n in range(2 * BATCH // GROUP):
                        yield n, n % 2, slice(n // 2 * GROUP, (n // 2 + 1) * GROUP)

                def spread_over(ap, b, shape):
                    return ap[:, b, None].broadcast_to(shape)

                with nc.Block() as block:
                    @block.gpsimd
                    def _(pool):
                        i_ = dict(allow_small_or_imprecise_dtypes=True)
                        nc.gpsimd.iota(rev[:, :], [[-1, EXPERTS]], base=EXPERTS, channel_multiplier=0, **i_).then_inc(consts, 1)
                        nc.gpsimd.iota(lanes[:, :], [[1, P]], base=0, channel_multiplier=0, **i_).then_inc(consts, 1)
                        nc.gpsimd.iota(places[:, :], [[1, TILES_MOE]], base=0, channel_multiplier=0, **i_).then_inc(consts, 1)
                        for run in range(RUNS):
                            lo, hi = run * RUN, min((run + 1) * RUN, BATCH)
                            nc.gpsimd.iota(id_part[:, lo:hi], [[SEQ, hi - lo]], base=1, channel_multiplier=1, **i_).then_inc(consts, 1)
                        nc.gpsimd.iota(experts_row[:, :], [[1, EXPERTS]], base=0, channel_multiplier=0, **i_).then_inc(consts, 1)
                        nc.gpsimd.iota(spare_id[:, :], [[0, 1]], base=TOKENS + 1, channel_multiplier=1, **i_).then_inc(consts, 1)
                        pool.wait_ge(gates_ready, 1)
                        for j, part_of in enumerate((first_part, weights)):
                            nc.gpsimd.tensor_tensor(part_of[:, :, :], pick[j][:, :, :], gate[j][:, :, None].broadcast_to(BE), ALU.mult).then_inc(parts_ready, 1)
                        pool.wait_ge(parts_ready, 2)
                        nc.gpsimd.tensor_tensor(weights[:, :, :], weights[:, :, :], first_part[:, :, :], ALU.add).then_inc(weights_ready, 1)
                        for n, j, b in groups():
                            if n >= RING:
                                pool.wait_ge(placed, n - RING + 1)
                            pool.wait_ge(tile_found, n + 1)
                            nc.gpsimd.tensor_tensor(at_tile[n % RING][:, :, :], in_tile[n % RING][:, :, :],
                                                    spread_over(field, b, TILES), ALU.mult).then_inc(tile_spread, 1)

                    @block.vector
                    def _(dve):
                        done = [0]

                        def then(ins):
                            done[0] += 1
                            ins.then_inc(step_done, 1)
                            dve.wait_ge(step_done, done[0])

                        def per_token(ap):
                            return ap[:, :, None].broadcast_to(BE)

                        nc.vector.tensor_copy(prefix_h[:, :], prefix_sb[:, :]).then_inc(halves_ready, 1)
                        nc.vector.tensor_copy(ones_h[:, :], ones[0:SEQ, :]).then_inc(halves_ready, 1)
                        dve.wait_ge(consts, 5 + RUNS)
                        revb = rev[0:SEQ, None, :].broadcast_to(BE)
                        for j, (src, top) in enumerate(((logits, best), (rest, second))):
                            then(nc.vector.tensor_reduce(top[:, :], src[:, :, :], AX.X, ALU.max))
                            then(nc.vector.tensor_tensor(hit[:, :, :], src[:, :, :], per_token(top), ALU.is_equal))
                            then(nc.vector.tensor_tensor(key[:, :, :], hit[:, :, :], revb, ALU.mult))
                            then(nc.vector.tensor_reduce(key_max[:, :], key[:, :, :], AX.X, ALU.max))
                            then(nc.vector.tensor_tensor(pick[j][:, :, :], revb, per_token(key_max), ALU.is_equal))
                            if j == 0:
                                then(nc.vector.scalar_tensor_tensor(out=rest[:, :, :], in0=pick[0][:, :, :], scalar=-3.0e38,
                                                                    in1=logits[:, :, :], op0=ALU.mult, op1=ALU.add))
                        nc.vector.tensor_tensor(gap[:, :], second[:, :], best[:, :], ALU.subtract).then_inc(exp_in, 1)
                        then(nc.vector.tensor_tensor(both[:, :, :], pick[0][:, :, :], pick[1][:, :, :], ALU.add))
                        dve.wait_ge(exp_out, 1)
                        then(nc.vector.tensor_scalar(key_max[:, :], gap[:, :], 1.0, None, ALU.add))
                        then(nc.vector.reciprocal(gate[0][:, :], key_max[:, :]))
                        nc.vector.tensor_tensor(gate[1][:, :], gate[0][:, :], gap[:, :], ALU.mult).then_inc(gates_ready, 1)
                        dve.wait_ge(counted, 2)
                        then(nc.vector.tensor_copy(before[:, :, :], b4[0:SEQ, :].rearrange("p (b e) -> p b e", e=EXPERTS)))
                        then(nc.vector.tensor_copy(total[:, :, :], b5[:, :].rearrange("p (b e) -> p b e", e=EXPERTS)))
                        src, k, turn = total, 1, 0
                        while k < BATCH:
                            dst = scan[turn]
                            then(nc.vector.tensor_copy(dst[:, 0:k, :], src[:, 0:k, :]))
                            then(nc.vector.tensor_tensor(dst[:, k:, :], src[:, k:, :], src[:, 0:BATCH - k, :], ALU.add))
                            src, k, turn = dst, 2 * k, 1 - turn
                        running = src
                        then(nc.vector.tensor_scalar(count_i[:, :], running[:, BATCH - 1, :], float(P - 1), None, ALU.add))
                        then(nc.vector.tensor_scalar(count_i[:, :], count_i[:, :], 7, None, ALU.arith_shift_right))
                        then(nc.vector.tensor_copy(tiles_f[:, :], count_i[:, :]))
                        then(nc.vector.memset(tile_end[:, :], 0.0))
                        for e in range(EXPERTS):
                            then(nc.vector.tensor_tensor(tile_end[:, e + 1:e + 2], tile_end[:, e:e + 1], tiles_f[:, e:e + 1], ALU.add))
                        then(nc.vector.tensor_scalar(first_slot[:, :], tile_end[:, 0:EXPERTS], float(P), None, ALU.mult))
                        TE = [P, TILES_MOE, EXPERTS]
                        then(nc.vector.tensor_tensor(passed[:, :, :], places[:, :, None].broadcast_to(TE),
                                                     tile_end[:, None, 1:].broadcast_to(TE), ALU.is_ge))
                        then(nc.vector.tensor_reduce(expert_f[:, :], passed[:, :, :], AX.X, ALU.add))
                        then(nc.vector.tensor_scalar(expert_f[:, :], expert_f[:, :], float(EXPERTS - 1), None, ALU.min))
                        then(nc.vector.tensor_tensor(is_expert[:, :, :], expert_f[:, :, None].broadcast_to(TE),
                                                     experts_row[:, None, :].broadcast_to(TE), ALU.is_equal))
                        then(nc.vector.tensor_scalar(is_expert[:, :, :], is_expert[:, :, :], y_scale[:, :], None, ALU.mult))
                        then(nc.vector.tensor_scalar(expert_of[:, :], expert_f[:, :], float(EXPERTS - 1), None, ALU.min))
                        then(nc.vector.tensor_tensor(before[:, :, :], before[:, :, :], running[0:SEQ, :, :], ALU.add))
                        then(nc.vector.tensor_tensor(before[:, :, :], before[:, :, :], total[0:SEQ, :, :], ALU.subtract))
                        then(nc.vector.tensor_tensor(before[:, :, :], before[:, :, :], first_slot[0:SEQ, None, :].broadcast_to(BE), ALU.add))
                        for j in range(2):
                            then(nc.vector.tensor_tensor(key[:, :, :], before[:, :, :], pick[j][:, :, :], ALU.mult))
                            then(nc.vector.tensor_reduce(slot_f[j][:, :], key[:, :, :], AX.X, ALU.add))
                            then(nc.vector.tensor_copy(slot_i[j][:, :], slot_f[j][:, :]))
                            then(nc.vector.tensor_scalar(tile_i[:, :], slot_i[j][:, :], 7, None, ALU.arith_shift_right))
                            then(nc.vector.tensor_scalar(lane_i[:, :], slot_i[j][:, :], P - 1, None, ALU.bitwise_and))
                            then(nc.vector.tensor_copy(tile_f[j][:, :], tile_i[:, :]))
                            then(nc.vector.tensor_copy(lane_f[j][:, :], lane_i[:, :]))
                        then(nc.vector.tensor_copy(field[:, :], id_part[0:SEQ, :]))
                        for n, j, b in groups():
                            if n >= RING:
                                dve.wait_ge(placed, n - RING + 1)
                            nc.vector.tensor_tensor(in_tile[n % RING][:, :, :], places[0:SEQ, None, :].broadcast_to(TILES),
                                                    spread_over(tile_f[j], b, TILES), ALU.is_equal).then_inc(tile_found, 1)
                            nc.vector.tensor_tensor(at_lane[n % RING][:, :, :], lanes[0:SEQ, None, :].broadcast_to(LANES),
                                                    spread_over(lane_f[j], b, LANES), ALU.is_equal).then_inc(lane_spread, 1)
                        dve.wait_ge(placed, 2 * BATCH // GROUP)
                        then(nc.vector.tensor_copy(found[:, :, :], b6[:, 0:RUNS * TILES_MOE].rearrange("p (r t) -> p r t", r=RUNS)))
                        mark, tok = passed[:, :, 0], expert_f
                        then(nc.vector.tensor_tensor(tok[:, :], found[:, 0, :], found[:, 1, :], ALU.add))
                        for run in range(2, RUNS):
                            then(nc.vector.tensor_tensor(tok[:, :], tok[:, :], found[:, run, :], ALU.add))
                        then(nc.vector.tensor_scalar(mark, tok[:, :], 0.0, spare_id[:, :], ALU.is_equal, ALU.mult))
                        then(nc.vector.tensor_tensor(tok[:, :], tok[:, :], mark, ALU.add))
                        for run in range(1, RUNS):
                            then(nc.vector.tensor_scalar(mark, found[:, run, :], 0.5, float(run * RUN * SEQ), ALU.is_ge, ALU.mult))
                            then(nc.vector.tensor_tensor(tok[:, :], tok[:, :], mark, ALU.add))
                        then(nc.vector.tensor_scalar(token_of[:, :], tok[:, :], -1.0, None, ALU.add))

                    @block.sync
                    def _(sp):
                        sp.wait_ge(weights_ready, 1)
                        sp.dma_start(xn_rows[0:TOKENS, DIM:].rearrange("(b p) e -> p b e", p=SEQ), weights[:, :, :]).then_inc(weights_stored, 16)
                        sp.wait_ge(weights_stored, 16)

                    @block.scalar
                    def _(act):
                        act.wait_ge(exp_in, 1)
                        nc.scalar.activation(gap[:, :], gap[:, :], ACT.Exp).then_inc(exp_out, 1)

                    @block.tensor
                    def _(pe):
                        pe.wait_ge(halves_ready, 2)
                        pe.wait_ge(step_done, 12)
                        flat = both[:, :, :].rearrange("p b e -> p (b e)")
                        nc.tensor.matmul(b4[0:SEQ, :], prefix_h[:, :], flat, start=True, stop=True).then_inc(counted, 1)
                        nc.tensor.matmul(b5[:, :], ones_h[:, :], flat, start=True, stop=True).then_inc(counted, 1)
                        for n, _, b in groups():
                            pe.wait_ge(lane_spread, n + 1)
                            pe.wait_ge(tile_spread, n + 1)
                            run = b.start // RUN
                            for g in range(GROUP):
                                last = nc.tensor.matmul(b6[:, run * TILES_MOE:(run + 1) * TILES_MOE], at_lane[n % RING][:, g, :], at_tile[n % RING][:, g, :],
                                                        start=(b.start == run * RUN and n % 2 == 0 and g == 0),
                                                        stop=((b.stop == BATCH or b.stop % RUN == 0) and n % 2 == 1 and g == GROUP - 1))
                            last.then_inc(placed, 1)

        def experts():
            with ExitStack() as st:
                def tb(name, shape, dt=fp32):
                    return st.enter_context(nc.sbuf_tensor(name, shape, dt))

                def ring(name, shape, dt=fp32):
                    return [tb(f"{name}{i}", shape, dt) for i in range(2)]

                idx, idx_out = ring("idx", [P, 1], i32), ring("idx_out", [P, 1], i32)
                xg = ring("xg", [P, DIM + EXPERTS])
                x_hi, x_lo = ring("x_hi", [P, KD, P], fp16), ring("x_lo", [P, KD, P], fp16)
                silu, hid, y = ring("silu", [P, HIDDEN]), ring("hid", [P, HIDDEN]), ring("y", [P, DIM])
                hid_hi, hid_lo = ring("hid_hi", [P, KH, P], fp16), ring("hid_lo", [P, KH, P], fp16)
                own, weight = tb("own", [P, EXPERTS]), ring("weight", [P, 1])
                names = """idx_ready idx_out_ready x_turned x_hi_ready x_lo_ready gate_mm up_mm silu_ready hid_ready
                    hid_turned hid_hi_ready hid_lo_ready y_mm y_ready own_ready weight_ready""".split()
                s = {n: sem("d_" + n) for n in names}
                gathered = [sem(f"d_gathered{i}") for i in range(2)]
                added = sem("d_added")
                N = TILES_MOE
                UNROLL = 4
                FIRST, LAST = 1, N // UNROLL - 1

                def steps(eng, step, lo, hi, before_run=None):
                    def run(i, first, last):
                        if before_run:
                            before_run(i, first)
                        for u in range(first, last):
                            step(i, u)

                    for t in range(lo, UNROLL * FIRST):
                        run(t // UNROLL, t % UNROLL, t % UNROLL + 1)
                    with eng.Fori(FIRST, LAST) as i:
                        run(i, 0, UNROLL)
                    for t in range(UNROLL * LAST, hi):
                        run(t // UNROLL, t % UNROLL, t % UNROLL + 1)

                def part(i, off):
                    if isinstance(i, int):
                        n = UNROLL * i + off
                        return n, off % 2, 2 * i + off // 2, 0 <= n < N, lambda k: 0 <= n + k < N
                    return UNROLL * i + off, off % 2, 2 * i + off // 2, True, lambda k: True

                with nc.Block() as block:
                    @block.gpsimd
                    def _(pool):
                        def step(i, u):
                            n, q, half, on, has = part(i, u + 2)
                            if on:
                                if has(-2):
                                    pool.wait_ge(gathered[q], 16 * half)
                                    pool.wait_ge(s["x_turned"], n - 1)
                                    pool.wait_ge(s["own_ready"], n - 1)
                                pool.sem_inc(held["pool"], 1)
                                nc.gpsimd.tensor_copy(idx[q][:, :], token_of[:, bass.ds(n, 1)]).then_inc(s["idx_ready"], 1)
                                pool.wait_ge(s["idx_ready"], n + 1)
                                pool.sem_inc(held["pool"], 1)
                                nc.gpsimd.indirect_dma_start(xg[q][:, :], None, xn_rows, bass.IndirectOffsetOnAxis(idx[q][:, :], 0)).then_inc(gathered[q], 16)
                            n, q, half, on, has = part(i, u - 1)
                            if on:
                                if has(-1):
                                    pool.wait_ge(added, 16 * n)
                                pool.sem_inc(held["pool"], 1)
                                nc.gpsimd.tensor_copy(idx_out[q][:, :], token_of[:, bass.ds(n, 1)]).then_inc(s["idx_out_ready"], 1)
                                pool.wait_ge(s["idx_out_ready"], n + 1)
                                pool.wait_ge(s["y_ready"], n + 1)
                                pool.sem_inc(held["pool"], 1)
                                nc.gpsimd.indirect_dma_start(out, bass.IndirectOffsetOnAxis(idx_out[q][:, :], 0), y[q][:, :], None,
                                                             compute_op=ALU.add).then_inc(added, 16)
                        steps(pool, step, -2, N + 1)
                        pool.wait_ge(added, 16 * N)

                    @block.scalar
                    def _(act):
                        def step(i, u):
                            n, q, half, on, has = part(i, u - 1)
                            if on:
                                act.wait_ge(s["hid_turned"], n + 1)
                                if has(-2):
                                    act.wait_ge(s["y_mm"], n - 1)
                                nc.scalar.activation(hid_hi[q][:, :, :].rearrange("p c n -> p (c n)"), b4[:, :], ACT.Copy).then_inc(s["hid_hi_ready"], 1)
                            n, q, half, on, has = part(i, u)
                            if on:
                                act.wait_ge(s["gate_mm"], n + 1)
                                if has(-2):
                                    act.wait_ge(s["hid_ready"], n - 1)
                                nc.scalar.activation(silu[q][:, :], quad[:, 2 * q, :], ACT.Silu, scale=unscale[:, 1:2]).then_inc(s["silu_ready"], 1)
                            n, q, half, on, has = part(i, u + 1)
                            if on:
                                act.wait_ge(s["x_turned"], n + 1)
                                if has(-2):
                                    act.wait_ge(s["up_mm"], n - 1)
                                nc.scalar.activation(x_hi[q][:, :, :].rearrange("p c n -> p (c n)"), b5[:, 0:DIM], ACT.Copy).then_inc(s["x_hi_ready"], 1)
                        steps(act, step, -1, N + 1)

                    @block.vector
                    def _(dve):
                        def step(i, u):
                            n, q, half, on, has = part(i, u - 1)
                            if on:
                                dve.wait_ge(s["hid_hi_ready"], n + 1)
                                if has(-2):
                                    dve.wait_ge(s["y_mm"], n - 1)
                                nc.vector.tensor_tensor(hid_lo[q][:, :, :].rearrange("p c n -> p (c n)"), b4[:, :],
                                                        hid_hi[q][:, :, :].rearrange("p c n -> p (c n)"), ALU.subtract).then_inc(s["hid_lo_ready"], 1)
                            n, q, half, on, has = part(i, u)
                            if on:
                                dve.wait_ge(s["up_mm"], n + 1)
                                dve.wait_ge(s["silu_ready"], n + 1)
                                if has(-2):
                                    dve.wait_ge(s["hid_turned"], n - 1)
                                nc.vector.scalar_tensor_tensor(out=hid[q][:, :], in0=quad[:, 2 * q + 1, :], scalar=up_scale[:, :], in1=silu[q][:, :],
                                                               op0=ALU.mult, op1=ALU.mult).then_inc(s["hid_ready"], 1)
                            n, q, half, on, has = part(i, u + 1)
                            if on:
                                dve.wait_ge(s["x_hi_ready"], n + 1)
                                if has(-2):
                                    dve.wait_ge(s["up_mm"], n - 1)
                                nc.vector.tensor_tensor(x_lo[q][:, :, :].rearrange("p c n -> p (c n)"), b5[:, 0:DIM],
                                                        x_hi[q][:, :, :].rearrange("p c n -> p (c n)"), ALU.subtract).then_inc(s["x_lo_ready"], 1)
                            n, q, half, on, has = part(i, u - 1)
                            if on:
                                dve.wait_ge(s["y_mm"], n + 1)
                                dve.wait_ge(s["weight_ready"], n + 1)
                                if has(-2):
                                    dve.wait_ge(added, 16 * (n - 1))
                                nc.vector.tensor_scalar(y[q][:, :], (b6, b7)[q][:, 0:DIM], weight[q][:, :], None, ALU.mult).then_inc(s["y_ready"], 1)
                            n, q, half, on, has = part(i, u + 1)
                            if on:
                                dve.wait_ge(gathered[q], 16 * (half + 1))
                                if has(-1):
                                    dve.wait_ge(s["weight_ready"], n)
                                nc.vector.tensor_tensor(own[:, :], xg[q][:, DIM:], is_expert[:, :, :].rearrange("p t e -> p (t e)")[:, bass.ds(n * EXPERTS, EXPERTS)],
                                                        ALU.mult).then_inc(s["own_ready"], 1)
                                dve.wait_ge(s["own_ready"], n + 1)
                                if has(-2):
                                    dve.wait_ge(s["y_ready"], n - 1)
                                nc.vector.tensor_reduce(weight[q][:, :], own[:, :], AX.X, ALU.add).then_inc(s["weight_ready"], 1)
                        steps(dve, step, -1, N + 1)

                    @block.tensor
                    def _(pe):
                        def terms(dst, hi, lo, chunks, col, width):
                            for k in range(chunks):
                                for m, (x, w) in enumerate(((hi, w_hi), (hi, w_lo), (lo, w_hi))):
                                    last = nc.tensor.matmul(dst, x[:, k, :], w[:, bass.ds(col + k * (2 * width if width == HIDDEN else width), width)],
                                                            start=(k == 0 and m == 0), stop=(k == chunks - 1 and m == 2))
                            return last

                        expert = {}

                        def load_expert(i, u):
                            n, q, half, on, has = part(i, u)
                            if on:
                                expert[u] = pe.value_load(expert_of[0:1, bass.ds(n, 1)], min_val=0, max_val=EXPERTS - 1)

                        def before_run(i, first):
                            expert.clear()
                            for u in (first - 1, first):
                                load_expert(i, u)

                        def step(i, u):
                            n, q, half, on, has = part(i, u - 1)
                            if on:
                                pe.wait_ge(s["hid_ready"], n + 1)
                                if has(-1):
                                    pe.wait_ge(s["hid_lo_ready"], n)
                                for k in range(KH):
                                    last = nc.tensor.transpose(b4[:, k * P:(k + 1) * P], hid[q][:, k * P:(k + 1) * P], idt[:, :])
                                last.then_inc(s["hid_turned"], 1)
                            n, q, half, on, has = part(i, u)
                            if on:
                                pe.wait_ge(s["x_hi_ready"], n + 1)
                                pe.wait_ge(s["x_lo_ready"], n + 1)
                                if has(-2):
                                    pe.wait_ge(s["hid_ready"], n - 1)
                                terms(quad[:, 2 * q, :], x_hi[q], x_lo[q], KD, expert[u] * W_EXPERT, HIDDEN).then_inc(s["gate_mm"], 1)
                                terms(quad[:, 2 * q + 1, :], x_hi[q], x_lo[q], KD, expert[u] * W_EXPERT + HIDDEN,
                                      HIDDEN).then_inc(s["up_mm"], 1)
                                if not isinstance(i, int) and u + 1 < UNROLL:
                                    load_expert(i, u + 1)
                            n, q, half, on, has = part(i, u + 1)
                            if on:
                                pe.wait_ge(gathered[q], 16 * (half + 1))
                                if has(-1):
                                    pe.wait_ge(s["x_lo_ready"], n)
                                for k in range(KD):
                                    last = nc.tensor.transpose(b5[:, k * P:(k + 1) * P], xg[q][:, k * P:(k + 1) * P], idt[:, :])
                                last.then_inc(s["x_turned"], 1)
                            n, q, half, on, has = part(i, u - 1)
                            if on:
                                pe.wait_ge(s["hid_hi_ready"], n + 1)
                                pe.wait_ge(s["hid_lo_ready"], n + 1)
                                if has(-2):
                                    pe.wait_ge(s["y_ready"], n - 1)
                                terms((b6, b7)[q][:, 0:DIM], hid_hi[q], hid_lo[q], KH, expert[u - 1] * W_EXPERT + KD * 2 * HIDDEN,
                                      DIM).then_inc(s["y_mm"], 1)
                        steps(pe, step, -1, N + 1, before_run)

        zero_tile = sb("zero_tile", [P, DIM + EXPERTS])
        tokenizer()
        attention()
        routing()
        experts()


def kernel(**inputs):
    import concourse.bacc as bacc
    from concourse.bass_utils import run_bass_kernel_spmd

    a = {k: np.asarray(v) for k, v in inputs.items()}
    G, PT = GRID, PATCH
    patches = a["x"].reshape(BATCH, CHANNELS, G, PT, G, PT).transpose(0, 2, 4, 3, 5, 1).reshape(BATCH * PATCHES, PATCH_DIM)
    rows = lambda w: w.reshape(-1, P, w.shape[-1]).transpose(1, 0, 2)
    wqkv = np.concatenate([rows(a[f"L0_attn_w{c}"].T) for c in "qkv"], axis=2)
    freq = 1.0 / 10000.0 ** (np.arange(0, HEAD_DIM, 2, dtype=np.float32) / HEAD_DIM)
    angle = np.outer(np.arange(SEQ, dtype=np.float32), freq.astype(np.float32))
    cos, sin = np.cos(angle), np.sin(angle)
    rope = np.stack([np.tile(np.repeat(cos, 2, axis=1), (1, 2 * HEADS)),
                     np.tile(np.stack([sin, -sin], axis=2).reshape(SEQ, HEAD_DIM), (1, 2 * HEADS))], axis=1).astype(np.float32)
    w13 = a["L0_ffn_moe_w13"].reshape(EXPERTS, KD, P, 2 * HIDDEN).transpose(2, 0, 1, 3).reshape(P, EXPERTS, -1)
    w2 = a["L0_ffn_moe_w2"].reshape(EXPERTS, KH, P, DIM).transpose(2, 0, 1, 3).reshape(P, EXPERTS, -1)
    experts_w = np.concatenate([w13, w2], axis=2).reshape(P, -1)
    arrays = dict(
        patches=patches, txt=a["txt"].reshape(BATCH * TEXT, DIM),
        ln1_g=a["L0_tok_ln1_g"].reshape(KT, P).T, ln1_b=a["L0_tok_ln1_b"].reshape(KT, P).T,
        w_proj=rows(a["L0_tok_W_proj"]), b_proj=a["L0_tok_b_proj"], ln2_g=a["L0_tok_ln2_g"], ln2_b=a["L0_tok_ln2_b"],
        cls_token=a["L0_tok_cls_token"].reshape(1, DIM), pos_emb=a["L0_tok_pos_emb"].reshape(1 + PATCHES, DIM),
        wqkv=wqkv, router=rows(a["L0_ffn_moe_router"]), experts_w=experts_w,
        ident=np.eye(P, dtype=np.float32), rope=rope,
        prefix=np.triu(np.ones((SEQ, SEQ), np.float32), 1),
    )
    nc = bacc.Bacc("TRN2", target_bir_lowering=False, num_devices=1)
    sent, args = {}, {}
    for name, x in arrays.items():
        x = np.ascontiguousarray(x)
        sent[f"in_{name}"] = x
        args[name] = nc.dram_tensor(f"in_{name}", x.shape, mybir.dt.from_np(x.dtype), kind="ExternalInput").ap()
    out = nc.dram_tensor("out", (TOKENS + SPARE, DIM), mybir.dt.float32, kind="ExternalOutput").ap()
    build(nc, out=out, **args)
    got = run_bass_kernel_spmd(nc, [sent], core_ids=[0]).results[0]["out"]
    return got[:TOKENS].reshape(BATCH, SEQ, DIM)
```
